# Optimizing a Trainium2 kernel written in Bass

```python
import numpy as np
import jax
import jax.numpy as jnp

def _softmax(x, axis=-1):
    return jax.nn.softmax(x, axis=axis)

def _gelu(x):
    return jax.nn.gelu(x, approximate=True)

def _silu(x):
    return jax.nn.silu(x)

def _sigmoid(x):
    return jax.nn.sigmoid(x)

def _layernorm(x, axis=-1, eps=1e-05):
    m = jnp.mean(x, axis=axis, keepdims=True)
    v = jnp.var(x, axis=axis, keepdims=True)
    return (x - m) / jnp.sqrt(v + eps)

def _scatter_add(tgt, idx, src, axis=0):
    return tgt.at[idx].add(src)

def _segment_sum(src, seg, n):
    return jax.ops.segment_sum(src, seg, n)
kernel_name = 'mk_hybrid_d1_jaxref_r4_ed8cb4'

def setup_inputs(seed: int=0):
    np.random.seed(seed)
    _w = jnp.asarray

    def _L0_attn_a_setup():
        import jax, jax.numpy as jnp
        import numpy as np
        from jax import lax
        D_MODEL = 256
        EXPAND = 2
        D_INNER = EXPAND * D_MODEL
        HEADDIM = 64
        NHEADS = D_INNER // HEADDIM
        D_STATE = 128
        D_CONV = 4
        NGROUPS = 1
        CONV_DIM = D_INNER + 2 * NGROUPS * D_STATE
        D_IN_PROJ = 2 * D_INNER + 2 * NGROUPS * D_STATE + NHEADS
        BATCH, SEQLEN = (2, 512)
        EPS = 1e-05

        def _causal_depthwise_conv(x, w, b):
            K = w.shape[1]
            xp = jnp.pad(x, ((0, 0), (K - 1, 0), (0, 0)))
            L = x.shape[1]
            out = b[None, None, :]
            for k in range(K):
                out = out + xp[:, k:k + L, :] * w[:, k][None, None, :]
            return out

        def _ssd_scan(dt, A, x, Bm, Cm):
            Bsz = x.shape[0]
            dA = jnp.exp(dt * A[None, None, :])
            dtx = dt[..., None] * x

            def step(h, inp):
                dA_t, dtx_t, B_t, C_t = inp
                h = h * dA_t[:, :, None, None] + dtx_t[..., None] * B_t[:, None, None, :]
                y = jnp.einsum('bhpn,bn->bhp', h, C_t)
                return (h, y)
            h0 = jnp.zeros((Bsz, NHEADS, HEADDIM, D_STATE), x.dtype)
            _, ys = lax.scan(step, h0, (dA.transpose(1, 0, 2), dtx.transpose(1, 0, 2, 3), Bm.transpose(1, 0, 2), Cm.transpose(1, 0, 2)))
            return ys.transpose(1, 0, 2, 3)
        key = jax.random.key(seed)
        ks = jax.random.split(key, 10)
        u = jax.random.normal(ks[0], (BATCH, SEQLEN, D_MODEL), jnp.float32)
        W_in = jax.random.normal(ks[1], (D_IN_PROJ, D_MODEL), jnp.float32) * D_MODEL ** (-0.5)
        conv_w = jax.random.normal(ks[2], (CONV_DIM, D_CONV), jnp.float32) * D_CONV ** (-0.5)
        conv_b = jnp.zeros((CONV_DIM,), jnp.float32)
        dt_bias = jnp.log(jnp.exp(jax.random.uniform(ks[3], (NHEADS,), jnp.float32, minval=0.001, maxval=0.1)) - 1.0)
        A_log = jnp.log(jax.random.uniform(ks[4], (NHEADS,), jnp.float32, minval=1.0, maxval=16.0))
        D = jnp.ones((NHEADS,), jnp.float32)
        norm_w = jnp.ones((D_INNER,), jnp.float32)
        W_out = jax.random.normal(ks[5], (D_MODEL, D_INNER), jnp.float32) * D_INNER ** (-0.5)
        return {'u': u, 'W_in': W_in, 'conv_w': conv_w, 'conv_b': conv_b, 'dt_bias': dt_bias, 'A_log': A_log, 'D': D, 'norm_w': norm_w, 'W_out': W_out}
    _L0_attn_a_in = _L0_attn_a_setup()

    def _L0_attn_b_setup():
        import jax, jax.numpy as jnp
        import numpy as np
        NUM_HEAD = 16
        HEAD_DIM = 64
        RES_DIM = 256
        LN_EPS = 1e-05

        def _layer_norm(x, w, b):
            mu = jnp.mean(x, axis=-1, keepdims=True)
            var = jnp.var(x, axis=-1, keepdims=True)
            return (x - mu) * jax.lax.rsqrt(var + LN_EPS) * w + b
        key = jax.random.key(seed)
        k1, k2, k3 = jax.random.split(key, 3)
        slen, bsz = (512, 4)
        x = jax.random.normal(k1, (slen, bsz, RES_DIM), dtype=jnp.float32)
        w_qkv = jax.random.normal(k2, (NUM_HEAD * 3 * HEAD_DIM, RES_DIM), dtype=jnp.float32) * (1.0 / np.sqrt(RES_DIM))
        w_out = jax.random.normal(k3, (RES_DIM, NUM_HEAD * HEAD_DIM), dtype=jnp.float32) * (1.0 / np.sqrt(NUM_HEAD * HEAD_DIM))
        ln_w = jnp.ones((RES_DIM,), dtype=jnp.float32)
        ln_b = jnp.zeros((RES_DIM,), dtype=jnp.float32)
        return {'x': x, 'w_qkv': w_qkv, 'w_out': w_out, 'ln_w': ln_w, 'ln_b': ln_b}
    _L0_attn_b_in = _L0_attn_b_setup()

    def _L0_ffn_setup():
        import jax, jax.numpy as jnp
        import numpy as np
        D, H, N, K = (256, 512, 8, 2)
        B, S = (4, 512)
        key = jax.random.key(seed)
        ks = jax.random.split(key, 4)
        x = jax.random.normal(ks[0], (B, S, D), dtype=jnp.float32)
        Wr = jax.random.normal(ks[1], (N, D), dtype=jnp.float32) / np.sqrt(D)
        br = jnp.zeros((N,), jnp.float32)
        Wl1 = jax.random.normal(ks[2], (N, D, 2 * H), dtype=jnp.float32) / np.sqrt(D)
        bl1 = jnp.zeros((N, 2 * H), jnp.float32)
        Wl2 = jax.random.normal(ks[3], (N, H, D), dtype=jnp.float32) / np.sqrt(H)
        bl2 = jnp.zeros((N, D), jnp.float32)
        biases_N = jnp.zeros((N,), jnp.float32)
        return {'x': x, 'Wr': Wr, 'br': br, 'Wl1': Wl1, 'bl1': bl1, 'Wl2': Wl2, 'bl2': bl2, 'biases_N': biases_N}
    _L0_ffn_in = _L0_ffn_setup()
    _d = {'L0_attn_a_u': _L0_attn_a_in['u'], 'L0_attn_a_W_in': _L0_attn_a_in['W_in'], 'L0_attn_a_conv_w': _L0_attn_a_in['conv_w'], 'L0_attn_a_conv_b': _L0_attn_a_in['conv_b'], 'L0_attn_a_dt_bias': _L0_attn_a_in['dt_bias'], 'L0_attn_a_A_log': _L0_attn_a_in['A_log'], 'L0_attn_a_D': _L0_attn_a_in['D'], 'L0_attn_a_norm_w': _L0_attn_a_in['norm_w'], 'L0_attn_a_W_out': _L0_attn_a_in['W_out'], 'L0_attn_b_w_qkv': _L0_attn_b_in['w_qkv'], 'L0_attn_b_w_out': _L0_attn_b_in['w_out'], 'L0_attn_b_ln_w': _L0_attn_b_in['ln_w'], 'L0_attn_b_ln_b': _L0_attn_b_in['ln_b'], 'L0_ffn_Wr': _L0_ffn_in['Wr'], 'L0_ffn_br': _L0_ffn_in['br'], 'L0_ffn_Wl1': _L0_ffn_in['Wl1'], 'L0_ffn_bl1': _L0_ffn_in['bl1'], 'L0_ffn_Wl2': _L0_ffn_in['Wl2'], 'L0_ffn_bl2': _L0_ffn_in['bl2'], 'L0_ffn_biases_N': _L0_ffn_in['biases_N']}
    _x0 = _d['L0_attn_a_u']
    _d['L0_attn_a_u'] = jax.random.normal(jax.random.fold_in(jax.random.key(seed), 1), (2, 2048, 256), dtype=_x0.dtype)
    del _x0
    return _d

def reference(L0_attn_a_u, L0_attn_a_W_in, L0_attn_a_conv_w, L0_attn_a_conv_b, L0_attn_a_dt_bias, L0_attn_a_A_log, L0_attn_a_D, L0_attn_a_norm_w, L0_attn_a_W_out, L0_attn_b_w_qkv, L0_attn_b_w_out, L0_attn_b_ln_w, L0_attn_b_ln_b, L0_ffn_Wr, L0_ffn_br, L0_ffn_Wl1, L0_ffn_bl1, L0_ffn_Wl2, L0_ffn_bl2, L0_ffn_biases_N):

    def _L0_attn_a_ref(u, W_in, conv_w, conv_b, dt_bias, A_log, D, norm_w, W_out):
        import jax, jax.numpy as jnp
        import numpy as np
        from jax import lax
        D_MODEL = 256
        EXPAND = 2
        D_INNER = EXPAND * D_MODEL
        HEADDIM = 64
        NHEADS = D_INNER // HEADDIM
        D_STATE = 128
        D_CONV = 4
        NGROUPS = 1
        CONV_DIM = D_INNER + 2 * NGROUPS * D_STATE
        D_IN_PROJ = 2 * D_INNER + 2 * NGROUPS * D_STATE + NHEADS
        BATCH, SEQLEN = (2, 512)
        EPS = 1e-05

        def _causal_depthwise_conv(x, w, b):
            K = w.shape[1]
            xp = jnp.pad(x, ((0, 0), (K - 1, 0), (0, 0)))
            L = x.shape[1]
            out = b[None, None, :]
            for k in range(K):
                out = out + xp[:, k:k + L, :] * w[:, k][None, None, :]
            return out

        def _ssd_scan(dt, A, x, Bm, Cm):
            Bsz = x.shape[0]
            dA = jnp.exp(dt * A[None, None, :])
            dtx = dt[..., None] * x

            def step(h, inp):
                dA_t, dtx_t, B_t, C_t = inp
                h = h * dA_t[:, :, None, None] + dtx_t[..., None] * B_t[:, None, None, :]
                y = jnp.einsum('bhpn,bn->bhp', h, C_t)
                return (h, y)
            h0 = jnp.zeros((Bsz, NHEADS, HEADDIM, D_STATE), x.dtype)
            _, ys = lax.scan(step, h0, (dA.transpose(1, 0, 2), dtx.transpose(1, 0, 2, 3), Bm.transpose(1, 0, 2), Cm.transpose(1, 0, 2)))
            return ys.transpose(1, 0, 2, 3)
        Bsz, L, _ = u.shape
        zxbcdt = jnp.einsum('bld,ed->ble', u, W_in)
        z = zxbcdt[..., :D_INNER]
        xBC = zxbcdt[..., D_INNER:D_INNER + CONV_DIM]
        dt = zxbcdt[..., D_INNER + CONV_DIM:]
        xBC = jax.nn.silu(_causal_depthwise_conv(xBC, conv_w, conv_b))
        x = xBC[..., :D_INNER].reshape(Bsz, L, NHEADS, HEADDIM)
        Bm = xBC[..., D_INNER:D_INNER + D_STATE]
        Cm = xBC[..., D_INNER + D_STATE:]
        dt = jax.nn.softplus(dt + dt_bias[None, None, :])
        A = -jnp.exp(A_log)
        y = _ssd_scan(dt, A, x, Bm, Cm)
        y = y + D[None, None, :, None] * x
        y = y.reshape(Bsz, L, D_INNER)
        y = y * jax.nn.silu(z)
        y = y * lax.rsqrt(jnp.mean(y * y, axis=-1, keepdims=True) + EPS) * norm_w[None, None, :]
        return jnp.einsum('ble,de->bld', y, W_out)

    def _L0_attn_b_ref(x, w_qkv, w_out, ln_w, ln_b):
        import jax, jax.numpy as jnp
        import numpy as np
        NUM_HEAD = 16
        HEAD_DIM = 64
        RES_DIM = 256
        LN_EPS = 1e-05

        def _layer_norm(x, w, b):
            mu = jnp.mean(x, axis=-1, keepdims=True)
            var = jnp.var(x, axis=-1, keepdims=True)
            return (x - mu) * jax.lax.rsqrt(var + LN_EPS) * w + b
        slen, bsz, _ = x.shape
        scale = 1.0 / np.sqrt(RES_DIM).astype(np.float32)
        x_in = _layer_norm(x, ln_w, ln_b)
        qkv = x_in @ w_qkv.T
        qkv = qkv.reshape(slen, bsz, NUM_HEAD, 3 * HEAD_DIM)
        q, k, v = jnp.split(qkv, 3, axis=-1)
        scores = jnp.einsum('ibnd,jbnd->ijbn', q, k) * scale
        attn = jax.nn.softmax(scores, axis=1)
        attn_out = jnp.einsum('ijbn,jbnd->ibnd', attn, v)
        attn_out = attn_out.reshape(slen, bsz, NUM_HEAD * HEAD_DIM)
        attn_out = attn_out @ w_out.T
        return x + attn_out

    def _L0_ffn_ref(x, Wr, br, Wl1, bl1, Wl2, bl2, biases_N):
        import jax, jax.numpy as jnp
        import numpy as np
        D, H, N, K = (256, 512, 8, 2)
        B, S = (4, 512)
        Bb, Ss, Dd = x.shape
        scores_BSN = jnp.einsum('bsd,nd->bsn', x, Wr) + br
        w_BSN = jax.nn.softmax(scores_BSN, axis=-1)
        _, idx_BSK = jax.lax.top_k(scores_BSN + biases_N[None, None, :], K)
        val_BSK = jnp.take_along_axis(w_BSN, idx_BSK, axis=-1)
        val_BSK = val_BSK / jnp.sum(val_BSK, axis=-1, keepdims=True)
        M = Bb * Ss
        x_MD = x.reshape(M, Dd)
        idx_MK = idx_BSK.reshape(M, K)
        val_MK = val_BSK.reshape(M, K)
        h_NM2H = jnp.einsum('md,ndh->nmh', x_MD, Wl1) + bl1[:, None, :]
        a_NMH, b_NMH = (h_NM2H[..., :H], h_NM2H[..., H:])
        y_NMD = jnp.einsum('nmh,nhd->nmd', jax.nn.silu(a_NMH) * b_NMH, Wl2) + bl2[:, None, :]
        ew_MN = jnp.zeros((M, N), x.dtype)
        ew_MN = ew_MN.at[jnp.arange(M)[:, None], idx_MK].set(val_MK)
        y_MD = jnp.einsum('mn,nmd->md', ew_MN, y_NMD)
        return y_MD.reshape(Bb, Ss, Dd)
    x = L0_attn_a_u
    x = x + _L0_attn_a_ref(_layernorm(x, axis=-1), L0_attn_a_W_in, L0_attn_a_conv_w, L0_attn_a_conv_b, L0_attn_a_dt_bias, L0_attn_a_A_log, L0_attn_a_D, L0_attn_a_norm_w, L0_attn_a_W_out)
    x = x + _L0_ffn_ref(_layernorm(x, axis=-1), L0_ffn_Wr, L0_ffn_br, L0_ffn_Wl1, L0_ffn_bl1, L0_ffn_Wl2, L0_ffn_bl2, L0_ffn_biases_N)
    x = x + _L0_attn_b_ref(_layernorm(x, axis=-1), L0_attn_b_w_qkv, L0_attn_b_w_out, L0_attn_b_ln_w, L0_attn_b_ln_b)
    x = x + _L0_ffn_ref(_layernorm(x, axis=-1), L0_ffn_Wr, L0_ffn_br, L0_ffn_Wl1, L0_ffn_bl1, L0_ffn_Wl2, L0_ffn_bl2, L0_ffn_biases_N)
    return x

_drawn_inputs = setup_inputs


def setup_inputs(seed=0):
    import zlib

    import numpy as np

    out = dict(_drawn_inputs(seed))
    spreads = {'L0_attn_a_conv_b': (0.0, 0.1),
     'L0_attn_a_D': (1.0, 0.2),
     'L0_attn_a_norm_w': (1.0, 0.2),
     'L0_attn_b_ln_w': (1.0, 0.2),
     'L0_attn_b_ln_b': (0.0, 0.1),
     'L0_ffn_br': (0.0, 0.1),
     'L0_ffn_bl1': (0.0, 0.1),
     'L0_ffn_bl2': (0.0, 0.1),
     'L0_ffn_biases_N': (0.0, 0.1)}
    factors = {}
    for name, (base, spread) in spreads.items():
        noise = np.random.default_rng([zlib.crc32(name.encode()), seed]).standard_normal(out[name].shape)
        drawn = base * np.exp(spread * noise) if base else spread * noise
        out[name] = jnp.asarray(drawn.astype(out[name].dtype))
    for name, factor in factors.items():
        out[name] = (out[name] * factor).astype(out[name].dtype)
    return out
```

```python
import concourse.bass as bass
from concourse import mybir
from contextlib import ExitStack

B, L, D = 2, 2048, 256
P = 128
NC = L // P
NQ = B * NC
KD = D // P
H, HD = 8, 64
DI = H * HD
NS = 128
CONV = DI + 2 * NS
MC = CONV // P
TAPS = 4
E, HF = 8, 512
TOPK = 2
KF = HF // P
SLOTS_T = B * L * TOPK // P + E - 1
ST = SLOTS_T + 1
AH, AD = 16, 64
AI = AH * AD
KA = AI // P
EPS = 1e-5
NTOK = B * L
BIG = 3.0e38
MASKED = -1.0e30

C_ID, C_UP, C_ONE, C_US, C_IOTA, C_MASK = 0, 128, 256, 384, 512, 640
C_IT = 768
C_TOK = C_IT + ST
C_K128 = C_TOK + NQ
C_REV = C_K128 + NQ
C_PAD = C_REV + E
C_N = C_PAD + 1


def hybrid_block(nc: bass.Bass, u, w_in, conv_w, conv_b, dt_bias, a_log, d_skip, norm_w, w_mix_out,
                 w_qkv, w_att_out, ln_w, ln_b, w_route, b_route, w1, b1, w2, b2, bias_n, consts, out):
    f32, bf16, i32 = mybir.dt.float32, mybir.dt.bfloat16, mybir.dt.int32
    ALU = mybir.AluOpType
    ACT = mybir.ActivationFunctionType
    AX = mybir.AxisListType
    ds = bass.ds

    ctx = ExitStack()
    with ctx:
        def sb(name, cols, dt=f32):
            return ctx.enter_context(nc.sbuf_tensor(name, [P, cols], dt))

        def sem(name):
            return ctx.enter_context(nc.semaphore(name))

        X = sb("X", NQ * D)
        KEEP = sb("KEEP", NQ * D)
        W1 = sb("W1", E * KD * 2 * HF)
        W1v = W1[:, :].rearrange("p (e k n) -> p e k n", e=E, k=KD)
        CST = sb("CST", C_N)
        WR = sb("WR", KD * E)
        STATS = sb("STATS", NQ * 6)
        MEAN, RSTD, VARE, RST2 = (sb(n, NQ) for n in ("MEAN", "RSTD", "VARE", "RST2"))
        TMP = [sb(f"TMP{i}", NQ) for i in range(3)]
        ROUTE_B = sb("ROUTE_B", 2 * E)
        GATE = sb("GATE", ST)
        IDX = sb("IDX", ST, i32)
        EXPERT = sb("EXPERT", ST, i32)
        IDC = sb("IDC", 4, i32)
        PHASE = sb("PHASE", 18848)

        Xv = X[:, :].rearrange("p (q d) -> p q d", d=D)
        KEEPv = KEEP[:, :].rearrange("p (q d) -> p q d", d=D)
        STv = STATS[:, :].rearrange("p (q s) -> p q s", s=6)
        ident = CST[:, C_ID:C_ID + P]

        def carve(base):
            at = [0]

            def take(cols):
                at[0] += cols
                assert at[0] <= base.shape[1], at[0]
                return base[:, at[0] - cols:at[0]]
            return take

        BK = [ctx.enter_context(nc.psum_tensor(f"BK{i}", [P, 512], f32)) for i in range(8)]

        def spread(ap, n):
            return ap.unsqueeze(2).broadcast_to([ap.shape[0], ap.shape[1], n])

        def repeat(ap, n):
            return ap.unsqueeze(1).broadcast_to([ap.shape[0], n, ap.shape[1]])

        def need(eng, s, value):
            if not isinstance(value, int) or value > 0:
                eng.wait_ge(s, value)

        class Steps:

            def __init__(self, eng, s):
                self.eng, self.s, self.n = eng, s, 0

            def __call__(self, instruction):
                instruction.then_inc(self.s, 1)
                self.n += 1
                return self.n

            def after(self, n=None):
                self.eng.wait_ge(self.s, self.n if n is None else n)

            def clear(self):
                if self.n:
                    self.after()
                    self.eng.sem_clear(self.s)
                    self.n = 0

        bar = sem("phase_done")
        bars = {}

        def barrier(eng, gp=False):
            n = bars[id(eng)] = bars.get(id(eng), 0) + 1
            eng.drain().then_inc(bar, 1)
            eng.wait_ge(bar, 5 * n)

        dve_step, act_step, pool_step, pe_step = sem("dve_step"), sem("act_step"), sem("pool_step"), sem("pe_step")
        loaded_x, loaded_small, loaded_w1, loaded_w2 = sem("loaded_x"), sem("loaded_small"), sem("loaded_w1"), sem("loaded_w2")
        stored_x, zeroed = sem("stored_x"), sem("zeroed")

        xn_dram = nc.dram_tensor("xn_dram", [NTOK + P, D], f32, kind="Internal").ap()
        acc_dram = nc.dram_tensor("acc_dram", [NTOK + P, D], f32, kind="Internal").ap()

        take = carve(PHASE)
        WIN = take(KD * 1288).rearrange("p (k n) -> p k n", k=KD)
        WOUT = take(4 * D).rearrange("p (k n) -> p k n", k=4)
        CW = take(MC * TAPS).rearrange("p (m s) -> p m s", m=MC)
        CB = take(MC)
        DTB, ALG, DSK = take(H), take(H), take(H)
        NW = take(4)
        PA, PNC, PEC, PDT, PWD, PET = (take(NQ * H) for _ in range(6))
        XB = take(MC * 2 * 131).rearrange("p (m b t) -> p m b t", m=MC, b=2)
        ACC = take(MC * 2 * P).rearrange("p (m b t) -> p m b t", m=MC, b=2)
        XC = take(MC * 2 * P).rearrange("p (m b t) -> p m b t", m=MC, b=2)
        XTS = take(2 * D).rearrange("p (k b t) -> p k b t", k=KD, b=2)
        XS, XDT, XDEC, DX, ZS, SST = (take(2 * DI).rearrange("p (b n) -> p b n", b=2) for _ in range(6))
        BT = take(2 * NS).rearrange("p (b n) -> p b n", b=2)
        LM = take(H * P).rearrange("p (h i) -> p h i", h=H)
        Y = take(DI).unsqueeze(1)
        YT = take(4 * P).rearrange("p (k t) -> p k t", k=4)
        SS = take(NQ)
        ANOW = take(2 * H).rearrange("p (b h) -> p b h", b=2)
        MB = CST[:, C_MASK:C_MASK + P].bitcast(bf16)
        identb, maskb = MB[:, 0:P], MB[:, P:2 * P]
        SP_ = [ACC.rearrange("p m b t -> p (m b t)")[:, i * 256:(i + 1) * 256] for i in range(6)]
        XNB0 = XS
        XT0 = XDT.rearrange("p b (k t) -> p b k t", t=P)[:, :, 0:KD, :]

        take = carve(PHASE)
        W2 = take(E * KF * D).rearrange("p (e k n) -> p e k n", e=E, k=KF)
        B1 = take(E * 2 * HF).rearrange("p (e n) -> p e n", e=E)
        B2 = take(E * D).rearrange("p (e n) -> p e n", e=E)
        ftake = carve(KEEP)
        XG, YO = (ftake(2 * D).rearrange("p (b n) -> p b n", b=2) for _ in range(2))
        XTF = ftake(2 * D).rearrange("p (b k t) -> p b k t", b=2, k=KD)
        HA, HB, HT = (ftake(2 * HF).rearrange("p (b n) -> p b n", b=2) for _ in range(3))
        HTv = HT.rearrange("p b (k t) -> p b k t", t=P)

        def rstd_steps(dve, st, act_sq, act_done, n_call, mean, rstd, vare, extra=None):
            me, m2e, mo, m2o = STv[:, :, 1], STv[:, :, 2], STv[:, :, 4], STv[:, :, 5]
            t0, t1, t2 = (t[:, :] for t in TMP)
            a = st(dve.tensor_tensor(t0, me, mo, ALU.add))
            b = st(dve.tensor_tensor(t1, me, mo, ALU.subtract))
            c = st(dve.tensor_tensor(t2, m2e, m2o, ALU.add))
            st.after(a)
            st(dve.tensor_scalar(mean[:, :], t0, 0.5, None, ALU.mult))
            st.after()
            d = st(dve.tensor_tensor(t0, t1, t1, ALU.mult))
            st(dve.tensor_scalar(t2, t2, 1.0 / D, EPS, ALU.mult, ALU.add))
            st.after()
            st(dve.scalar_tensor_tensor(vare[:, :], t0, 0.25, t2, ALU.mult, ALU.add))
            st.after()
            root(dve, st, act_sq, act_done, n_call, vare[:, :], rstd[:, :])

        def root(dve, st, ready, done, n, v, r):
            dve.tensor_copy(TMP[0][:, :], v).then_inc(ready, 1)
            dve.wait_ge(done, n)
            st(dve.reciprocal(r, TMP[1][:, :]))
            st.after()
            st(dve.tensor_tensor(TMP[2][:, :], r, r, ALU.mult))
            st.after()
            st(dve.tensor_tensor(TMP[2][:, :], TMP[2][:, :], v, ALU.mult))
            st.after()
            st(dve.tensor_scalar(TMP[2][:, :], TMP[2][:, :], -0.5, 1.5, ALU.mult, ALU.add))
            st.after()
            st(dve.tensor_tensor(r, r, TMP[2][:, :], ALU.mult))
            st.after()

        root_ready, root_done = sem("root_ready"), sem("root_done")

        def act_root(act, n):
            act.wait_ge(root_ready, n)
            act.activation(TMP[1][:, :], TMP[0][:, :], ACT.Sqrt).then_inc(root_done, 1)

        class Norm:

            def __init__(self, tag, xnb, xt, w8, mean, rstd, keep, store):
                self.xn, self.tr, self.xt, self.pj, self.kept = (
                    sem(f"{n}_{tag}") for n in ("normed", "transposed", "xt_ready", "projected", "kept"))
                self.st = [sem(f"normed_stored{b}_{tag}") for b in range(2)]
                self.xnb, self.xT, self.w8, self.mean, self.rstd = xnb, xt, w8, mean, rstd
                self.keep, self.store = keep, store

        def norm_dve(dve, N):
            def body(c):
                for b in range(2):
                    q = 2 * c + b
                    need(dve, N.tr, q - 1)
                    if N.store:
                        need(dve, N.st[b], 16 * c)
                    dve.tensor_scalar(N.xnb[:, b, 0:D], Xv[:, ds(q, 1), :], N.mean[:, ds(q, 1)],
                                      N.rstd[:, ds(q, 1)], ALU.subtract, ALU.mult).then_inc(N.xn, 1)
            body(0)
            with dve.Fori(1, NC) as c:
                body(c)

        def norm_act(act, N):
            def body(c):
                for b in range(2):
                    q = 2 * c + b
                    need(act, N.pj, q - 1)
                    if N.keep:
                        need(act, N.kept, q - 1)
                    act.wait_ge(N.tr, q + 1)
                    act.activation(N.xT[:, b], BK[b][:, 0:D], ACT.Copy).then_inc(N.xt, 1)
            body(0)
            with act.Fori(1, NC) as c:
                body(c)

        def norm_pe(pe, N, dest):
            def transpose(c, b):
                q = 2 * c + b
                need(pe, N.xt, q - 1)
                pe.wait_ge(N.xn, q + 1)
                for k in range(KD):
                    t = pe.transpose(BK[b][:, k * P:(k + 1) * P], N.xnb[:, b, k * P:(k + 1) * P], ident)
                t.then_inc(N.tr, 1)

            def project(c, b):
                q = 2 * c + b
                pe.wait_ge(N.xt, q + 1)
                for k in range(KD):
                    m = pe.matmul(dest[:, ds(q * 8, 8)], N.xT[:, b, k, :], N.w8[:, k, :],
                                  start=k == 0, stop=k == KD - 1)
                m.then_inc(N.pj, 1)
            transpose(0, 0)
            transpose(0, 1)
            project(0, 0)
            with pe.Fori(1, NC) as c:
                transpose(c, 0)
                project(c - 1, 1)
                transpose(c, 1)
                project(c, 0)
            project(NC - 1, 1)

        def norm_sp(sp, N):
            def body(c):
                for b in range(2):
                    sp.wait_ge(N.xn, 2 * c + b + 1)
                    sp.dma_start(xn_dram[ds(c * P + b * L, P), :], N.xnb[:, b, 0:D]).then_inc(N.st[b], 16)
            body(0)
            with sp.Fori(1, NC) as c:
                body(c)
            for b in range(2):
                sp.wait_ge(N.st[b], 16 * NC)

        wdt = WIN[:, :, DI + CONV:DI + CONV + H]
        norm_a = Norm("a", XNB0, XT0, wdt, MEAN, RSTD, True, False)
        wr8 = WR[:, :].rearrange("p (k n) -> p k n", k=KD)

        M = {n: sem("mix_" + n) for n in (
            "act_in", "act_out", "cum", "consts", "a_now", "xts", "xbc", "taken", "tapped", "xc", "z", "zs",
            "rg", "bc", "decay", "masked", "y2st", "y1", "y", "state", "scaled", "ytr", "yt", "po", "po_out",
            "xtr", "xs", "xdt", "xdec", "square")}
        R = [{n: sem(f"{n}_{f}") for n in (
            "exp_in", "exp_out", "masks", "counts", "routed", "onehot", "listed", "lists", "idx",
            "gath0", "gath1", "tr", "xt", "up0", "up1", "ha", "silu", "hb", "gated", "htr", "ht", "y", "yo",
            "scat0", "scat1", "e_ready")} for f in range(2)]

        def router_scratch(base):
            t = carve(base)
            r = {}
            for n in ("SC", "W", "SBI", "EQ", "OH1", "OH2", "M12", "INC", "RK"):
                r[n] = t(NQ * E)
            for n in ("MX", "Z", "R1", "R2", "V1", "V2", "P1", "P2", "G1", "G2", "T1", "T2", "TI"):
                r[n] = t(NQ)
            r["CNT"], r["END"] = t(E), t(E)
            r["CMP"] = t(E * NQ)
            r["EF"] = t(ST)
            r["OHR"] = t(2 * P).rearrange("p (b n) -> p b n", b=2)
            r["RHS"] = t(2 * 2 * ST).rearrange("p (b j n) -> p b j n", b=2, j=2)
            r["ZERO"] = t(2 * ST)
            r["XNB"] = t(2 * D).rearrange("p (b n) -> p b n", b=2)
            r["XT"] = t(2 * D).rearrange("p (b k t) -> p b k t", b=2, k=KD)
            return r
        G = router_scratch(KEEP)
        norm_f = [Norm(f"f{f}", G["XNB"], G["XT"], wr8, MEAN, RSTD, False, True) for f in range(2)]

        def route_dve(dve, st, f):
            g, r = G, R[f]
            v3 = lambda ap: ap.rearrange("p (q e) -> p q e", e=E)
            sc, w, sbi, eq = g["SC"], g["W"], g["SBI"], g["EQ"]
            rev = repeat(CST[:, C_REV:C_REV + E], NQ)
            st(dve.tensor_tensor(v3(sc), v3(BK[2][:, 0:NQ * E]), repeat(ROUTE_B[:, 0:E], NQ), ALU.add))
            st.after()
            st(dve.tensor_reduce(g["MX"], v3(sc), AX.X, ALU.max))
            st(dve.tensor_tensor(v3(sbi), v3(sc), repeat(ROUTE_B[:, E:2 * E], NQ), ALU.add))
            st.after()
            dve.tensor_tensor(v3(w), v3(sc), spread(g["MX"], E), ALU.subtract).then_inc(r["exp_in"], 1)
            for k in range(TOPK):
                oh, rk = g[f"OH{k + 1}"], g[f"R{k + 1}"]
                st(dve.tensor_reduce(g["T1"], v3(sbi), AX.X, ALU.max))
                st.after()
                st(dve.tensor_tensor(v3(eq), v3(sbi), spread(g["T1"], E), ALU.is_equal))
                st.after()
                st(dve.tensor_tensor(v3(eq), v3(eq), rev, ALU.mult))
                st.after()
                st(dve.tensor_reduce(rk, v3(eq), AX.X, ALU.max))
                st.after()
                st(dve.tensor_tensor(v3(oh), spread(rk, E), rev, ALU.is_equal))
                st.after()
                if k == 0:
                    st(dve.scalar_tensor_tensor(sbi, oh, -BIG, sbi, ALU.mult, ALU.add))
                    st.after()
            dve.tensor_tensor(g["M12"], g["OH1"], g["OH2"], ALU.add).then_inc(r["masks"], 1)
            dve.wait_ge(r["exp_out"], 1)
            st(dve.tensor_reduce(g["Z"], v3(w), AX.X, ALU.add))
            st.after()
            st(dve.reciprocal(g["Z"], g["Z"]))
            st.after()
            st(dve.tensor_tensor(v3(w), v3(w), spread(g["Z"], E), ALU.mult))
            st.after()
            for k in range(TOPK):
                st(dve.tensor_tensor(eq, w, g[f"OH{k + 1}"], ALU.mult))
                st.after()
                st(dve.tensor_reduce(g[f"V{k + 1}"], v3(eq), AX.X, ALU.add))
                st.after()
            st(dve.tensor_tensor(g["T1"], g["V1"], g["V2"], ALU.add))
            st.after()
            st(dve.reciprocal(g["T1"], g["T1"]))
            st.after()
            for k in range(TOPK):
                st(dve.tensor_tensor(g[f"G{k + 1}"], g[f"V{k + 1}"], g["T1"], ALU.mult))
            dve.wait_ge(r["counts"], 1)
            tot = BK[3][:, 256:512]
            st(dve.tensor_copy(g["RK"], tot))
            st(dve.memset(eq, 1.0))
            st.after()
            for e in range(E):
                st(dve.tensor_tensor_scan(v3(g["INC"])[:, :, e], v3(eq)[:, :, e], v3(g["RK"])[:, :, e],
                                          0.0, ALU.mult, ALU.add))
            st.after()
            last = v3(g["INC"])[:, NQ - 1, :]
            cmp3 = g["CMP"].rearrange("p (e k) -> p e k", e=E)
            st(dve.tensor_tensor(cmp3, spread(last, NQ), repeat(CST[:, C_K128:C_K128 + NQ], E), ALU.is_gt))
            st.after()
            st(dve.tensor_reduce(g["CNT"], cmp3, AX.X, ALU.add))
            st.after()
            st(dve.tensor_tensor_scan(g["END"], eq[:, 0:E], g["CNT"], 0.0, ALU.mult, ALU.add))
            st.after()
            st(dve.tensor_tensor(g["CNT"], g["END"], g["CNT"], ALU.subtract))
            st.after()
            st(dve.tensor_scalar(g["CNT"], g["CNT"], float(P), None, ALU.mult))
            st(dve.tensor_tensor(g["INC"], g["INC"], g["RK"], ALU.subtract))
            st.after()
            st(dve.tensor_tensor(g["INC"], g["INC"], BK[3][:, 0:256], ALU.add))
            st.after()
            st(dve.tensor_tensor(v3(g["INC"]), v3(g["INC"]), repeat(g["CNT"], NQ), ALU.add))
            st.after()
            ti = g["TI"].bitcast(i32)
            for k in range(TOPK):
                p, row = g[f"P{k + 1}"], g[f"R{k + 1}"]
                st(dve.tensor_tensor(eq, g["INC"], g[f"OH{k + 1}"], ALU.mult))
                st.after()
                st(dve.tensor_reduce(g["T1"], v3(eq), AX.X, ALU.add))
                st.after()
                st(dve.tensor_copy(ti, g["T1"]))
                st.after()
                st(dve.tensor_single_scalar(ti, ti, 7, ALU.arith_shift_right))
                st.after()
                st(dve.tensor_copy(p, ti))
                st.after()
                st(dve.scalar_tensor_tensor(row, p, -float(P), g["T1"], ALU.mult, ALU.add))
                st.after()
                st(dve.tensor_tensor(g[f"V{k + 1}"], CST[:, C_TOK:C_TOK + NQ], row, ALU.subtract))
                st.after()
            st(dve.memset(g["EF"], 0.0))
            st(dve.memset(g["ZERO"], 0.0))
            st.after()
            for e in range(E - 1):
                st(dve.scalar_tensor_tensor(g["EF"], CST[:, C_IT:C_IT + ST], g["END"][:, e:e + 1], g["EF"],
                                            ALU.is_ge, ALU.add))
                st.after()
            dve.tensor_copy(EXPERT[:, :], g["EF"]).then_inc(r["e_ready"], 1)
            st.clear()

            def onehots(q):
                for k in range(TOPK):
                    need(dve, r["listed"], 2 * q + k - 1)
                    st(dve.tensor_scalar(g["OHR"][:, k], CST[:, C_IOTA:C_IOTA + P],
                                         g[f"R{k + 1}"][:, ds(q, 1)], None, ALU.is_equal))
                    st(dve.tensor_scalar(g["RHS"][:, k, 0], CST[:, C_IT:C_IT + ST],
                                         g[f"P{k + 1}"][:, ds(q, 1)], g[f"V{k + 1}"][:, ds(q, 1)],
                                         ALU.is_equal, ALU.mult))
                    st.after()
                    dve.tensor_scalar(g["RHS"][:, k, 1], CST[:, C_IT:C_IT + ST],
                                      g[f"P{k + 1}"][:, ds(q, 1)], g[f"G{k + 1}"][:, ds(q, 1)],
                                      ALU.is_equal, ALU.mult).then_inc(r["onehot"], 1)
                st.clear()
            onehots(0)
            with dve.Fori(1, NQ) as q:
                onehots(q)
            dve.wait_ge(r["lists"], 1)
            st(dve.tensor_scalar(g["EF"], BK[4][:, 0:ST], CST[:, C_PAD:C_PAD + 1], None, ALU.add))
            st(dve.tensor_copy(GATE[:, :], BK[4][:, ST:2 * ST]))
            st.after()
            dve.tensor_copy(IDX[:, :], g["EF"]).then_inc(r["idx"], 1)
            st.clear()

        def route_act(act, f):
            act.wait_ge(R[f]["exp_in"], 1)
            act.activation(G["W"], G["W"], ACT.Exp).then_inc(R[f]["exp_out"], 1)

        def route_pe(pe, f):
            r, g = R[f], G
            pe.wait_ge(r["masks"], 1)
            pe.matmul(BK[3][:, 0:256], CST[:, C_US:C_US + P], g["M12"], start=True, stop=True)
            pe.matmul(BK[3][:, 256:512], CST[:, C_ONE:C_ONE + P], g["M12"], start=True, stop=True
                      ).then_inc(r["counts"], 1)
            pe.wait_ge(r["e_ready"], 1)
            pe.matmul(BK[4][:, 0:2 * ST], ident, g["ZERO"], start=True, stop=False)

            def add(q):
                for k in range(TOPK):
                    pe.wait_ge(r["onehot"], 2 * q + k + 1)
                    pe.matmul(BK[4][:, 0:2 * ST], g["OHR"][:, k], g["RHS"][:, k].rearrange("p j n -> p (j n)"),
                              start=False, stop=False).then_inc(r["listed"], 1)
            with pe.Fori(0, NQ) as q:
                add(q)
            pe.matmul(BK[4][:, 0:2 * ST], ident, g["ZERO"], start=False, stop=True).then_inc(r["lists"], 1)

        def experts(eng_name, eng, st, f, acc):
            r = R[f]
            gath, scat = (r["gath0"], r["gath1"]), (r["scat0"], r["scat1"])

            if eng_name in ("pe", "dve"):
                coming = eng.alloc_register(f"{eng_name}_coming_{f}")
                under_way = [eng.alloc_register(f"{eng_name}_expert{p}_{f}") for p in range(2)]

            def fetch_expert(t):
                eng.load(coming, EXPERT[0:1, ds(t, 1)])

            def take_expert(p):
                eng.reg_mov(under_way[p], coming)

            def expert(p):
                return eng.snap(under_way[p], min_val=0, max_val=E - 1)

            def gather(t, p):
                need(eng, r["tr"], t - 1)
                eng.wait_ge(r["idx"], 1)
                st(eng.tensor_copy(IDC[:, p:p + 1], IDX[:, ds(t, 1)]))
                st.after()
                eng.indirect_dma_start(out=XG[:, p, :], out_offset=None, in_=xn_dram,
                                       in_offset=bass.IndirectOffsetOnAxis(ap=IDC[:, p:p + 1], axis=0)
                                       ).then_inc(gath[p], 16)

            def scatter(t, h, p):
                eng.wait_ge(r["yo"], t + 1)
                if not (isinstance(t, int) and t == 0):
                    eng.wait_ge(scat[1 - p], 16 * (h + p))
                st(eng.tensor_copy(IDC[:, 2 + p:3 + p], IDX[:, ds(t, 1)]))
                st.after()
                eng.indirect_dma_start(out=acc, out_offset=bass.IndirectOffsetOnAxis(ap=IDC[:, 2 + p:3 + p], axis=0),
                                       in_=YO[:, p, :], in_offset=None, compute_op=ALU.add
                                       ).then_inc(scat[p], 16)

            def pe_transpose(t, h, p):
                need(eng, r["xt"], t)
                eng.wait_ge(gath[p], 16 * (h + 1))
                for k in range(KD):
                    i = eng.transpose(BK[4][:, k * P:(k + 1) * P], XG[:, p, k * P:(k + 1) * P], ident)
                i.then_inc(r["tr"], 1)

            def pe_up(t, p, n):
                if n == 0:
                    take_expert(p)
                e = expert(p)
                if n == 0:
                    eng.wait_ge(r["xt"], t + 1)
                need(eng, r["hb" if n else "ha"], t - 1)
                for k in range(KD):
                    i = eng.matmul(BK[2 * p + n][:, :], XTF[:, p, k, :],
                                   W1v[:, ds(e, 1), k, n * HF:(n + 1) * HF], start=k == 0, stop=k == KD - 1)
                i.then_inc(r[f"up{n}"], 1)
                if n:
                    fetch_expert(t + 1)

            def pe_hidden(t, p):
                need(eng, r["ht"], t)
                eng.wait_ge(r["gated"], t + 1)
                for k in range(KF):
                    i = eng.transpose(BK[5][:, k * P:(k + 1) * P], HB[:, p, k * P:(k + 1) * P], ident)
                i.then_inc(r["htr"], 1)

            def pe_down(t, p):
                e = expert(p)
                need(eng, r["yo"], t)
                eng.wait_ge(r["ht"], t + 1)
                for k in range(KF):
                    i = eng.matmul(BK[6][:, 0:D], HTv[:, p, k, :], W2[:, ds(e, 1), k, :],
                                   start=k == 0, stop=k == KF - 1)
                i.then_inc(r["y"], 1)

            def act_xt(t, p):
                need(eng, r["up1"], t - 1)
                eng.wait_ge(r["tr"], t + 1)
                eng.activation(XTF[:, p], BK[4][:, 0:D], ACT.Copy).then_inc(r["xt"], 1)

            def act_silu(t, p):
                eng.wait_ge(r["ha"], t + 1)
                eng.activation(HA[:, p], HA[:, p], ACT.Silu).then_inc(r["silu"], 1)

            def act_ht(t, p):
                need(eng, r["y"], t - 1)
                eng.wait_ge(r["htr"], t + 1)
                eng.activation(HT[:, p], BK[5][:, :], ACT.Copy).then_inc(r["ht"], 1)

            def dve_hidden(t, p):
                take_expert(p)
                e = expert(p)
                eng.wait_ge(r["up0"], t + 1)
                need(eng, r["gated"], t - 1)
                eng.tensor_tensor(HA[:, p], BK[2 * p][:, :], B1[:, ds(e, 1), 0:HF], ALU.add).then_inc(r["ha"], 1)
                eng.wait_ge(r["up1"], t + 1)
                need(eng, r["htr"], t - 1)
                eng.tensor_tensor(HB[:, p], BK[2 * p + 1][:, :], B1[:, ds(e, 1), HF:2 * HF], ALU.add
                                  ).then_inc(r["hb"], 1)
                eng.wait_ge(r["silu"], t + 1)
                eng.wait_ge(r["hb"], t + 1)
                eng.tensor_tensor(HB[:, p], HB[:, p], HA[:, p], ALU.mult).then_inc(r["gated"], 1)
                fetch_expert(t + 1)

            def dve_out(t, h, p):
                e = expert(p)
                need(eng, scat[p], 16 * h)
                eng.wait_ge(r["y"], t + 1)
                st(eng.tensor_tensor(YO[:, p], BK[6][:, 0:D], B2[:, ds(e, 1), :], ALU.add))
                st.after()
                eng.tensor_scalar(YO[:, p], YO[:, p], GATE[:, ds(t, 1)], None, ALU.mult).then_inc(r["yo"], 1)

            def body(h, parts=(0, 1)):
                for p in parts:
                    t = 2 * h + p
                    const = isinstance(h, int)

                    def there(x):
                        return not const or x < SLOTS_T
                    o = 1 - p
                    if eng_name == "pe":
                        if there(t + 1):
                            pe_up(t + 1, o, 0)
                        pe_hidden(t, p)
                        if there(t + 1):
                            pe_up(t + 1, o, 1)
                        if there(t + 2):
                            pe_transpose(t + 2, h + 1, p)
                        pe_down(t, p)
                    if eng_name == "pool":
                        if there(t + 3):
                            gather(t + 3, o)
                        scatter(t, h, p)
                        st.clear()
                    if eng_name == "act":
                        act_ht(t, p)
                        if there(t + 1):
                            act_silu(t + 1, o)
                        if there(t + 2):
                            act_xt(t + 2, p)
                    if eng_name == "dve":
                        if there(t + 1):
                            dve_hidden(t + 1, o)
                        dve_out(t, h, p)
                        st.clear()

            if eng_name == "pe":
                fetch_expert(0)
                pe_transpose(0, 0, 0)
                pe_up(0, 0, 0)
                pe_up(0, 0, 1)
                pe_transpose(1, 0, 1)
            if eng_name == "pool":
                for t in range(3):
                    gather(t, t % 2)
                st.clear()
            if eng_name == "act":
                act_xt(0, 0)
                act_silu(0, 0)
                act_xt(1, 1)
            if eng_name == "dve":
                fetch_expert(0)
                dve_hidden(0, 0)
            body(0)
            with eng.Fori(1, SLOTS_T // 2 - 1) as h:
                body(h)
            body(SLOTS_T // 2 - 1)
            body(SLOTS_T // 2, (0,))
            if eng_name == "pool":
                eng.wait_ge(scat[0], 16 * (SLOTS_T // 2 + 1))
                eng.wait_ge(scat[1], 16 * (SLOTS_T // 2))

        take = carve(PHASE)
        WQKV = take(3 * KD * AI).rearrange("p (s k n) -> p s k n", s=3, k=KD)
        WAO = take(KA * D).rearrange("p (k n) -> p k n", k=KA)
        LNWB = take(2 * KD).rearrange("p (s k) -> p s k", s=2)
        XH = take(2 * D).rearrange("p (b n) -> p b n", b=2)
        XTA = take(3 * D).rearrange("p (b k t) -> p b k t", b=3, k=KD)
        KDF, VDF, V1S = take(HF), take(HF), take(HF)
        PRD = take(2 * HF).rearrange("p (b n) -> p b n", b=2)
        SCO = take(2 * 8)
        SMX = take(2 * 8)
        SEX = take(2 * 2 * 8).rearrange("p (j n) -> p j n", j=2)
        SPR = take(2 * 8)
        OA = take(2 * HF).rearrange("p (b n) -> p b n", b=2)
        OT = take(2 * AI).rearrange("p (b k t) -> p b k t", b=2, k=KA)
        XR = take(2 * D).rearrange("p (b n) -> p b n", b=2)
        A = {n: sem("att_" + n) for n in (
            "w", "x", "xh", "tr", "xt", "xd", "kd", "vd", "v1", "q0", "q1", "kds", "vds", "v1s", "prod", "sin", "sexp",
            "out", "otr", "ot", "po", "x3", "mix", "x3b")}

        block = ctx.enter_context(nc.Block())

        @block.sync
        def _(sp):
            sp.dma_start(CST[:, :], consts).then_inc(loaded_small, 16)
            for b in range(2):
                sp.dma_start(Xv.rearrange("p (c b) d -> p c b d", b=2)[:, :, b, :],
                             u[b * L:(b + 1) * L, :].rearrange("(c p) d -> p c d", p=P)).then_inc(loaded_x, 16)
            sp.dma_start(WIN, w_in.rearrange("(k p) n -> p k n", p=P)).then_inc(loaded_small, 16)
            sp.dma_start(WOUT, w_mix_out.rearrange("(k p) n -> p k n", p=P)).then_inc(loaded_small, 16)
            sp.dma_start(CW, conv_w.rearrange("(m p) s -> p m s", p=P)).then_inc(loaded_small, 16)
            sp.dma_start(CB, conv_b.rearrange("(m p) -> p m", p=P), allow_slow_non_contiguous=True).then_inc(loaded_small, 16)
            sp.dma_start(NW, norm_w.rearrange("(m p) -> p m", p=P), allow_slow_non_contiguous=True).then_inc(loaded_small, 16)
            for dst, src in ((DTB, dt_bias), (ALG, a_log), (DSK, d_skip), (ROUTE_B[:, 0:E], b_route),
                             (ROUTE_B[:, E:2 * E], bias_n)):
                sp.dma_start(dst, src.unsqueeze(0).broadcast_to([P, 8])).then_inc(loaded_small, 16)
            sp.dma_start(WR[:, :].rearrange("p (k n) -> p k n", k=KD),
                         w_route.rearrange("(k p) n -> p k n", p=P)).then_inc(loaded_small, 16)
            for e in range(E):
                sp.dma_start(W1v[:, e], w1[e].rearrange("(k p) n -> p k n", p=P)).then_inc(loaded_w1, 16)
            barrier(sp)
            barrier(sp)

            def load_w2(n):
                sp.dma_start(W2, w2.rearrange("e (k p) n -> p e k n", p=P)).then_inc(loaded_w2, 16)
                sp.dma_start(B1, b1.unsqueeze(0).broadcast_to([P, E, 2 * HF])).then_inc(loaded_w2, 16)
                sp.dma_start(B2, b2.unsqueeze(0).broadcast_to([P, E, D])).then_inc(loaded_w2, 16)

            def store_x(dst, n):
                for b in range(2):
                    sp.dma_start(dst[b * L:(b + 1) * L, :].rearrange("(c p) d -> p c d", p=P),
                                 Xv.rearrange("p (c b) d -> p c b d", b=2)[:, :, b, :]).then_inc(stored_x, 16)
            load_w2(0)
            barrier(sp)
            store_x(acc_dram, 0)
            norm_sp(sp, norm_f[0])
            sp.wait_ge(stored_x, 32)
            barrier(sp)
            sp.wait_ge(loaded_w2, 48)
            barrier(sp)
            for b in range(2):
                sp.dma_start(Xv.rearrange("p (c b) d -> p c b d", b=2)[:, :, b, :],
                             acc_dram[b * L:(b + 1) * L, :].rearrange("(c p) d -> p c d", p=P)).then_inc(A["x"], 16)
            for s in range(3):
                sp.dma_start(WQKV[:, s], w_qkv[s].rearrange("(k p) n -> p k n", p=P)).then_inc(A["w"], 16)
            sp.dma_start(WAO, w_att_out.rearrange("(k p) n -> p k n", p=P)).then_inc(A["w"], 16)
            for s, src in enumerate((ln_w, ln_b)):
                sp.dma_start(LNWB[:, s], src.rearrange("(k p) -> p k", p=P), allow_slow_non_contiguous=True).then_inc(A["w"], 16)
            barrier(sp)
            load_w2(1)
            store_x(out, 1)
            norm_sp(sp, norm_f[1])
            sp.wait_ge(stored_x, 64)
            barrier(sp)
            sp.wait_ge(loaded_w2, 96)
            barrier(sp)

        @block.vector
        def _(dve):
            st = Steps(dve, dve_step)
            dve.wait_ge(loaded_x, 32)
            with dve.Fori(0, NQ) as q:
                dve.bn_stats(STv[:, ds(q, 1), :], Xv[:, ds(q, 1), :])
            dve.drain()
            rstd_steps(dve, st, root_ready, root_done, 1, MEAN, RSTD, VARE)
            st.clear()
            dve.wait_ge(loaded_small, 16 * 12)
            norm_dve(dve, norm_a)
            st(dve.tensor_copy(YT[:, 0], CST[:, C_MASK:C_MASK + P]))
            st.after()
            st(dve.tensor_copy(identb, CST[:, C_ID:C_ID + P]))
            st(dve.tensor_copy(maskb, YT[:, 0]))
            st(dve.memset(XB[:, :, :, 0:3], 0.0))
            st(dve.memset(SST, 0.0))
            for k in range(4):
                st(dve.tensor_scalar(WOUT[:, k, :], WOUT[:, k, :], NW[:, k:k + 1], None, ALU.mult))
            x, ax, s, w, pl, rl = SP_
            v3 = lambda ap: ap.rearrange("p (q h) -> p q h", h=H)
            dve.wait_ge(norm_a.pj, NQ)
            st(dve.tensor_tensor(v3(x), v3(BK[2][:, 0:NQ * H]), repeat(DTB, NQ), ALU.add))
            st.after()
            st(dve.scalar_tensor_tensor(ax, x, -1.0, x, ALU.mult, ALU.max))
            dve.tensor_scalar(rl, x, 0.0, None, ALU.max).then_inc(M["act_in"], 1)
            dve.wait_ge(M["act_out"], 1)
            st(dve.tensor_scalar(w, ax, 2.0, None, ALU.add))
            st.after()
            st(dve.reciprocal(w, w))
            st.after()
            st(dve.tensor_tensor(s, ax, w, ALU.mult))
            st.after()
            st(dve.tensor_tensor(w, s, s, ALU.mult))
            st.after()
            st(dve.tensor_scalar(pl, w, 1.0 / 17, None, ALU.mult))
            for d in (15, 13, 11, 9, 7, 5, 3):
                st.after()
                st(dve.scalar_tensor_tensor(pl, pl, 1.0 / d, w, ALU.add, ALU.mult))
            st.after()
            st(dve.scalar_tensor_tensor(pl, pl, 1.0, s, ALU.add, ALU.mult))
            st.after()
            st(dve.scalar_tensor_tensor(PDT, pl, 2.0, rl, ALU.mult, ALU.add))
            st.after()
            st(dve.tensor_scalar(ALG, ALG, -1.0, None, ALU.mult))
            st.after()
            dve.tensor_tensor(v3(PA), v3(PDT), repeat(ALG, NQ), ALU.mult).then_inc(M["act_in"], 1)
            dve.wait_ge(M["cum"], 1)
            st(dve.tensor_scalar(PNC, BK[3][:, 0:256], -1.0, None, ALU.mult))
            st(dve.tensor_copy(PEC, BK[3][:, 0:256]))
            st(dve.tensor_copy(PET, BK[3][:, 256:512]))
            st.after()
            dve.tensor_tensor(PWD, PET, PNC, ALU.add).then_inc(M["act_in"], 1)
            dve.wait_ge(M["act_out"], 2)
            st(dve.tensor_tensor(PWD, PWD, PDT, ALU.mult))
            st.clear()
            barrier(dve)

            def taps(c, lo, hi, prev):
                ns = prev
                for i in range(lo, hi):
                    s, m = divmod(i, MC)
                    if s:
                        st.after(ns[i - MC])
                    ins = dve.scalar_tensor_tensor(ACC[:, m], XB[:, m, :, s:s + P], CW[:, m, s:s + 1], ACC[:, m],
                                                   ALU.mult, ALU.add)
                    if i == 3 * MC - 1:
                        ins.then_inc(M["tapped"], 1)
                    else:
                        ns[i] = st(ins)
                return ns

            def mask(c, b):
                dve.wait_ge(M["decay"], 2 * c + b + 1)
                dve.wait_ge(M["bc"], 2 * c + b + 1)
                dve.tensor_tensor(LM, LM, BK[1][:, 0:P].unsqueeze(1).broadcast_to([P, H, P]),
                                  ALU.mult).then_inc(M["masked"], 1)

            def outputs(c, b):
                q = 2 * c + b
                y3 = Y[:, 0].rearrange("p (h n) -> p h n", h=H)
                dve.wait_ge(M["y2st"], q + 1)
                need(dve, M["ytr"], q)
                need(dve, M["square"], q)
                st(dve.tensor_tensor(y3, BK[0][:, :].rearrange("p (h n) -> p h n", h=H),
                                     spread(PEC[:, ds(q * 8, 8)], HD), ALU.mult))
                dve.wait_ge(M["scaled"], q + 1)
                st(dve.tensor_tensor(SST[:, b], SST[:, b], BK[2][:, :], ALU.add))
                dve.wait_ge(M["y1"], q + 1)
                st.after()
                st(dve.tensor_tensor(Y[:, 0], Y[:, 0], BK[1][:, :], ALU.add))
                st.after()
                st(dve.tensor_tensor(Y[:, 0], Y[:, 0], DX[:, b], ALU.add))
                dve.wait_ge(M["zs"], q + 1)
                st.after()
                dve.tensor_tensor(Y[:, 0], Y[:, 0], ZS[:, b], ALU.mult).then_inc(M["y"], 1)

            def xdt(c, b):
                q = 2 * c + b
                dve.wait_ge(M["xs"], q + 1)
                need(dve, M["y1"], q - 1)
                dve.tensor_tensor(XDT[:, b].rearrange("p (h n) -> p h n", h=H),
                                  XS[:, b].rearrange("p (h n) -> p h n", h=H),
                                  spread(PDT[:, ds(q * 8, 8)], HD), ALU.mult).then_inc(M["xdt"], 1)

            def mixer(c1, c):
                if c is not None:
                    mask(c, 0)
                if c1 is not None:
                    dve.wait_ge(M["taken"], c1 + 1)
                    ns = taps(c1, 0, 9, {})
                if c is not None:
                    outputs(c, 0)
                    mask(c, 1)
                if c1 is not None:
                    taps(c1, 9, 18, ns)
                if c is not None:
                    outputs(c, 1)
                if c1 is not None:
                    xdt(c1, 0)
                    xdt(c1, 1)
                st.clear()
            mixer(0, None)
            mixer(1, 0)
            with dve.Fori(1, NC - 1) as c:
                mixer(c + 1, c)
            mixer(None, NC - 1)
            barrier(dve)

            st(dve.tensor_scalar(VARE[:, :], SS, 1.0 / DI, EPS, ALU.mult, ALU.add))
            st.after()
            root(dve, st, root_ready, root_done, 2, VARE[:, :], RST2[:, :])
            st.clear()
            with dve.Fori(0, NQ) as q:
                st(dve.scalar_tensor_tensor(Xv[:, ds(q, 1), :], KEEPv[:, ds(q, 1), :], RST2[:, ds(q, 1)],
                                            Xv[:, ds(q, 1), :], ALU.mult, ALU.add))
                st.after()
                st(dve.bn_stats(STv[:, ds(q, 1), :], Xv[:, ds(q, 1), :]))
                st.clear()
            rstd_steps(dve, st, root_ready, root_done, 3, MEAN, RSTD, VARE)
            st.clear()
            barrier(dve)
            norm_dve(dve, norm_f[0])
            dve.wait_ge(norm_f[0].pj, NQ)
            route_dve(dve, st, 0)
            barrier(dve)
            dve.wait_ge(loaded_w2, 48)
            experts("dve", dve, st, 0, acc_dram)
            barrier(dve)

            dve.wait_ge(A["x"], 32)
            with dve.Fori(0, NQ) as q:
                dve.bn_stats(STv[:, ds(q, 1), :], Xv[:, ds(q, 1), :])
            dve.drain()
            rstd_steps(dve, st, root_ready, root_done, 4, MEAN, RSTD, VARE)
            st(dve.tensor_scalar(TMP[2][:, :], VARE[:, :], -EPS, None, ALU.add))
            st.after()
            st(dve.tensor_tensor(TMP[2][:, :], TMP[2][:, :], RSTD[:, :], ALU.mult))
            st.after()
            st(dve.tensor_tensor(TMP[2][:, :], TMP[2][:, :], RSTD[:, :], ALU.mult))
            st.after()
            st(dve.tensor_scalar(VARE[:, :], TMP[2][:, :], EPS, None, ALU.add))
            st.after()
            root(dve, st, root_ready, root_done, 5, VARE[:, :], RST2[:, :])
            st(dve.tensor_tensor(RST2[:, :], RST2[:, :], RSTD[:, :], ALU.mult))
            st.clear()
            dve.wait_ge(A["w"], 96)

            def normed(c):
                for b in range(2):
                    q = 2 * c + b
                    need(dve, A["tr"], c)
                    dve.tensor_scalar(XH[:, b], Xv[:, ds(q, 1), :], MEAN[:, ds(q, 1)],
                                      RST2[:, ds(q, 1)], ALU.subtract, ALU.mult).then_inc(A["xh"], 1)

            def difference(c):
                dve.wait_ge(A["xt"], c + 1)
                need(dve, A["v1"], 2 * c)
                dve.tensor_tensor(XTA[:, 2], XTA[:, 0], XTA[:, 1], ALU.subtract).then_inc(A["xd"], 1)

            def attend(c, h, between=None):
                s = 2 * c + h
                dve.wait_ge(A["kds"], s + 1)
                for b, sq in enumerate((A["q0"], A["q1"])):
                    dve.wait_ge(sq, s + 1)
                    dve.tensor_tensor(PRD[:, b], BK[1 + b][:, :], KDF, ALU.mult).then_inc(A["prod"], 1)
                for b in range(2):
                    dve.wait_ge(A["prod"], 2 * s + b + 1)
                    st(dve.tensor_reduce(SCO[:, b * 8:(b + 1) * 8], PRD[:, b].rearrange("p (h n) -> p h n", h=8),
                                         AX.X, ALU.add))
                st.after()
                scale = 1.0 / 16.0
                st(dve.tensor_scalar(SMX, SCO, scale, 0.0, ALU.mult, ALU.max))
                st.after()
                st(dve.scalar_tensor_tensor(SEX[:, 0], SCO, scale, SMX, ALU.mult, ALU.subtract))
                dve.tensor_scalar(SEX[:, 1], SMX, -1.0, None, ALU.mult).then_inc(A["sin"], 1)
                if between is not None:
                    difference(between)
                dve.wait_ge(A["sexp"], s + 1)
                st(dve.tensor_tensor(SMX, SEX[:, 0], SEX[:, 1], ALU.add))
                st.after()
                st(dve.reciprocal(SMX, SMX))
                st.after()
                st(dve.tensor_tensor(SPR, SEX[:, 0], SMX, ALU.mult))
                dve.wait_ge(A["v1s"], s + 1)
                dve.wait_ge(A["vds"], s + 1)
                st.after()
                for b in range(2):
                    need(dve, A["otr"], 2 * s + b - 1)
                    st(dve.tensor_tensor(OA[:, b].rearrange("p (h n) -> p h n", h=8),
                                         VDF.rearrange("p (h n) -> p h n", h=8),
                                         spread(SPR[:, b * 8:(b + 1) * 8], AD), ALU.mult))
                    st.after()
                    dve.tensor_tensor(OA[:, b], OA[:, b], V1S, ALU.add).then_inc(A["out"], 1)

            def residual(c):
                for b in range(2):
                    q = 2 * c + b
                    st(dve.tensor_scalar(XR[:, b], Xv[:, ds(q, 1), :], MEAN[:, ds(q, 1)], RSTD[:, ds(q, 1)],
                                         ALU.subtract, ALU.mult))
                    st.after()
                    st(dve.tensor_tensor(XR[:, b], XR[:, b], Xv[:, ds(q, 1), :], ALU.add))
                    dve.wait_ge(A["po"], 2 * c + 2)
                    st.after()
                    st(dve.tensor_tensor(Xv[:, ds(q, 1), :], XR[:, b], BK[6][:, b * D:(b + 1) * D], ALU.add))
                    st.after()
                    dve.bn_stats(STv[:, ds(q, 1), :], Xv[:, ds(q, 1), :]).then_inc(A["x3"], 1)

            def att(c, first=False, last=False):
                if not last:
                    normed(c + 1)
                attend(c, 0)
                if not first:
                    residual(c - 1)
                attend(c, 1, None if last else c + 1)
                st.clear()
            normed(0)
            difference(0)
            att(0, first=True)
            with dve.Fori(1, NC - 1) as c:
                att(c)
            att(NC - 1, last=True)
            residual(NC - 1)
            dve.wait_ge(A["x3"], NQ)
            rstd_steps(dve, st, root_ready, root_done, 6, MEAN, RSTD, VARE)
            st.clear()
            barrier(dve)
            norm_dve(dve, norm_f[1])
            dve.wait_ge(norm_f[1].pj, NQ)
            route_dve(dve, st, 1)
            barrier(dve)
            dve.wait_ge(loaded_w2, 96)
            experts("dve", dve, st, 1, out)
            barrier(dve)

        @block.scalar
        def _(act):
            act_root(act, 1)
            norm_act(act, norm_a)
            act.wait_ge(M["act_in"], 1)
            act.activation(SP_[1], SP_[1], ACT.Exp, scale=-1.0)
            act.activation(ALG, ALG, ACT.Exp).then_inc(M["act_out"], 1)
            act.wait_ge(M["act_in"], 3)
            act.activation(PEC, PEC, ACT.Exp)
            act.activation(PET, PET, ACT.Exp)
            act.activation(PWD, PWD, ACT.Exp).then_inc(M["act_out"], 1)
            barrier(act)
            st = Steps(act, act_step)

            def pre(c):
                act.wait_ge(M["xbc"], c + 1)
                if not (isinstance(c, int) and c == 0):
                    act.wait_ge(M["tapped"], c)
                    st(act.activation(XB[:, :, :, 0:3], XB[:, :, :, P:P + 3], ACT.Copy))
                need(act, M["xc"], c)
                for m in range(MC):
                    st(act.activation(ACC[:, m], BK[m // 2][:, (m % 2) * 256:(m % 2) * 256 + 256].rearrange(
                        "p (b t) -> p b t", b=2), ACT.Identity, bias=CB[:, m:m + 1], scale=CW[:, m, 3:4]))
                if not (isinstance(c, int) and c == 0):
                    st.after(1)
                for j in range(3):
                    i = act.activation(XB[:, 2 * j:2 * j + 2, :, 3:3 + P],
                                       BK[j][:, :].rearrange("p (m b t) -> p m b t", m=2, b=2), ACT.Copy)
                    if j < 2:
                        st(i)
                    else:
                        st.after()
                        i.then_inc(M["taken"], 1)

            def decays(c, b):
                q = 2 * c + b
                act.wait_ge(M["rg"], q + 1)
                need(act, M["y1"], q)
                for h in range(H):
                    i = act.activation(LM[:, h], BK[3 + h // 4][:, (h % 4) * P:(h % 4 + 1) * P], ACT.Exp,
                                       bias=PNC[:, ds(q * 8 + h, 1)])
                i.then_inc(M["decay"], 1)

            def y_out(c, b):
                q = 2 * c + b
                act.wait_ge(M["y"], q + 1)
                act.wait_ge(M["ytr"], q + 1)
                need(act, M["po"], q)
                act.activation(YT, BK[5][:, :].rearrange("p (k t) -> p k t", k=4), ACT.Copy).then_inc(M["yt"], 1)
                act.activation(ZS[:, b], Y[:, 0], ACT.Square, accum_out=SS[:, ds(q, 1)]).then_inc(M["square"], 1)

            def po_out(c, b):
                q = 2 * c + b
                act.wait_ge(M["po"], q + 1)
                act.activation(KEEPv[:, ds(q, 1), :], BK[6][:, 256:512], ACT.Copy).then_inc(M["po_out"], 1)

            def zs(c, b):
                q = 2 * c + b
                act.wait_ge(M["z"], q + 1)
                need(act, M["y"], q - 1)
                need(act, M["square"], q - 1)
                act.activation(ZS[:, b], BK[7][:, :], ACT.Silu).then_inc(M["zs"], 1)

            def xs(c, b):
                q = 2 * c + b
                act.wait_ge(M["xtr"], q + 1)
                need(act, M["xdec"], q - 1)
                need(act, M["y2st"], q - 1)
                st(act.activation(BT[:, b], BK[6][:, 0:P], ACT.Copy))
                st.after()
                act.activation(XS[:, b], BK[5][:, :], ACT.Copy).then_inc(M["xs"], 1)

            def mixer(c1, c):
                if c1 is not None:
                    pre(c1)
                if c is not None:
                    decays(c, 0)
                    decays(c, 1)
                    y_out(c, 0)
                    po_out(c, 0)
                if c1 is not None:
                    act.wait_ge(M["tapped"], c1 + 1)
                    need(act, M["y2st"], 2 * c1)
                    need(act, M["xtr"], 2 * c1)
                    act.activation(XC, ACC, ACT.Silu).then_inc(M["xc"], 1)
                    zs(c1, 0)
                if c is not None:
                    y_out(c, 1)
                if c1 is not None:
                    xs(c1, 0)
                if c is not None:
                    po_out(c, 1)
                if c1 is not None:
                    zs(c1, 1)
                    xs(c1, 1)
                st.clear()
            mixer(0, None)
            mixer(1, 0)
            with act.Fori(1, NC - 1) as c:
                mixer(c + 1, c)
            mixer(None, NC - 1)
            barrier(act)
            act_root(act, 2)
            act_root(act, 3)
            barrier(act)
            norm_act(act, norm_f[0])
            route_act(act, 0)
            barrier(act)
            experts("act", act, st, 0, acc_dram)
            barrier(act)
            act_root(act, 4)
            act_root(act, 5)
            act.wait_ge(A["w"], 96)

            def heads(c):
                act.wait_ge(A["tr"], c + 1)
                need(act, A["v1"], 2 * c)
                need(act, A["xd"], c)
                for k in range(KD):
                    i = act.activation(XTA[:, 0:2, k, :],
                                       BK[0][:, :].rearrange("p (b k t) -> p b k t", b=2, k=KD)[:, :, k, :],
                                       ACT.Identity, bias=LNWB[:, 1, k:k + 1], scale=LNWB[:, 0, k:k + 1])
                i.then_inc(A["xt"], 1)

            def copies(c, h):
                s = 2 * c + h
                act.wait_ge(A["kd"], s + 1)
                need(act, A["prod"], 2 * s)
                act.activation(KDF, BK[3][:, :], ACT.Copy).then_inc(A["kds"], 1)
                act.wait_ge(A["vd"], s + 1)
                need(act, A["out"], 2 * s)
                act.activation(VDF, BK[4][:, :], ACT.Copy).then_inc(A["vds"], 1)
                act.wait_ge(A["v1"], s + 1)
                act.activation(V1S, BK[5][:, :], ACT.Copy).then_inc(A["v1s"], 1)

            def exps(c, h):
                s = 2 * c + h
                act.wait_ge(A["sin"], s + 1)
                act.activation(SEX, SEX, ACT.Exp).then_inc(A["sexp"], 1)

            def transposed(c, h):
                s = 2 * c + h
                for b in range(2):
                    act.wait_ge(A["otr"], 2 * s + b + 1)
                    if h == 0:
                        need(act, A["po"], 2 * c)
                    act.activation(OT[:, b, 4 * h:4 * h + 4, :], BK[7 - 7 * b][:, :].rearrange("p (k t) -> p k t", k=4),
                                   ACT.Copy).then_inc(A["ot"], 1)

            def att(c, first=False, last=False):
                copies(c, 0)
                if not first:
                    transposed(c - 1, 1)
                exps(c, 0)
                copies(c, 1)
                if not last:
                    heads(c + 1)
                transposed(c, 0)
                exps(c, 1)
            heads(0)
            att(0, first=True)
            with act.Fori(1, NC - 1) as c:
                att(c)
            att(NC - 1, last=True)
            transposed(NC - 1, 1)
            act_root(act, 6)
            barrier(act)
            norm_act(act, norm_f[1])
            route_act(act, 1)
            barrier(act)
            experts("act", act, st, 1, out)
            barrier(act)

        @block.gpsimd
        def _(pool):
            st = Steps(pool, pool_step)
            st(pool.memset(DX, 0.0))
            st.after()
            for dst in (xn_dram, acc_dram, out):
                pool.dma_start(dst[NTOK:NTOK + P, :], DX[:, 0, 0:D]).then_inc(zeroed, 16)
            pool.wait_ge(zeroed, 48)
            st.clear()
            with pool.Fori(0, NC) as c:
                for b in range(2):
                    pool.wait_ge(norm_a.xt, 2 * c + b + 1)
                    pool.tensor_copy(KEEPv[:, ds(2 * c + b, 1), :], XT0[:, b].rearrange("p k t -> p (k t)")
                                     ).then_inc(norm_a.kept, 1)
            barrier(pool)

            def project_in(c):
                need(pool, M["z"], 2 * c)
                pool.tensor_copy(XTS, KEEPv[:, ds(2 * c, 2), :].rearrange("p b (k t) -> p k b t", k=KD)
                                 ).then_inc(M["xts"], 1)

            def decays(c):
                need(pool, M["rg"], 2 * c)
                pool.tensor_copy(ANOW.rearrange("p b h -> p (b h)"), PA[:, ds(16 * c, 16)]).then_inc(M["a_now"], 1)

            def state(c, b):
                q = 2 * c + b
                pool.wait_ge(M["y2st"], q + 1)
                s3 = SST[:, b].rearrange("p (h n) -> p h n", h=H)
                pool.tensor_tensor(s3, s3, spread(PET[:, ds(q * 8, 8)], HD), ALU.mult).then_inc(M["scaled"], 1)

            def inputs(c, b):
                q = 2 * c + b
                x3 = XS[:, b].rearrange("p (h n) -> p h n", h=H)
                pool.wait_ge(M["xs"], q + 1)
                need(pool, M["y2st"], q - 1)
                need(pool, M["y"], q - 1)
                st(pool.tensor_tensor(DX[:, b].rearrange("p (h n) -> p h n", h=H), x3, spread(DSK, HD), ALU.mult))
                st.after()
                pool.tensor_tensor(XDEC[:, b].rearrange("p (h n) -> p h n", h=H), x3,
                                   spread(PWD[:, ds(q * 8, 8)], HD), ALU.mult).then_inc(M["xdec"], 1)

            def mixer(c1, c):
                if c1 is not None:
                    project_in(c1)
                if c is not None:
                    decays(c)
                    state(c, 0)
                    state(c, 1)
                if c1 is not None:
                    inputs(c1, 0)
                    inputs(c1, 1)
                st.clear()
            mixer(0, None)
            mixer(1, 0)
            with pool.Fori(1, NC - 1) as c:
                mixer(c + 1, c)
            mixer(None, NC - 1)
            barrier(pool)
            barrier(pool)
            barrier(pool)
            experts("pool", pool, st, 0, acc_dram)
            barrier(pool)
            barrier(pool)
            barrier(pool)
            experts("pool", pool, st, 1, out)
            barrier(pool)

        @block.tensor
        def _(pe):
            pe.wait_ge(loaded_small, 16 * 12)
            norm_pe(pe, norm_a, BK[2])
            pe.wait_ge(M["act_in"], 2)
            pe.matmul(BK[3][:, 0:256], CST[:, C_UP:C_UP + P], PA, start=True, stop=True)
            pe.matmul(BK[3][:, 256:512], CST[:, C_ONE:C_ONE + P], PA, start=True, stop=True).then_inc(M["cum"], 1)
            barrier(pe)

            def xbc(c):
                pe.wait_ge(M["xts"], c + 1)
                need(pe, M["y"], 2 * c - 2)
                for m in range(MC):
                    for k in range(KD):
                        i = pe.matmul(BK[m // 2][:, (m % 2) * 256:(m % 2) * 256 + 256],
                                      WIN[:, k, DI + m * P:DI + (m + 1) * P],
                                      XTS[:, k].rearrange("p b t -> p (b t)"), start=k == 0, stop=k == KD - 1)
                i.then_inc(M["xbc"], 1)

            def z(c, b):
                q = 2 * c + b
                need(pe, M["zs"], q)
                for k in range(KD):
                    i = pe.matmul(BK[7][:, :], XTS[:, k, b, :], WIN[:, k, 0:DI], start=k == 0, stop=k == KD - 1)
                i.then_inc(M["z"], 1)

            def x_back(c, b):
                q = 2 * c + b
                pe.wait_ge(M["xc"], c + 1)
                need(pe, M["yt"], 2 * c)
                need(pe, M["po_out"], 2 * c - 1 + b)
                need(pe, M["xs"], q)
                for m in range(4):
                    pe.transpose(BK[5][:, m * P:(m + 1) * P], XC[:, m, b, :], ident)
                pe.transpose(BK[6][:, 0:P], XC[:, 4, b, :], ident).then_inc(M["xtr"], 1)

            def decay(c, b):
                q = 2 * c + b
                pe.wait_ge(M["a_now"], c + 1)
                need(pe, M["decay"], q)
                for g in range(2):
                    pe.matmul(BK[3 + g][:, :].rearrange("p (h i) -> p h i", h=4), identb,
                              maskb.unsqueeze(1).broadcast_to([P, 4, P]), start=True, stop=False)
                    for h in range(4):
                        i = pe.matmul(BK[3 + g][:, h * P:(h + 1) * P], ANOW[:, b, 4 * g + h:4 * g + h + 1].broadcast_to([P, P]),
                                  CST[:, C_UP:C_UP + P], start=False, stop=h == 3)
                        if g == 1 and h == 3:
                            i.then_inc(M["rg"], 1)

            def sums(c, b):
                q = 2 * c + b
                need(pe, M["taken"], c + 2 if not isinstance(c, int) or c < NC - 1 else c + 1)
                need(pe, M["y"], q)
                pe.matmul(BK[1][:, 0:P], XC[:, 4, b, :], XC[:, 5, b, :], start=True, stop=True).then_inc(M["bc"], 1)
                pe.wait_ge(M["xdec"], q + 1)
                pe.matmul(BK[0][:, :], XC[:, 5, b, :], SST[:, b], start=True, stop=True)
                pe.matmul(BK[2][:, :], BT[:, b], XDEC[:, b], start=True, stop=True).then_inc(M["y2st"], 1)
                pe.wait_ge(M["masked"], q + 1)
                pe.wait_ge(M["xdt"], q + 1)
                for h in range(H):
                    i = pe.matmul(BK[1][:, h * HD:(h + 1) * HD], LM[:, h, :], XDT[:, b, h * HD:(h + 1) * HD],
                                  start=True, stop=True)
                i.then_inc(M["y1"], 1)

            def y_back(c, b):
                q = 2 * c + b
                need(pe, M["yt"], q)
                need(pe, M["xs"], 2 * c + 2)
                pe.wait_ge(M["y"], q + 1)
                for k in range(4):
                    i = pe.transpose(BK[5][:, k * P:(k + 1) * P], Y[:, 0, k * P:(k + 1) * P], ident)
                i.then_inc(M["ytr"], 1)

            def mix_out(c, b, mx):
                q = 2 * c + b
                pe.wait_ge(M["yt"], q + 1)
                need(pe, M["po_out"], q)
                pe.wait_ge(M["xs"], mx)
                for k in range(4):
                    i = pe.matmul(BK[6][:, 256:512], YT[:, k, :], WOUT[:, k, :], start=k == 0, stop=k == 3)
                i.then_inc(M["po"], 1)

            def mixer(c1, c):
                if c1 is not None:
                    xbc(c1)
                if c is not None:
                    decay(c, 0)
                    sums(c, 0)
                    decay(c, 1)
                    y_back(c, 0)
                    sums(c, 1)
                    mix_out(c, 0, 2 * c + 2)
                if c1 is not None:
                    z(c1, 0)
                if c is not None:
                    y_back(c, 1)
                if c1 is not None:
                    x_back(c1, 0)
                if c is not None:
                    mix_out(c, 1, 2 * c + (2 if c1 is None else 3))
                if c1 is not None:
                    z(c1, 1)
                    x_back(c1, 1)
            mixer(0, None)
            mixer(1, 0)
            with pe.Fori(1, NC - 1) as c:
                mixer(c + 1, c)
            mixer(None, NC - 1)
            barrier(pe)
            barrier(pe)
            norm_pe(pe, norm_f[0], BK[2])
            route_pe(pe, 0)
            barrier(pe)
            pe.wait_ge(loaded_w1, 16 * E)
            pe.wait_ge(loaded_w2, 48)
            st = Steps(pe, pe_step)
            experts("pe", pe, st, 0, acc_dram)
            barrier(pe)
            pe.wait_ge(A["w"], 96)

            def heads(c):
                pe.wait_ge(A["xh"], 2 * c + 2)
                need(pe, A["xt"], c)
                need(pe, A["ot"], 4 * c - 4)
                for b in range(2):
                    for k in range(KD):
                        i = pe.transpose(BK[0][:, (2 * b + k) * P:(2 * b + k + 1) * P], XH[:, b, k * P:(k + 1) * P], ident)
                i.then_inc(A["tr"], 1)

            def project(c, h):
                s = 2 * c + h
                pe.wait_ge(A["xt"], c + 1)
                for bank, lhs, w, done, free, n in ((1, 0, 0, "q0", "prod", 2 * s), (2, 1, 0, "q1", "prod", 2 * s),
                                                    (3, 2, 1, "kd", "kds", s), (4, 2, 2, "vd", "vds", s),
                                                    (5, 1, 2, "v1", "v1s", s)):
                    need(pe, A[free], n)
                    if done == "kd":
                        pe.wait_ge(A["xd"], c + 1)
                    for k in range(KD):
                        i = pe.matmul(BK[bank][:, :], XTA[:, lhs, k, :], WQKV[:, w, k, h * HF:(h + 1) * HF],
                                      start=k == 0, stop=k == KD - 1)
                    i.then_inc(A[done], 1)

            def transposed(c, h, last=False):
                s = 2 * c + h
                for b in range(2):
                    need(pe, A["ot"], 2 * s + b - 1)
                    if b == 1:
                        pe.wait_ge(A["xt"], c + 1 if h or last else c + 2)
                    pe.wait_ge(A["out"], 2 * s + b + 1)
                    for k in range(4):
                        i = pe.transpose(BK[7 - 7 * b][:, k * P:(k + 1) * P], OA[:, b, k * P:(k + 1) * P], ident)
                    i.then_inc(A["otr"], 1)

            def att_out(c):
                need(pe, A["x3"], 2 * c)
                for b in range(2):
                    pe.wait_ge(A["ot"], 4 * c + 3 + b)
                    for k in range(KA):
                        i = pe.matmul(BK[6][:, b * D:(b + 1) * D], OT[:, b, k, :], WAO[:, k, :],
                                      start=k == 0, stop=k == KA - 1)
                    i.then_inc(A["po"], 1)

            def att(c, first=False, last=False):
                project(c, 0)
                if not first:
                    transposed(c - 1, 1)
                    att_out(c - 1)
                project(c, 1)
                if not last:
                    heads(c + 1)
                transposed(c, 0, last)
            heads(0)
            att(0, first=True)
            with pe.Fori(1, NC - 1) as c:
                att(c)
            att(NC - 1, last=True)
            transposed(NC - 1, 1)
            att_out(NC - 1)
            barrier(pe)
            norm_pe(pe, norm_f[1], BK[2])
            route_pe(pe, 1)
            barrier(pe)
            pe.wait_ge(loaded_w2, 96)
            experts("pe", pe, st, 1, out)
            barrier(pe)


def constants():
    import numpy as np
    c = np.zeros((P, C_N), np.float32)
    i, j = np.arange(P)[:, None], np.arange(P)[None, :]
    c[:, C_ID:C_ID + P] = i == j
    c[:, C_UP:C_UP + P] = i <= j
    c[:, C_ONE:C_ONE + P] = 1
    c[:, C_US:C_US + P] = i < j
    c[:, C_IOTA:C_IOTA + P] = j
    c[:, C_MASK:C_MASK + P] = np.where(j < i, MASKED, 0)
    c[:, C_IT:C_IT + ST] = np.arange(ST)
    q = np.arange(NQ)[None, :]
    c[:, C_TOK:C_TOK + NQ] = (q % 2) * L + (q // 2) * P + i - NTOK
    c[:, C_K128:C_K128 + NQ] = P * q
    c[:, C_REV:C_REV + E] = E - np.arange(E)
    c[:, C_PAD] = NTOK + np.arange(P)
    return c


def kernel(**inputs):
    import numpy as _np
    import concourse.bacc as _bacc
    from concourse import mybir as _mybir
    from concourse.bass_utils import run_bass_kernel_spmd as _run

    a = {k.split("_", 1)[1]: _np.asarray(v) for k, v in inputs.items()}
    t = _np.ascontiguousarray
    arrays = {
        "u": a["attn_a_u"].reshape(NTOK, D),
        "w_in": t(a["attn_a_W_in"].T),
        "conv_w": a["attn_a_conv_w"], "conv_b": a["attn_a_conv_b"], "dt_bias": a["attn_a_dt_bias"],
        "a_log": a["attn_a_A_log"], "d_skip": a["attn_a_D"], "norm_w": a["attn_a_norm_w"],
        "w_mix_out": t(a["attn_a_W_out"].T),
        "w_qkv": t(a["attn_b_w_qkv"].reshape(AH, 3, AD, D).transpose(1, 3, 0, 2)).reshape(3, D, AI),
        "w_att_out": t(a["attn_b_w_out"].T), "ln_w": a["attn_b_ln_w"], "ln_b": a["attn_b_ln_b"],
        "w_route": t(a["ffn_Wr"].T), "b_route": a["ffn_br"],
        "w1": a["ffn_Wl1"], "b1": a["ffn_bl1"], "w2": a["ffn_Wl2"], "b2": a["ffn_bl2"],
        "bias_n": a["ffn_biases_N"], "consts": constants(),
    }
    nc = _bacc.Bacc("TRN2", target_bir_lowering=False, num_devices=1)
    arrays = {f"in_{k}": t(v) for k, v in arrays.items()}
    args = [nc.dram_tensor(k, v.shape, _mybir.dt.from_np(v.dtype), kind="ExternalInput").ap() for k, v in arrays.items()]
    args.append(nc.dram_tensor("out_0", (NTOK + P, D), _mybir.dt.float32, kind="ExternalOutput").ap())
    hybrid_block(nc, *args)
    r = _run(nc, [arrays], core_ids=[0])
    return r.results[0]["out_0"][:NTOK].reshape(B, L, D)
```

```python
import concourse.bass as bass
from concourse import mybir
from contextlib import ExitStack

B, L, D = 2, 2048, 256
P = 128
NC = L // P
NQ = B * NC
KD = D // P
H, HD = 8, 64
DI = H * HD
NS = 128
CONV = DI + 2 * NS
MC = CONV // P
TAPS = 4
E, HF = 8, 512
TOPK = 2
KF = HF // P
SLOTS_T = B * L * TOPK // P + E - 1
ST = SLOTS_T + 1
AH, AD = 16, 64
AI = AH * AD
KA = AI // P
EPS = 1e-5
NTOK = B * L
BIG = 3.0e38
MASKED = -1.0e30

C_ID, C_UP, C_ONE, C_US, C_IOTA, C_MASK = 0, 128, 256, 384, 512, 640
C_IT = 768
C_TOK = C_IT + ST
C_K128 = C_TOK + NQ
C_REV = C_K128 + NQ
C_PAD = C_REV + E
C_N = C_PAD + 1


def hybrid_block(nc: bass.Bass, u, w_in, conv_w, conv_b, dt_bias, a_log, d_skip, norm_w, w_mix_out,
                 w_qkv, w_att_out, ln_w, ln_b, w_route, b_route, w1, b1, w2, b2, bias_n, consts, out):
    f32, bf16, i32 = mybir.dt.float32, mybir.dt.bfloat16, mybir.dt.int32
    ALU = mybir.AluOpType
    ACT = mybir.ActivationFunctionType
    AX = mybir.AxisListType
    ds = bass.ds

    ctx = ExitStack()
    with ctx:
        def sb(name, cols, dt=f32):
            return ctx.enter_context(nc.sbuf_tensor(name, [P, cols], dt))

        def sem(name):
            return ctx.enter_context(nc.semaphore(name))

        X = sb("X", NQ * D)
        KEEP = sb("KEEP", NQ * D)
        W1 = sb("W1", E * KD * 2 * HF)
        W1v = W1[:, :].rearrange("p (e k n) -> p e k n", e=E, k=KD)
        CST = sb("CST", C_N)
        WR = sb("WR", KD * E)
        STATS = sb("STATS", NQ * 6)
        MEAN, RSTD, VARE, RST2 = (sb(n, NQ) for n in ("MEAN", "RSTD", "VARE", "RST2"))
        TMP = [sb(f"TMP{i}", NQ) for i in range(3)]
        ROUTE_B = sb("ROUTE_B", 2 * E)
        GATE = sb("GATE", ST)
        IDX = sb("IDX", ST, i32)
        EXPERT = sb("EXPERT", ST, i32)
        IDC = sb("IDC", 4, i32)
        PHASE = sb("PHASE", 18848)

        Xv = X[:, :].rearrange("p (q d) -> p q d", d=D)
        KEEPv = KEEP[:, :].rearrange("p (q d) -> p q d", d=D)
        STv = STATS[:, :].rearrange("p (q s) -> p q s", s=6)
        ident = CST[:, C_ID:C_ID + P]

        def carve(base):
            at = [0]

            def take(cols):
                at[0] += cols
                assert at[0] <= base.shape[1], at[0]
                return base[:, at[0] - cols:at[0]]
            return take

        BK = [ctx.enter_context(nc.psum_tensor(f"BK{i}", [P, 512], f32)) for i in range(8)]

        def spread(ap, n):
            return ap.unsqueeze(2).broadcast_to([ap.shape[0], ap.shape[1], n])

        def repeat(ap, n):
            return ap.unsqueeze(1).broadcast_to([ap.shape[0], n, ap.shape[1]])

        def need(eng, s, value):
            if not isinstance(value, int) or value > 0:
                eng.wait_ge(s, value)

        class Steps:

            def __init__(self, eng, s):
                self.eng, self.s, self.n = eng, s, 0

            def __call__(self, instruction):
                instruction.then_inc(self.s, 1)
                self.n += 1
                return self.n

            def after(self, n=None):
                self.eng.wait_ge(self.s, self.n if n is None else n)

            def clear(self):
                if self.n:
                    self.after()
                    self.eng.sem_clear(self.s)
                    self.n = 0

        bar = sem("phase_done")
        bars = {}

        def barrier(eng, gp=False):
            n = bars[id(eng)] = bars.get(id(eng), 0) + 1
            eng.drain().then_inc(bar, 1)
            eng.wait_ge(bar, 5 * n)

        dve_step, act_step, pool_step, pe_step = sem("dve_step"), sem("act_step"), sem("pool_step"), sem("pe_step")
        loaded_x, loaded_small, loaded_w1, loaded_w2 = sem("loaded_x"), sem("loaded_small"), sem("loaded_w1"), sem("loaded_w2")
        stored_x, zeroed = sem("stored_x"), sem("zeroed")

        xn_dram = nc.dram_tensor("xn_dram", [NTOK + P, D], f32, kind="Internal").ap()
        acc_dram = nc.dram_tensor("acc_dram", [NTOK + P, D], f32, kind="Internal").ap()

        take = carve(PHASE)
        WIN = take(KD * 1288).rearrange("p (k n) -> p k n", k=KD)
        WOUT = take(4 * D).rearrange("p (k n) -> p k n", k=4)
        CW = take(MC * TAPS).rearrange("p (m s) -> p m s", m=MC)
        CB = take(MC)
        DTB, ALG, DSK = take(H), take(H), take(H)
        NW = take(4)
        PA, PNC, PEC, PDT, PWD, PET = (take(NQ * H) for _ in range(6))
        XB = take(MC * 2 * 131).rearrange("p (m b t) -> p m b t", m=MC, b=2)
        ACC = take(MC * 2 * P).rearrange("p (m b t) -> p m b t", m=MC, b=2)
        XC = take(MC * 2 * P).rearrange("p (m b t) -> p m b t", m=MC, b=2)
        XTS = take(2 * D).rearrange("p (k b t) -> p k b t", k=KD, b=2)
        XS, XDT, XDEC, DX, ZS, SST = (take(2 * DI).rearrange("p (b n) -> p b n", b=2) for _ in range(6))
        BT = take(2 * NS).rearrange("p (b n) -> p b n", b=2)
        Y = take(2 * DI).rearrange("p (b n) -> p b n", b=2)
        YT = take(2 * 4 * P).rearrange("p (b k t) -> p b k t", b=2, k=4)
        LM = W1[:, (E - 1) * KD * 2 * HF:].rearrange("p (b h i) -> p b h i", b=2, h=H)
        SS = take(NQ)
        ANOW = take(2 * H).rearrange("p (b h) -> p b h", b=2)
        MB = CST[:, C_MASK:C_MASK + P].bitcast(bf16)
        identb, maskb = MB[:, 0:P], MB[:, P:2 * P]
        SP_ = [ACC.rearrange("p m b t -> p (m b t)")[:, i * 256:(i + 1) * 256] for i in range(6)]
        XNB0 = XS
        XT0 = XDT.rearrange("p b (k t) -> p b k t", t=P)[:, :, 0:KD, :]

        take = carve(PHASE)
        W2 = take(E * KF * D).rearrange("p (e k n) -> p e k n", e=E, k=KF)
        B1 = take(E * 2 * HF).rearrange("p (e n) -> p e n", e=E)
        B2 = take(E * D).rearrange("p (e n) -> p e n", e=E)
        ftake = carve(KEEP)
        XG, YO = (ftake(2 * D).rearrange("p (b n) -> p b n", b=2) for _ in range(2))
        XTF = ftake(2 * D).rearrange("p (b k t) -> p b k t", b=2, k=KD)
        HA, HB, HT = (ftake(2 * HF).rearrange("p (b n) -> p b n", b=2) for _ in range(3))
        HTv = HT.rearrange("p b (k t) -> p b k t", t=P)

        def rstd_steps(dve, st, act_sq, act_done, n_call, mean, rstd, vare, extra=None):
            me, m2e, mo, m2o = STv[:, :, 1], STv[:, :, 2], STv[:, :, 4], STv[:, :, 5]
            t0, t1, t2 = (t[:, :] for t in TMP)
            a = st(dve.tensor_tensor(t0, me, mo, ALU.add))
            b = st(dve.tensor_tensor(t1, me, mo, ALU.subtract))
            c = st(dve.tensor_tensor(t2, m2e, m2o, ALU.add))
            st.after(a)
            st(dve.tensor_scalar(mean[:, :], t0, 0.5, None, ALU.mult))
            st.after()
            d = st(dve.tensor_tensor(t0, t1, t1, ALU.mult))
            st(dve.tensor_scalar(t2, t2, 1.0 / D, EPS, ALU.mult, ALU.add))
            st.after()
            st(dve.scalar_tensor_tensor(vare[:, :], t0, 0.25, t2, ALU.mult, ALU.add))
            st.after()
            root(dve, st, act_sq, act_done, n_call, vare[:, :], rstd[:, :])

        def root(dve, st, ready, done, n, v, r):
            dve.tensor_copy(TMP[0][:, :], v).then_inc(ready, 1)
            dve.wait_ge(done, n)
            st(dve.reciprocal(r, TMP[1][:, :]))
            st.after()
            st(dve.tensor_tensor(TMP[2][:, :], r, r, ALU.mult))
            st.after()
            st(dve.tensor_tensor(TMP[2][:, :], TMP[2][:, :], v, ALU.mult))
            st.after()
            st(dve.tensor_scalar(TMP[2][:, :], TMP[2][:, :], -0.5, 1.5, ALU.mult, ALU.add))
            st.after()
            st(dve.tensor_tensor(r, r, TMP[2][:, :], ALU.mult))
            st.after()

        root_ready, root_done = sem("root_ready"), sem("root_done")

        def act_root(act, n):
            act.wait_ge(root_ready, n)
            act.activation(TMP[1][:, :], TMP[0][:, :], ACT.Sqrt).then_inc(root_done, 1)

        class Norm:

            def __init__(self, tag, xnb, xt, w8, mean, rstd, keep, store):
                self.xn, self.tr, self.xt, self.pj, self.kept = (
                    sem(f"{n}_{tag}") for n in ("normed", "transposed", "xt_ready", "projected", "kept"))
                self.st = [sem(f"normed_stored{b}_{tag}") for b in range(2)]
                self.xnb, self.xT, self.w8, self.mean, self.rstd = xnb, xt, w8, mean, rstd
                self.keep, self.store = keep, store

        def norm_dve(dve, N):
            def body(c):
                for b in range(2):
                    q = 2 * c + b
                    need(dve, N.tr, q - 1)
                    if N.store:
                        need(dve, N.st[b], 16 * c)
                    dve.tensor_scalar(N.xnb[:, b, 0:D], Xv[:, ds(q, 1), :], N.mean[:, ds(q, 1)],
                                      N.rstd[:, ds(q, 1)], ALU.subtract, ALU.mult).then_inc(N.xn, 1)
            body(0)
            with dve.Fori(1, NC) as c:
                body(c)

        def norm_act(act, N):
            def body(c):
                for b in range(2):
                    q = 2 * c + b
                    need(act, N.pj, q - 1)
                    if N.keep:
                        need(act, N.kept, q - 1)
                    act.wait_ge(N.tr, q + 1)
                    act.activation(N.xT[:, b], BK[b][:, 0:D], ACT.Copy).then_inc(N.xt, 1)
            body(0)
            with act.Fori(1, NC) as c:
                body(c)

        def norm_pe(pe, N, dest):
            def transpose(c, b):
                q = 2 * c + b
                need(pe, N.xt, q - 1)
                pe.wait_ge(N.xn, q + 1)
                for k in range(KD):
                    t = pe.transpose(BK[b][:, k * P:(k + 1) * P], N.xnb[:, b, k * P:(k + 1) * P], ident)
                t.then_inc(N.tr, 1)

            def project(c, b):
                q = 2 * c + b
                pe.wait_ge(N.xt, q + 1)
                for k in range(KD):
                    m = pe.matmul(dest[:, ds(q * 8, 8)], N.xT[:, b, k, :], N.w8[:, k, :],
                                  start=k == 0, stop=k == KD - 1)
                m.then_inc(N.pj, 1)
            transpose(0, 0)
            transpose(0, 1)
            project(0, 0)
            with pe.Fori(1, NC) as c:
                transpose(c, 0)
                project(c - 1, 1)
                transpose(c, 1)
                project(c, 0)
            project(NC - 1, 1)

        def norm_sp(sp, N):
            def body(c):
                for b in range(2):
                    sp.wait_ge(N.xn, 2 * c + b + 1)
                    sp.dma_start(xn_dram[ds(c * P + b * L, P), :], N.xnb[:, b, 0:D]).then_inc(N.st[b], 16)
            body(0)
            with sp.Fori(1, NC) as c:
                body(c)
            for b in range(2):
                sp.wait_ge(N.st[b], 16 * NC)

        wdt = WIN[:, :, DI + CONV:DI + CONV + H]
        norm_a = Norm("a", XNB0, XT0, wdt, MEAN, RSTD, True, False)
        wr8 = WR[:, :].rearrange("p (k n) -> p k n", k=KD)

        M = {n: sem("mix_" + n) for n in (
            "act_in", "act_out", "cum", "a_now", "xts", "xbc", "taken", "tapped", "xc", "z", "zs", "rg", "bc",
            "decay", "masked", "y2", "st", "y1", "y2_read", "y1_read", "st_read", "y", "scaled", "ytr", "yt", "po", "po_out",
            "xtr", "xs", "xdt", "xdec", "dx", "square")}
        R = [{n: sem(f"{n}_{f}") for n in (
            "exp_in", "exp_out", "masks", "counts", "routed", "onehot", "listed", "lists", "idx",
            "gath0", "gath1", "tr", "xt", "up0", "up1", "ha", "silu", "hb", "gated", "htr", "ht", "y", "yo",
            "scat0", "scat1", "e_ready")} for f in range(2)]

        def router_scratch(base):
            t = carve(base)
            r = {}
            for n in ("SC", "W", "SBI", "EQ", "OH1", "OH2", "M12", "INC", "RK"):
                r[n] = t(NQ * E)
            for n in ("MX", "Z", "R1", "R2", "V1", "V2", "P1", "P2", "G1", "G2", "T1", "T2", "TI"):
                r[n] = t(NQ)
            r["CNT"], r["END"] = t(E), t(E)
            r["CMP"] = t(E * NQ)
            r["EF"] = t(ST)
            r["OHR"] = t(2 * P).rearrange("p (b n) -> p b n", b=2)
            r["RHS"] = t(2 * 2 * ST).rearrange("p (b j n) -> p b j n", b=2, j=2)
            r["ZERO"] = t(2 * ST)
            r["XNB"] = t(2 * D).rearrange("p (b n) -> p b n", b=2)
            r["XT"] = t(2 * D).rearrange("p (b k t) -> p b k t", b=2, k=KD)
            return r
        G = router_scratch(KEEP)
        norm_f = [Norm(f"f{f}", G["XNB"], G["XT"], wr8, MEAN, RSTD, False, True) for f in range(2)]

        def route_dve(dve, st, f):
            g, r = G, R[f]
            v3 = lambda ap: ap.rearrange("p (q e) -> p q e", e=E)
            sc, w, sbi, eq = g["SC"], g["W"], g["SBI"], g["EQ"]
            rev = repeat(CST[:, C_REV:C_REV + E], NQ)
            st(dve.tensor_tensor(v3(sc), v3(BK[2][:, 0:NQ * E]), repeat(ROUTE_B[:, 0:E], NQ), ALU.add))
            st.after()
            st(dve.tensor_reduce(g["MX"], v3(sc), AX.X, ALU.max))
            st(dve.tensor_tensor(v3(sbi), v3(sc), repeat(ROUTE_B[:, E:2 * E], NQ), ALU.add))
            st.after()
            dve.tensor_tensor(v3(w), v3(sc), spread(g["MX"], E), ALU.subtract).then_inc(r["exp_in"], 1)
            for k in range(TOPK):
                oh, rk = g[f"OH{k + 1}"], g[f"R{k + 1}"]
                st(dve.tensor_reduce(g["T1"], v3(sbi), AX.X, ALU.max))
                st.after()
                st(dve.tensor_tensor(v3(eq), v3(sbi), spread(g["T1"], E), ALU.is_equal))
                st.after()
                st(dve.tensor_tensor(v3(eq), v3(eq), rev, ALU.mult))
                st.after()
                st(dve.tensor_reduce(rk, v3(eq), AX.X, ALU.max))
                st.after()
                st(dve.tensor_tensor(v3(oh), spread(rk, E), rev, ALU.is_equal))
                st.after()
                if k == 0:
                    st(dve.scalar_tensor_tensor(sbi, oh, -BIG, sbi, ALU.mult, ALU.add))
                    st.after()
            dve.tensor_tensor(g["M12"], g["OH1"], g["OH2"], ALU.add).then_inc(r["masks"], 1)
            dve.wait_ge(r["exp_out"], 1)
            st(dve.tensor_reduce(g["Z"], v3(w), AX.X, ALU.add))
            st.after()
            st(dve.reciprocal(g["Z"], g["Z"]))
            st.after()
            st(dve.tensor_tensor(v3(w), v3(w), spread(g["Z"], E), ALU.mult))
            st.after()
            for k in range(TOPK):
                st(dve.tensor_tensor(eq, w, g[f"OH{k + 1}"], ALU.mult))
                st.after()
                st(dve.tensor_reduce(g[f"V{k + 1}"], v3(eq), AX.X, ALU.add))
                st.after()
            st(dve.tensor_tensor(g["T1"], g["V1"], g["V2"], ALU.add))
            st.after()
            st(dve.reciprocal(g["T1"], g["T1"]))
            st.after()
            for k in range(TOPK):
                st(dve.tensor_tensor(g[f"G{k + 1}"], g[f"V{k + 1}"], g["T1"], ALU.mult))
            dve.wait_ge(r["counts"], 1)
            tot = BK[3][:, 256:512]
            st(dve.tensor_copy(g["RK"], tot))
            st(dve.memset(eq, 1.0))
            st.after()
            for e in range(E):
                st(dve.tensor_tensor_scan(v3(g["INC"])[:, :, e], v3(eq)[:, :, e], v3(g["RK"])[:, :, e],
                                          0.0, ALU.mult, ALU.add))
            st.after()
            last = v3(g["INC"])[:, NQ - 1, :]
            cmp3 = g["CMP"].rearrange("p (e k) -> p e k", e=E)
            st(dve.tensor_tensor(cmp3, spread(last, NQ), repeat(CST[:, C_K128:C_K128 + NQ], E), ALU.is_gt))
            st.after()
            st(dve.tensor_reduce(g["CNT"], cmp3, AX.X, ALU.add))
            st.after()
            st(dve.tensor_tensor_scan(g["END"], eq[:, 0:E], g["CNT"], 0.0, ALU.mult, ALU.add))
            st.after()
            st(dve.tensor_tensor(g["CNT"], g["END"], g["CNT"], ALU.subtract))
            st.after()
            st(dve.tensor_scalar(g["CNT"], g["CNT"], float(P), None, ALU.mult))
            st(dve.tensor_tensor(g["INC"], g["INC"], g["RK"], ALU.subtract))
            st.after()
            st(dve.tensor_tensor(g["INC"], g["INC"], BK[3][:, 0:256], ALU.add))
            st.after()
            st(dve.tensor_tensor(v3(g["INC"]), v3(g["INC"]), repeat(g["CNT"], NQ), ALU.add))
            st.after()
            ti = g["TI"].bitcast(i32)
            for k in range(TOPK):
                p, row = g[f"P{k + 1}"], g[f"R{k + 1}"]
                st(dve.tensor_tensor(eq, g["INC"], g[f"OH{k + 1}"], ALU.mult))
                st.after()
                st(dve.tensor_reduce(g["T1"], v3(eq), AX.X, ALU.add))
                st.after()
                st(dve.tensor_copy(ti, g["T1"]))
                st.after()
                st(dve.tensor_single_scalar(ti, ti, 7, ALU.arith_shift_right))
                st.after()
                st(dve.tensor_copy(p, ti))
                st.after()
                st(dve.scalar_tensor_tensor(row, p, -float(P), g["T1"], ALU.mult, ALU.add))
                st.after()
                st(dve.tensor_tensor(g[f"V{k + 1}"], CST[:, C_TOK:C_TOK + NQ], row, ALU.subtract))
                st.after()
            st(dve.memset(g["EF"], 0.0))
            st(dve.memset(g["ZERO"], 0.0))
            st.after()
            for e in range(E - 1):
                st(dve.scalar_tensor_tensor(g["EF"], CST[:, C_IT:C_IT + ST], g["END"][:, e:e + 1], g["EF"],
                                            ALU.is_ge, ALU.add))
                st.after()
            dve.tensor_copy(EXPERT[:, :], g["EF"]).then_inc(r["e_ready"], 1)
            st.clear()

            def onehots(q):
                for k in range(TOPK):
                    need(dve, r["listed"], 2 * q + k - 1)
                    st(dve.tensor_scalar(g["OHR"][:, k], CST[:, C_IOTA:C_IOTA + P],
                                         g[f"R{k + 1}"][:, ds(q, 1)], None, ALU.is_equal))
                    st(dve.tensor_scalar(g["RHS"][:, k, 0], CST[:, C_IT:C_IT + ST],
                                         g[f"P{k + 1}"][:, ds(q, 1)], g[f"V{k + 1}"][:, ds(q, 1)],
                                         ALU.is_equal, ALU.mult))
                    st.after()
                    dve.tensor_scalar(g["RHS"][:, k, 1], CST[:, C_IT:C_IT + ST],
                                      g[f"P{k + 1}"][:, ds(q, 1)], g[f"G{k + 1}"][:, ds(q, 1)],
                                      ALU.is_equal, ALU.mult).then_inc(r["onehot"], 1)
                st.clear()
            onehots(0)
            with dve.Fori(1, NQ) as q:
                onehots(q)
            dve.wait_ge(r["lists"], 1)
            st(dve.tensor_scalar(g["EF"], BK[4][:, 0:ST], CST[:, C_PAD:C_PAD + 1], None, ALU.add))
            st(dve.tensor_copy(GATE[:, :], BK[4][:, ST:2 * ST]))
            st.after()
            dve.tensor_copy(IDX[:, :], g["EF"]).then_inc(r["idx"], 1)
            st.clear()

        def route_act(act, f):
            act.wait_ge(R[f]["exp_in"], 1)
            act.activation(G["W"], G["W"], ACT.Exp).then_inc(R[f]["exp_out"], 1)

        def route_pe(pe, f):
            r, g = R[f], G
            pe.wait_ge(r["masks"], 1)
            pe.matmul(BK[3][:, 0:256], CST[:, C_US:C_US + P], g["M12"], start=True, stop=True)
            pe.matmul(BK[3][:, 256:512], CST[:, C_ONE:C_ONE + P], g["M12"], start=True, stop=True
                      ).then_inc(r["counts"], 1)
            pe.wait_ge(r["e_ready"], 1)
            pe.matmul(BK[4][:, 0:2 * ST], ident, g["ZERO"], start=True, stop=False)

            def add(q):
                for k in range(TOPK):
                    pe.wait_ge(r["onehot"], 2 * q + k + 1)
                    pe.matmul(BK[4][:, 0:2 * ST], g["OHR"][:, k], g["RHS"][:, k].rearrange("p j n -> p (j n)"),
                              start=False, stop=False).then_inc(r["listed"], 1)
            with pe.Fori(0, NQ) as q:
                add(q)
            pe.matmul(BK[4][:, 0:2 * ST], ident, g["ZERO"], start=False, stop=True).then_inc(r["lists"], 1)

        def experts(eng_name, eng, st, f, acc):
            r = R[f]
            gath, scat = (r["gath0"], r["gath1"]), (r["scat0"], r["scat1"])

            if eng_name in ("pe", "dve"):
                coming = eng.alloc_register(f"{eng_name}_coming_{f}")
                under_way = [eng.alloc_register(f"{eng_name}_expert{p}_{f}") for p in range(2)]

            def fetch_expert(t):
                eng.load(coming, EXPERT[0:1, ds(t, 1)])

            def take_expert(p):
                eng.reg_mov(under_way[p], coming)

            def expert(p):
                return eng.snap(under_way[p], min_val=0, max_val=E - 1)

            def gather(t, p):
                need(eng, r["tr"], t - 1)
                eng.wait_ge(r["idx"], 1)
                st(eng.tensor_copy(IDC[:, p:p + 1], IDX[:, ds(t, 1)]))
                st.after()
                eng.indirect_dma_start(out=XG[:, p, :], out_offset=None, in_=xn_dram,
                                       in_offset=bass.IndirectOffsetOnAxis(ap=IDC[:, p:p + 1], axis=0)
                                       ).then_inc(gath[p], 16)

            def scatter(t, h, p):
                eng.wait_ge(r["yo"], t + 1)
                if not (isinstance(t, int) and t == 0):
                    eng.wait_ge(scat[1 - p], 16 * (h + p))
                st(eng.tensor_copy(IDC[:, 2 + p:3 + p], IDX[:, ds(t, 1)]))
                st.after()
                eng.indirect_dma_start(out=acc, out_offset=bass.IndirectOffsetOnAxis(ap=IDC[:, 2 + p:3 + p], axis=0),
                                       in_=YO[:, p, :], in_offset=None, compute_op=ALU.add
                                       ).then_inc(scat[p], 16)

            def pe_transpose(t, h, p):
                need(eng, r["xt"], t)
                eng.wait_ge(gath[p], 16 * (h + 1))
                for k in range(KD):
                    i = eng.transpose(BK[4][:, k * P:(k + 1) * P], XG[:, p, k * P:(k + 1) * P], ident)
                i.then_inc(r["tr"], 1)

            def pe_up(t, p, n):
                if n == 0:
                    take_expert(p)
                e = expert(p)
                if n == 0:
                    eng.wait_ge(r["xt"], t + 1)
                need(eng, r["hb" if n else "ha"], t - 1)
                for k in range(KD):
                    i = eng.matmul(BK[2 * p + n][:, :], XTF[:, p, k, :],
                                   W1v[:, ds(e, 1), k, n * HF:(n + 1) * HF], start=k == 0, stop=k == KD - 1)
                i.then_inc(r[f"up{n}"], 1)
                if n:
                    fetch_expert(t + 1)

            def pe_hidden(t, p):
                need(eng, r["ht"], t)
                eng.wait_ge(r["gated"], t + 1)
                for k in range(KF):
                    i = eng.transpose(BK[5][:, k * P:(k + 1) * P], HB[:, p, k * P:(k + 1) * P], ident)
                i.then_inc(r["htr"], 1)

            def pe_down(t, p):
                e = expert(p)
                need(eng, r["yo"], t)
                eng.wait_ge(r["ht"], t + 1)
                for k in range(KF):
                    i = eng.matmul(BK[6][:, 0:D], HTv[:, p, k, :], W2[:, ds(e, 1), k, :],
                                   start=k == 0, stop=k == KF - 1)
                i.then_inc(r["y"], 1)

            def act_xt(t, p):
                need(eng, r["up1"], t - 1)
                eng.wait_ge(r["tr"], t + 1)
                eng.activation(XTF[:, p], BK[4][:, 0:D], ACT.Copy).then_inc(r["xt"], 1)

            def act_silu(t, p):
                eng.wait_ge(r["ha"], t + 1)
                eng.activation(HA[:, p], HA[:, p], ACT.Silu).then_inc(r["silu"], 1)

            def act_ht(t, p):
                need(eng, r["y"], t - 1)
                eng.wait_ge(r["htr"], t + 1)
                eng.activation(HT[:, p], BK[5][:, :], ACT.Copy).then_inc(r["ht"], 1)

            def dve_hidden(t, p):
                take_expert(p)
                e = expert(p)
                eng.wait_ge(r["up0"], t + 1)
                need(eng, r["gated"], t - 1)
                eng.tensor_tensor(HA[:, p], BK[2 * p][:, :], B1[:, ds(e, 1), 0:HF], ALU.add).then_inc(r["ha"], 1)
                eng.wait_ge(r["up1"], t + 1)
                need(eng, r["htr"], t - 1)
                eng.tensor_tensor(HB[:, p], BK[2 * p + 1][:, :], B1[:, ds(e, 1), HF:2 * HF], ALU.add
                                  ).then_inc(r["hb"], 1)
                eng.wait_ge(r["silu"], t + 1)
                eng.wait_ge(r["hb"], t + 1)
                eng.tensor_tensor(HB[:, p], HB[:, p], HA[:, p], ALU.mult).then_inc(r["gated"], 1)
                fetch_expert(t + 1)

            def dve_out(t, h, p):
                e = expert(p)
                need(eng, scat[p], 16 * h)
                eng.wait_ge(r["y"], t + 1)
                st(eng.tensor_tensor(YO[:, p], BK[6][:, 0:D], B2[:, ds(e, 1), :], ALU.add))
                st.after()
                eng.tensor_scalar(YO[:, p], YO[:, p], GATE[:, ds(t, 1)], None, ALU.mult).then_inc(r["yo"], 1)

            def body(h, parts=(0, 1)):
                for p in parts:
                    t = 2 * h + p
                    const = isinstance(h, int)

                    def there(x):
                        return not const or x < SLOTS_T
                    o = 1 - p
                    if eng_name == "pe":
                        if there(t + 1):
                            pe_up(t + 1, o, 0)
                        pe_hidden(t, p)
                        if there(t + 1):
                            pe_up(t + 1, o, 1)
                        if there(t + 2):
                            pe_transpose(t + 2, h + 1, p)
                        pe_down(t, p)
                    if eng_name == "pool":
                        if there(t + 3):
                            gather(t + 3, o)
                        scatter(t, h, p)
                        st.clear()
                    if eng_name == "act":
                        act_ht(t, p)
                        if there(t + 1):
                            act_silu(t + 1, o)
                        if there(t + 2):
                            act_xt(t + 2, p)
                    if eng_name == "dve":
                        if there(t + 1):
                            dve_hidden(t + 1, o)
                        dve_out(t, h, p)
                        st.clear()

            if eng_name == "pe":
                fetch_expert(0)
                pe_transpose(0, 0, 0)
                pe_up(0, 0, 0)
                pe_up(0, 0, 1)
                pe_transpose(1, 0, 1)
            if eng_name == "pool":
                for t in range(3):
                    gather(t, t % 2)
                st.clear()
            if eng_name == "act":
                act_xt(0, 0)
                act_silu(0, 0)
                act_xt(1, 1)
            if eng_name == "dve":
                fetch_expert(0)
                dve_hidden(0, 0)
            body(0)
            with eng.Fori(1, SLOTS_T // 2 - 1) as h:
                body(h)
            body(SLOTS_T // 2 - 1)
            body(SLOTS_T // 2, (0,))
            if eng_name == "pool":
                eng.wait_ge(scat[0], 16 * (SLOTS_T // 2 + 1))
                eng.wait_ge(scat[1], 16 * (SLOTS_T // 2))

        take = carve(PHASE)
        WQKV = take(3 * KD * AI).rearrange("p (s k n) -> p s k n", s=3, k=KD)
        WAO = take(KA * D).rearrange("p (k n) -> p k n", k=KA)
        LNWB = take(2 * KD).rearrange("p (s k) -> p s k", s=2)
        XH = take(2 * D).rearrange("p (b n) -> p b n", b=2)
        XTA = take(3 * D).rearrange("p (b k t) -> p b k t", b=3, k=KD)
        KDF, VDF, V1S = take(HF), take(HF), take(HF)
        PRD = take(2 * HF).rearrange("p (b n) -> p b n", b=2)
        SCO = take(2 * 8)
        SMX = take(2 * 8)
        SEX = take(2 * 2 * 8).rearrange("p (j n) -> p j n", j=2)
        SPR = take(2 * 8)
        OA = take(2 * HF).rearrange("p (b n) -> p b n", b=2)
        OT = take(2 * AI).rearrange("p (b k t) -> p b k t", b=2, k=KA)
        XR = take(2 * D).rearrange("p (b n) -> p b n", b=2)
        A = {n: sem("att_" + n) for n in (
            "w", "x", "xh", "tr", "xt", "xd", "kd", "vd", "v1", "q0", "q1", "kds", "vds", "v1s", "prod", "sin", "sexp",
            "out", "otr", "ot", "po", "x3", "mix", "x3b")}

        block = ctx.enter_context(nc.Block())

        @block.sync
        def _(sp):
            sp.dma_start(CST[:, :], consts).then_inc(loaded_small, 16)
            for b in range(2):
                sp.dma_start(Xv.rearrange("p (c b) d -> p c b d", b=2)[:, :, b, :],
                             u[b * L:(b + 1) * L, :].rearrange("(c p) d -> p c d", p=P)).then_inc(loaded_x, 16)
            sp.dma_start(WIN, w_in.rearrange("(k p) n -> p k n", p=P)).then_inc(loaded_small, 16)
            sp.dma_start(WOUT, w_mix_out.rearrange("(k p) n -> p k n", p=P)).then_inc(loaded_small, 16)
            sp.dma_start(CW, conv_w.rearrange("(m p) s -> p m s", p=P)).then_inc(loaded_small, 16)
            sp.dma_start(CB, conv_b.rearrange("(m p) -> p m", p=P), allow_slow_non_contiguous=True).then_inc(loaded_small, 16)
            sp.dma_start(NW, norm_w.rearrange("(m p) -> p m", p=P), allow_slow_non_contiguous=True).then_inc(loaded_small, 16)
            for dst, src in ((DTB, dt_bias), (ALG, a_log), (DSK, d_skip), (ROUTE_B[:, 0:E], b_route),
                             (ROUTE_B[:, E:2 * E], bias_n)):
                sp.dma_start(dst, src.unsqueeze(0).broadcast_to([P, 8])).then_inc(loaded_small, 16)
            sp.dma_start(WR[:, :].rearrange("p (k n) -> p k n", k=KD),
                         w_route.rearrange("(k p) n -> p k n", p=P)).then_inc(loaded_small, 16)
            for e in range(E - 1):
                sp.dma_start(W1v[:, e], w1[e].rearrange("(k p) n -> p k n", p=P)).then_inc(loaded_w1, 16)
            barrier(sp)
            barrier(sp)

            def load_w2(n):
                sp.dma_start(W2, w2.rearrange("e (k p) n -> p e k n", p=P)).then_inc(loaded_w2, 16)
                sp.dma_start(B1, b1.unsqueeze(0).broadcast_to([P, E, 2 * HF])).then_inc(loaded_w2, 16)
                sp.dma_start(B2, b2.unsqueeze(0).broadcast_to([P, E, D])).then_inc(loaded_w2, 16)

            def store_x(dst, n):
                for b in range(2):
                    sp.dma_start(dst[b * L:(b + 1) * L, :].rearrange("(c p) d -> p c d", p=P),
                                 Xv.rearrange("p (c b) d -> p c b d", b=2)[:, :, b, :]).then_inc(stored_x, 16)
            sp.dma_start(W1v[:, E - 1], w1[E - 1].rearrange("(k p) n -> p k n", p=P)).then_inc(loaded_w1, 16)
            load_w2(0)
            barrier(sp)
            store_x(acc_dram, 0)
            norm_sp(sp, norm_f[0])
            sp.wait_ge(stored_x, 32)
            barrier(sp)
            sp.wait_ge(loaded_w2, 48)
            barrier(sp)
            for b in range(2):
                sp.dma_start(Xv.rearrange("p (c b) d -> p c b d", b=2)[:, :, b, :],
                             acc_dram[b * L:(b + 1) * L, :].rearrange("(c p) d -> p c d", p=P)).then_inc(A["x"], 16)
            for s in range(3):
                sp.dma_start(WQKV[:, s], w_qkv[s].rearrange("(k p) n -> p k n", p=P)).then_inc(A["w"], 16)
            sp.dma_start(WAO, w_att_out.rearrange("(k p) n -> p k n", p=P)).then_inc(A["w"], 16)
            for s, src in enumerate((ln_w, ln_b)):
                sp.dma_start(LNWB[:, s], src.rearrange("(k p) -> p k", p=P), allow_slow_non_contiguous=True).then_inc(A["w"], 16)
            barrier(sp)
            load_w2(1)
            store_x(out, 1)
            norm_sp(sp, norm_f[1])
            sp.wait_ge(stored_x, 64)
            barrier(sp)
            sp.wait_ge(loaded_w2, 96)
            barrier(sp)

        @block.vector
        def _(dve):
            st = Steps(dve, dve_step)
            dve.wait_ge(loaded_x, 32)
            with dve.Fori(0, NQ) as q:
                dve.bn_stats(STv[:, ds(q, 1), :], Xv[:, ds(q, 1), :])
            dve.drain()
            rstd_steps(dve, st, root_ready, root_done, 1, MEAN, RSTD, VARE)
            st.clear()
            dve.wait_ge(loaded_small, 16 * 12)
            norm_dve(dve, norm_a)
            st(dve.tensor_copy(YT[:, 0, 0], CST[:, C_MASK:C_MASK + P]))
            st.after()
            st(dve.tensor_copy(identb, CST[:, C_ID:C_ID + P]))
            st(dve.tensor_copy(maskb, YT[:, 0, 0]))
            st(dve.memset(XB[:, :, :, 0:3], 0.0))
            st(dve.memset(SST, 0.0))
            for k in range(4):
                st(dve.tensor_scalar(WOUT[:, k, :], WOUT[:, k, :], NW[:, k:k + 1], None, ALU.mult))
            x, ax, s, w, pl, rl = SP_
            v3 = lambda ap: ap.rearrange("p (q h) -> p q h", h=H)
            dve.wait_ge(norm_a.pj, NQ)
            st(dve.tensor_tensor(v3(x), v3(BK[2][:, 0:NQ * H]), repeat(DTB, NQ), ALU.add))
            st.after()
            st(dve.scalar_tensor_tensor(ax, x, -1.0, x, ALU.mult, ALU.max))
            dve.tensor_scalar(rl, x, 0.0, None, ALU.max).then_inc(M["act_in"], 1)
            dve.wait_ge(M["act_out"], 1)
            st(dve.tensor_scalar(w, ax, 2.0, None, ALU.add))
            st.after()
            st(dve.reciprocal(w, w))
            st.after()
            st(dve.tensor_tensor(s, ax, w, ALU.mult))
            st.after()
            st(dve.tensor_tensor(w, s, s, ALU.mult))
            st.after()
            st(dve.tensor_scalar(pl, w, 1.0 / 17, None, ALU.mult))
            for d in (15, 13, 11, 9, 7, 5, 3):
                st.after()
                st(dve.scalar_tensor_tensor(pl, pl, 1.0 / d, w, ALU.add, ALU.mult))
            st.after()
            st(dve.scalar_tensor_tensor(pl, pl, 1.0, s, ALU.add, ALU.mult))
            st.after()
            st(dve.scalar_tensor_tensor(PDT, pl, 2.0, rl, ALU.mult, ALU.add))
            st.after()
            st(dve.tensor_scalar(ALG, ALG, -1.0, None, ALU.mult))
            st.after()
            dve.tensor_tensor(v3(PA), v3(PDT), repeat(ALG, NQ), ALU.mult).then_inc(M["act_in"], 1)
            dve.wait_ge(M["cum"], 1)
            st(dve.tensor_scalar(PNC, BK[3][:, 0:256], -1.0, None, ALU.mult))
            st(dve.tensor_copy(PEC, BK[3][:, 0:256]))
            st(dve.tensor_copy(PET, BK[3][:, 256:512]))
            st.after()
            dve.tensor_tensor(PWD, PET, PNC, ALU.add).then_inc(M["act_in"], 1)
            dve.wait_ge(M["act_out"], 2)
            st(dve.tensor_tensor(PWD, PWD, PDT, ALU.mult))
            st.clear()
            barrier(dve)

            def taps(c, lo, hi, prev):
                ns = prev
                for i in range(lo, hi):
                    s, m = divmod(i, MC)
                    if s:
                        st.after(ns[i - MC])
                    ins = dve.scalar_tensor_tensor(ACC[:, m], XB[:, m, :, s:s + P], CW[:, m, s:s + 1], ACC[:, m],
                                                   ALU.mult, ALU.add)
                    if i == 3 * MC - 1:
                        ins.then_inc(M["tapped"], 1)
                    else:
                        ns[i] = st(ins)
                return ns

            def mask(c, b):
                dve.wait_ge(M["decay"], 2 * c + b + 1)
                if b:
                    dve.wait_ge(M["xs"], 2 * c + 2)
                else:
                    dve.wait_ge(M["bc"], c + 1)
                bc = BK[6][:, P:2 * P] if b else BK[1][:, 0:P]
                dve.tensor_tensor(LM[:, b], LM[:, b], bc.unsqueeze(1).broadcast_to([P, H, P]),
                                  ALU.mult).then_inc(M["masked"], 1)

            def from_state(c, b):
                q = 2 * c + b
                need(dve, M["ytr"], q - 1)
                need(dve, M["square"], q - 1)
                dve.wait_ge(M["y2"], q + 1)
                dve.tensor_tensor(Y[:, b].rearrange("p (h n) -> p h n", h=H),
                                  BK[0][:, :].rearrange("p (h n) -> p h n", h=H),
                                  spread(PEC[:, ds(q * 8, 8)], HD), ALU.mult).then_inc(M["y2_read"], 1)

            def within(c, b):
                q = 2 * c + b
                dve.wait_ge(M["y1"], q + 1)
                dve.wait_ge(M["y2_read"], q + 1)
                dve.tensor_tensor(Y[:, b], Y[:, b], BK[1][:, :], ALU.add).then_inc(M["y1_read"], 1)

            def increment(c, b):
                q = 2 * c + b
                dve.wait_ge(M["st"], q + 1)
                dve.wait_ge(M["scaled"], q + 1)
                dve.tensor_tensor(SST[:, b], SST[:, b], BK[2][:, :], ALU.add).then_inc(M["st_read"], 1)

            def outputs(c, b):
                q = 2 * c + b
                dve.wait_ge(M["dx"], q + 1)
                dve.wait_ge(M["y1_read"], q + 1)
                st(dve.tensor_tensor(Y[:, b], Y[:, b], DX[:, b], ALU.add))
                dve.wait_ge(M["zs"], q + 1)
                st.after()
                dve.tensor_tensor(Y[:, b], Y[:, b], ZS[:, b], ALU.mult).then_inc(M["y"], 1)

            def xdt(c, b):
                q = 2 * c + b
                dve.wait_ge(M["xs"], q + 1)
                need(dve, M["y1"], q - 1)
                dve.tensor_tensor(XDT[:, b].rearrange("p (h n) -> p h n", h=H),
                                  XS[:, b].rearrange("p (h n) -> p h n", h=H),
                                  spread(PDT[:, ds(q * 8, 8)], HD), ALU.mult).then_inc(M["xdt"], 1)

            def mixer(c, n):
                ns = {}

                def some_taps(lo, hi):
                    if n is not None:
                        taps(n, lo, hi, ns)
                if n is not None:
                    dve.wait_ge(M["taken"], 3 * n + 3)
                some_taps(0, 8)
                if c is not None:
                    xdt(c, 0)
                    mask(c, 0)
                    from_state(c, 0)
                    xdt(c, 1)
                    increment(c, 0)
                some_taps(8, 10)
                if c is not None:
                    within(c, 0)
                    mask(c, 1)
                    outputs(c, 0)
                    from_state(c, 1)
                    increment(c, 1)
                    within(c, 1)
                    outputs(c, 1)
                some_taps(10, 18)
                st.clear()
            mixer(None, 0)
            mixer(0, 1)
            with dve.Fori(1, NC - 1) as c:
                mixer(c, c + 1)
            mixer(NC - 1, None)
            barrier(dve)

            st(dve.tensor_scalar(VARE[:, :], SS, 1.0 / DI, EPS, ALU.mult, ALU.add))
            st.after()
            root(dve, st, root_ready, root_done, 2, VARE[:, :], RST2[:, :])
            st.clear()
            with dve.Fori(0, NQ) as q:
                st(dve.scalar_tensor_tensor(Xv[:, ds(q, 1), :], KEEPv[:, ds(q, 1), :], RST2[:, ds(q, 1)],
                                            Xv[:, ds(q, 1), :], ALU.mult, ALU.add))
                st.after()
                st(dve.bn_stats(STv[:, ds(q, 1), :], Xv[:, ds(q, 1), :]))
                st.clear()
            rstd_steps(dve, st, root_ready, root_done, 3, MEAN, RSTD, VARE)
            st.clear()
            barrier(dve)
            norm_dve(dve, norm_f[0])
            dve.wait_ge(norm_f[0].pj, NQ)
            route_dve(dve, st, 0)
            barrier(dve)
            dve.wait_ge(loaded_w2, 48)
            experts("dve", dve, st, 0, acc_dram)
            barrier(dve)

            dve.wait_ge(A["x"], 32)
            with dve.Fori(0, NQ) as q:
                dve.bn_stats(STv[:, ds(q, 1), :], Xv[:, ds(q, 1), :])
            dve.drain()
            rstd_steps(dve, st, root_ready, root_done, 4, MEAN, RSTD, VARE)
            st(dve.tensor_scalar(TMP[2][:, :], VARE[:, :], -EPS, None, ALU.add))
            st.after()
            st(dve.tensor_tensor(TMP[2][:, :], TMP[2][:, :], RSTD[:, :], ALU.mult))
            st.after()
            st(dve.tensor_tensor(TMP[2][:, :], TMP[2][:, :], RSTD[:, :], ALU.mult))
            st.after()
            st(dve.tensor_scalar(VARE[:, :], TMP[2][:, :], EPS, None, ALU.add))
            st.after()
            root(dve, st, root_ready, root_done, 5, VARE[:, :], RST2[:, :])
            st(dve.tensor_tensor(RST2[:, :], RST2[:, :], RSTD[:, :], ALU.mult))
            st.clear()
            dve.wait_ge(A["w"], 96)

            def normed(c):
                for b in range(2):
                    q = 2 * c + b
                    need(dve, A["tr"], c)
                    dve.tensor_scalar(XH[:, b], Xv[:, ds(q, 1), :], MEAN[:, ds(q, 1)],
                                      RST2[:, ds(q, 1)], ALU.subtract, ALU.mult).then_inc(A["xh"], 1)

            def difference(c):
                dve.wait_ge(A["xt"], c + 1)
                need(dve, A["v1"], 2 * c)
                dve.tensor_tensor(XTA[:, 2], XTA[:, 0], XTA[:, 1], ALU.subtract).then_inc(A["xd"], 1)

            def attend(c, h, between=None):
                s = 2 * c + h
                dve.wait_ge(A["kds"], s + 1)
                for b, sq in enumerate((A["q0"], A["q1"])):
                    dve.wait_ge(sq, s + 1)
                    dve.tensor_tensor(PRD[:, b], BK[1 + b][:, :], KDF, ALU.mult).then_inc(A["prod"], 1)
                for b in range(2):
                    dve.wait_ge(A["prod"], 2 * s + b + 1)
                    st(dve.tensor_reduce(SCO[:, b * 8:(b + 1) * 8], PRD[:, b].rearrange("p (h n) -> p h n", h=8),
                                         AX.X, ALU.add))
                st.after()
                scale = 1.0 / 16.0
                st(dve.tensor_scalar(SMX, SCO, scale, 0.0, ALU.mult, ALU.max))
                st.after()
                st(dve.scalar_tensor_tensor(SEX[:, 0], SCO, scale, SMX, ALU.mult, ALU.subtract))
                dve.tensor_scalar(SEX[:, 1], SMX, -1.0, None, ALU.mult).then_inc(A["sin"], 1)
                if between is not None:
                    difference(between)
                dve.wait_ge(A["sexp"], s + 1)
                st(dve.tensor_tensor(SMX, SEX[:, 0], SEX[:, 1], ALU.add))
                st.after()
                st(dve.reciprocal(SMX, SMX))
                st.after()
                st(dve.tensor_tensor(SPR, SEX[:, 0], SMX, ALU.mult))
                dve.wait_ge(A["v1s"], s + 1)
                dve.wait_ge(A["vds"], s + 1)
                st.after()
                for b in range(2):
                    need(dve, A["otr"], 2 * s + b - 1)
                    st(dve.tensor_tensor(OA[:, b].rearrange("p (h n) -> p h n", h=8),
                                         VDF.rearrange("p (h n) -> p h n", h=8),
                                         spread(SPR[:, b * 8:(b + 1) * 8], AD), ALU.mult))
                    st.after()
                    dve.tensor_tensor(OA[:, b], OA[:, b], V1S, ALU.add).then_inc(A["out"], 1)

            def residual(c):
                for b in range(2):
                    q = 2 * c + b
                    st(dve.tensor_scalar(XR[:, b], Xv[:, ds(q, 1), :], MEAN[:, ds(q, 1)], RSTD[:, ds(q, 1)],
                                         ALU.subtract, ALU.mult))
                    st.after()
                    st(dve.tensor_tensor(XR[:, b], XR[:, b], Xv[:, ds(q, 1), :], ALU.add))
                    dve.wait_ge(A["po"], 2 * c + 2)
                    st.after()
                    st(dve.tensor_tensor(Xv[:, ds(q, 1), :], XR[:, b], BK[6][:, b * D:(b + 1) * D], ALU.add))
                    st.after()
                    dve.bn_stats(STv[:, ds(q, 1), :], Xv[:, ds(q, 1), :]).then_inc(A["x3"], 1)

            def att(c, first=False, last=False):
                if not last:
                    normed(c + 1)
                attend(c, 0)
                if not first:
                    residual(c - 1)
                attend(c, 1, None if last else c + 1)
                st.clear()
            normed(0)
            difference(0)
            att(0, first=True)
            with dve.Fori(1, NC - 1) as c:
                att(c)
            att(NC - 1, last=True)
            residual(NC - 1)
            dve.wait_ge(A["x3"], NQ)
            rstd_steps(dve, st, root_ready, root_done, 6, MEAN, RSTD, VARE)
            st.clear()
            barrier(dve)
            norm_dve(dve, norm_f[1])
            dve.wait_ge(norm_f[1].pj, NQ)
            route_dve(dve, st, 1)
            barrier(dve)
            dve.wait_ge(loaded_w2, 96)
            experts("dve", dve, st, 1, out)
            barrier(dve)

        @block.scalar
        def _(act):
            act_root(act, 1)
            norm_act(act, norm_a)
            act.wait_ge(M["act_in"], 1)
            act.activation(SP_[1], SP_[1], ACT.Exp, scale=-1.0)
            act.activation(ALG, ALG, ACT.Exp).then_inc(M["act_out"], 1)
            act.wait_ge(M["act_in"], 3)
            act.activation(PEC, PEC, ACT.Exp)
            act.activation(PET, PET, ACT.Exp)
            act.activation(PWD, PWD, ACT.Exp).then_inc(M["act_out"], 1)
            barrier(act)
            st = Steps(act, act_step)

            def pre(n):
                if not (isinstance(n, int) and n == 0):
                    act.wait_ge(M["tapped"], n)
                    st(act.activation(XB[:, :, :, 0:3], XB[:, :, :, P:P + 3], ACT.Copy))
                need(act, M["xc"], n)
                for j in range(3):
                    act.wait_ge(M["xbc"], 3 * n + j + 1)
                    for m in (2 * j, 2 * j + 1):
                        act.activation(ACC[:, m], BK[j][:, (m % 2) * 256:(m % 2) * 256 + 256].rearrange(
                            "p (b t) -> p b t", b=2), ACT.Identity, bias=CB[:, m:m + 1], scale=CW[:, m, 3:4])
                    if j == 0 and not (isinstance(n, int) and n == 0):
                        st.after()
                    act.activation(XB[:, 2 * j:2 * j + 2, :, 3:3 + P],
                                   BK[j][:, :].rearrange("p (m b t) -> p m b t", m=2, b=2), ACT.Copy
                                   ).then_inc(M["taken"], 1)

            def decays(c, b):
                q = 2 * c + b
                act.wait_ge(M["rg"], q + 1)
                need(act, M["y1"], q - 1)
                for h in range(H):
                    i = act.activation(LM[:, b, h], BK[3 + h // 4][:, (h % 4) * P:(h % 4 + 1) * P], ACT.Exp,
                                       bias=PNC[:, ds(q * 8 + h, 1)])
                i.then_inc(M["decay"], 1)

            def yt(c, b):
                q = 2 * c + b
                act.wait_ge(M["ytr"], q + 1)
                need(act, M["po"], q - 1)
                act.activation(YT[:, b], BK[5][:, :].rearrange("p (k t) -> p k t", k=4), ACT.Copy
                               ).then_inc(M["yt"], 1)

            def square(c, b):
                q = 2 * c + b
                act.wait_ge(M["y"], q + 1)
                act.activation(ZS[:, b], Y[:, b], ACT.Square, accum_out=SS[:, ds(q, 1)]).then_inc(M["square"], 1)

            def po_out(c, b):
                q = 2 * c + b
                act.wait_ge(M["po"], q + 1)
                act.activation(KEEPv[:, ds(q, 1), :], BK[6][:, 256:512], ACT.Copy).then_inc(M["po_out"], 1)

            def zs(c, b):
                q = 2 * c + b
                act.wait_ge(M["z"], q + 1)
                need(act, M["y"], q - 1)
                need(act, M["square"], q - 1)
                act.activation(ZS[:, b], BK[7][:, :], ACT.Silu).then_inc(M["zs"], 1)

            def xs(c, b):
                q = 2 * c + b
                act.wait_ge(M["xtr"], q + 1)
                need(act, M["st"], q - 1)
                need(act, M["xdt"], q - 1)
                need(act, M["dx"], q - 1)
                act.activation(BT[:, b], BK[6][:, 0:P], ACT.Copy)
                act.activation(XS[:, b], BK[5][:, :], ACT.Copy).then_inc(M["xs"], 1)

            def xc(n):
                act.wait_ge(M["tapped"], n + 1)
                need(act, M["y2"], 2 * n)
                act.activation(XC, ACC, ACT.Silu).then_inc(M["xc"], 1)

            def mixer(c, n):
                if n is not None:
                    pre(n)
                if c is not None:
                    if not (isinstance(c, int) and c == 0):
                        po_out(c - 1, 1)
                    xs(c, 0)
                    zs(c, 0)
                    xs(c, 1)
                    decays(c, 1)
                    zs(c, 1)
                    yt(c, 0)
                    square(c, 0)
                if n is not None:
                    decays(n, 0)
                if c is not None:
                    po_out(c, 0)
                    yt(c, 1)
                    square(c, 1)
                if n is not None:
                    xc(n)
                st.clear()
            mixer(None, 0)
            mixer(0, 1)
            with act.Fori(1, NC - 1) as c:
                mixer(c, c + 1)
            mixer(NC - 1, None)
            po_out(NC - 1, 1)
            barrier(act)
            act_root(act, 2)
            act_root(act, 3)
            barrier(act)
            norm_act(act, norm_f[0])
            route_act(act, 0)
            barrier(act)
            experts("act", act, st, 0, acc_dram)
            barrier(act)
            act_root(act, 4)
            act_root(act, 5)
            act.wait_ge(A["w"], 96)

            def heads(c):
                act.wait_ge(A["tr"], c + 1)
                need(act, A["v1"], 2 * c)
                need(act, A["xd"], c)
                for k in range(KD):
                    i = act.activation(XTA[:, 0:2, k, :],
                                       BK[0][:, :].rearrange("p (b k t) -> p b k t", b=2, k=KD)[:, :, k, :],
                                       ACT.Identity, bias=LNWB[:, 1, k:k + 1], scale=LNWB[:, 0, k:k + 1])
                i.then_inc(A["xt"], 1)

            def copies(c, h):
                s = 2 * c + h
                act.wait_ge(A["kd"], s + 1)
                need(act, A["prod"], 2 * s)
                act.activation(KDF, BK[3][:, :], ACT.Copy).then_inc(A["kds"], 1)
                act.wait_ge(A["vd"], s + 1)
                need(act, A["out"], 2 * s)
                act.activation(VDF, BK[4][:, :], ACT.Copy).then_inc(A["vds"], 1)
                act.wait_ge(A["v1"], s + 1)
                act.activation(V1S, BK[5][:, :], ACT.Copy).then_inc(A["v1s"], 1)

            def exps(c, h):
                s = 2 * c + h
                act.wait_ge(A["sin"], s + 1)
                act.activation(SEX, SEX, ACT.Exp).then_inc(A["sexp"], 1)

            def transposed(c, h):
                s = 2 * c + h
                for b in range(2):
                    act.wait_ge(A["otr"], 2 * s + b + 1)
                    if h == 0:
                        need(act, A["po"], 2 * c)
                    act.activation(OT[:, b, 4 * h:4 * h + 4, :], BK[7 - 7 * b][:, :].rearrange("p (k t) -> p k t", k=4),
                                   ACT.Copy).then_inc(A["ot"], 1)

            def att(c, first=False, last=False):
                copies(c, 0)
                if not first:
                    transposed(c - 1, 1)
                exps(c, 0)
                copies(c, 1)
                if not last:
                    heads(c + 1)
                transposed(c, 0)
                exps(c, 1)
            heads(0)
            att(0, first=True)
            with act.Fori(1, NC - 1) as c:
                att(c)
            att(NC - 1, last=True)
            transposed(NC - 1, 1)
            act_root(act, 6)
            barrier(act)
            norm_act(act, norm_f[1])
            route_act(act, 1)
            barrier(act)
            experts("act", act, st, 1, out)
            barrier(act)

        @block.gpsimd
        def _(pool):
            st = Steps(pool, pool_step)
            st(pool.memset(DX, 0.0))
            st.after()
            for dst in (xn_dram, acc_dram, out):
                pool.dma_start(dst[NTOK:NTOK + P, :], DX[:, 0, 0:D]).then_inc(zeroed, 16)
            pool.wait_ge(zeroed, 48)
            st.clear()
            with pool.Fori(0, NC) as c:
                for b in range(2):
                    pool.wait_ge(norm_a.xt, 2 * c + b + 1)
                    pool.tensor_copy(KEEPv[:, ds(2 * c + b, 1), :], XT0[:, b].rearrange("p k t -> p (k t)")
                                     ).then_inc(norm_a.kept, 1)
            barrier(pool)

            def prepare(n):
                need(pool, M["rg"], 2 * n)
                pool.tensor_copy(ANOW.rearrange("p b h -> p (b h)"), PA[:, ds(16 * n, 16)]).then_inc(M["a_now"], 1)
                need(pool, M["z"], 2 * n)
                pool.tensor_copy(XTS, KEEPv[:, ds(2 * n, 2), :].rearrange("p b (k t) -> p k b t", k=KD)
                                 ).then_inc(M["xts"], 1)

            def state(c, b):
                q = 2 * c + b
                pool.wait_ge(M["y2"], q + 1)
                s3 = SST[:, b].rearrange("p (h n) -> p h n", h=H)
                pool.tensor_tensor(s3, s3, spread(PET[:, ds(q * 8, 8)], HD), ALU.mult).then_inc(M["scaled"], 1)

            def inputs(c, b):
                q = 2 * c + b
                x3 = XS[:, b].rearrange("p (h n) -> p h n", h=H)
                pool.wait_ge(M["xs"], q + 1)
                need(pool, M["st"], q - 1)
                pool.tensor_tensor(XDEC[:, b].rearrange("p (h n) -> p h n", h=H), x3,
                                   spread(PWD[:, ds(q * 8, 8)], HD), ALU.mult).then_inc(M["xdec"], 1)
                need(pool, M["y"], q - 1)
                pool.tensor_tensor(DX[:, b].rearrange("p (h n) -> p h n", h=H), x3, spread(DSK, HD), ALU.mult
                                   ).then_inc(M["dx"], 1)

            def mixer(c, n):
                if c is not None:
                    for b in range(2):
                        inputs(c, b)
                        state(c, b)
                if n is not None:
                    prepare(n)
            mixer(None, 0)
            mixer(0, 1)
            with pool.Fori(1, NC - 1) as c:
                mixer(c, c + 1)
            mixer(NC - 1, None)
            barrier(pool)
            barrier(pool)
            barrier(pool)
            experts("pool", pool, st, 0, acc_dram)
            barrier(pool)
            barrier(pool)
            barrier(pool)
            experts("pool", pool, st, 1, out)
            barrier(pool)

        @block.tensor
        def _(pe):
            pe.wait_ge(loaded_small, 16 * 12)
            norm_pe(pe, norm_a, BK[2])
            pe.wait_ge(M["act_in"], 2)
            pe.matmul(BK[3][:, 0:256], CST[:, C_UP:C_UP + P], PA, start=True, stop=True)
            pe.matmul(BK[3][:, 256:512], CST[:, C_ONE:C_ONE + P], PA, start=True, stop=True).then_inc(M["cum"], 1)
            barrier(pe)

            def xbc(n):
                need(pe, M["taken"], 3 * n)
                for m in range(MC):
                    for k in range(KD):
                        i = pe.matmul(BK[m // 2][:, (m % 2) * 256:(m % 2) * 256 + 256],
                                      WIN[:, k, DI + m * P:DI + (m + 1) * P],
                                      KEEPv[:, ds(2 * n, 2), k * P:(k + 1) * P], start=k == 0, stop=k == KD - 1)
                    if m % 2:
                        i.then_inc(M["xbc"], 1)

            def z(c, b):
                q = 2 * c + b
                pe.wait_ge(M["xts"], c + 1)
                need(pe, M["zs"], q)
                for k in range(KD):
                    i = pe.matmul(BK[7][:, :], XTS[:, k, b, :], WIN[:, k, 0:DI], start=k == 0, stop=k == KD - 1)
                i.then_inc(M["z"], 1)

            def x_back(c, b):
                pe.wait_ge(M["xc"], c + 1)
                if b == 0:
                    need(pe, M["yt"], 2 * c)
                    need(pe, M["po_out"], 2 * c)
                else:
                    pe.wait_ge(M["xs"], 2 * c + 1)
                for m in range(4):
                    pe.transpose(BK[5][:, m * P:(m + 1) * P], XC[:, m, b, :], ident)
                i = pe.transpose(BK[6][:, 0:P], XC[:, 4, b, :], ident)
                if b:
                    i = pe.matmul(BK[6][:, P:2 * P], XC[:, 4, b, :], XC[:, 5, b, :], start=True, stop=True)
                i.then_inc(M["xtr"], 1)

            def bc(c):
                pe.matmul(BK[1][:, 0:P], XC[:, 4, 0, :], XC[:, 5, 0, :], start=True, stop=True).then_inc(M["bc"], 1)

            def decay(c, b):
                q = 2 * c + b
                pe.wait_ge(M["a_now"], c + 1)
                need(pe, M["decay"], q)
                for g in range(2):
                    pe.matmul(BK[3 + g][:, :].rearrange("p (h i) -> p h i", h=4), identb,
                              maskb.unsqueeze(1).broadcast_to([P, 4, P]), start=True, stop=False)
                    for h in range(4):
                        i = pe.matmul(BK[3 + g][:, h * P:(h + 1) * P], ANOW[:, b, 4 * g + h:4 * g + h + 1].broadcast_to([P, P]),
                                      CST[:, C_UP:C_UP + P], start=False, stop=h == 3)
                i.then_inc(M["rg"], 1)

            def from_state(c, b):
                q = 2 * c + b
                need(pe, M["st_read"], q - 1)
                need(pe, M["y2_read"], q)
                pe.matmul(BK[0][:, :], XC[:, 5, b, :], SST[:, b], start=True, stop=True).then_inc(M["y2"], 1)

            def increment(c, b):
                q = 2 * c + b
                need(pe, M["st_read"], q)
                pe.wait_ge(M["xdec"], q + 1)
                pe.matmul(BK[2][:, :], BT[:, b], XDEC[:, b], start=True, stop=True).then_inc(M["st"], 1)

            def within(c, b):
                q = 2 * c + b
                need(pe, M["y1_read"], q)
                pe.wait_ge(M["masked"], q + 1)
                pe.wait_ge(M["xdt"], q + 1)
                for h in range(H):
                    i = pe.matmul(BK[1][:, h * HD:(h + 1) * HD], LM[:, b, h, :], XDT[:, b, h * HD:(h + 1) * HD],
                                  start=True, stop=True)
                i.then_inc(M["y1"], 1)

            def y_back(c, b):
                q = 2 * c + b
                if b == 0:
                    pe.wait_ge(M["xs"], 2 * c + 2)
                else:
                    pe.wait_ge(M["yt"], 2 * c + 1)
                pe.wait_ge(M["y"], q + 1)
                for k in range(4):
                    i = pe.transpose(BK[5][:, k * P:(k + 1) * P], Y[:, b, k * P:(k + 1) * P], ident)
                i.then_inc(M["ytr"], 1)

            def mix_out(c, b):
                q = 2 * c + b
                pe.wait_ge(M["yt"], q + 1)
                need(pe, M["po_out"], q)
                for k in range(4):
                    i = pe.matmul(BK[6][:, 256:512], YT[:, b, k, :], WOUT[:, k, :], start=k == 0, stop=k == 3)
                i.then_inc(M["po"], 1)

            def mixer(c, n):
                if n is not None:
                    xbc(n)
                if c is not None:
                    if not (isinstance(c, int) and c == 0):
                        mix_out(c - 1, 1)
                    decay(c, 1)
                    z(c, 0)
                    x_back(c, 0)
                    if n is not None:
                        pe.wait_ge(M["taken"], 3 * n + 3)
                    bc(c)
                    from_state(c, 0)
                    x_back(c, 1)
                    increment(c, 0)
                    z(c, 1)
                    within(c, 0)
                    from_state(c, 1)
                    increment(c, 1)
                    within(c, 1)
                    y_back(c, 0)
                if n is not None:
                    decay(n, 0)
                if c is not None:
                    mix_out(c, 0)
                    y_back(c, 1)
            mixer(None, 0)
            mixer(0, 1)
            with pe.Fori(1, NC - 1) as c:
                mixer(c, c + 1)
            mixer(NC - 1, None)
            mix_out(NC - 1, 1)
            barrier(pe)
            barrier(pe)
            norm_pe(pe, norm_f[0], BK[2])
            route_pe(pe, 0)
            barrier(pe)
            pe.wait_ge(loaded_w1, 16 * E)
            pe.wait_ge(loaded_w2, 48)
            st = Steps(pe, pe_step)
            experts("pe", pe, st, 0, acc_dram)
            barrier(pe)
            pe.wait_ge(A["w"], 96)

            def heads(c):
                pe.wait_ge(A["xh"], 2 * c + 2)
                need(pe, A["xt"], c)
                need(pe, A["ot"], 4 * c - 4)
                for b in range(2):
                    for k in range(KD):
                        i = pe.transpose(BK[0][:, (2 * b + k) * P:(2 * b + k + 1) * P], XH[:, b, k * P:(k + 1) * P], ident)
                i.then_inc(A["tr"], 1)

            def project(c, h):
                s = 2 * c + h
                pe.wait_ge(A["xt"], c + 1)
                for bank, lhs, w, done, free, n in ((1, 0, 0, "q0", "prod", 2 * s), (2, 1, 0, "q1", "prod", 2 * s),
                                                    (3, 2, 1, "kd", "kds", s), (4, 2, 2, "vd", "vds", s),
                                                    (5, 1, 2, "v1", "v1s", s)):
                    need(pe, A[free], n)
                    if done == "kd":
                        pe.wait_ge(A["xd"], c + 1)
                    for k in range(KD):
                        i = pe.matmul(BK[bank][:, :], XTA[:, lhs, k, :], WQKV[:, w, k, h * HF:(h + 1) * HF],
                                      start=k == 0, stop=k == KD - 1)
                    i.then_inc(A[done], 1)

            def transposed(c, h, last=False):
                s = 2 * c + h
                for b in range(2):
                    need(pe, A["ot"], 2 * s + b - 1)
                    if b == 1:
                        pe.wait_ge(A["xt"], c + 1 if h or last else c + 2)
                    pe.wait_ge(A["out"], 2 * s + b + 1)
                    for k in range(4):
                        i = pe.transpose(BK[7 - 7 * b][:, k * P:(k + 1) * P], OA[:, b, k * P:(k + 1) * P], ident)
                    i.then_inc(A["otr"], 1)

            def att_out(c):
                need(pe, A["x3"], 2 * c)
                for b in range(2):
                    pe.wait_ge(A["ot"], 4 * c + 3 + b)
                    for k in range(KA):
                        i = pe.matmul(BK[6][:, b * D:(b + 1) * D], OT[:, b, k, :], WAO[:, k, :],
                                      start=k == 0, stop=k == KA - 1)
                    i.then_inc(A["po"], 1)

            def att(c, first=False, last=False):
                project(c, 0)
                if not first:
                    transposed(c - 1, 1)
                    att_out(c - 1)
                project(c, 1)
                if not last:
                    heads(c + 1)
                transposed(c, 0, last)
            heads(0)
            att(0, first=True)
            with pe.Fori(1, NC - 1) as c:
                att(c)
            att(NC - 1, last=True)
            transposed(NC - 1, 1)
            att_out(NC - 1)
            barrier(pe)
            norm_pe(pe, norm_f[1], BK[2])
            route_pe(pe, 1)
            barrier(pe)
            pe.wait_ge(loaded_w2, 96)
            experts("pe", pe, st, 1, out)
            barrier(pe)


def constants():
    import numpy as np
    c = np.zeros((P, C_N), np.float32)
    i, j = np.arange(P)[:, None], np.arange(P)[None, :]
    c[:, C_ID:C_ID + P] = i == j
    c[:, C_UP:C_UP + P] = i <= j
    c[:, C_ONE:C_ONE + P] = 1
    c[:, C_US:C_US + P] = i < j
    c[:, C_IOTA:C_IOTA + P] = j
    c[:, C_MASK:C_MASK + P] = np.where(j < i, MASKED, 0)
    c[:, C_IT:C_IT + ST] = np.arange(ST)
    q = np.arange(NQ)[None, :]
    c[:, C_TOK:C_TOK + NQ] = (q % 2) * L + (q // 2) * P + i - NTOK
    c[:, C_K128:C_K128 + NQ] = P * q
    c[:, C_REV:C_REV + E] = E - np.arange(E)
    c[:, C_PAD] = NTOK + np.arange(P)
    return c


def kernel(**inputs):
    import numpy as _np
    import concourse.bacc as _bacc
    from concourse import mybir as _mybir
    from concourse.bass_utils import run_bass_kernel_spmd as _run

    a = {k.split("_", 1)[1]: _np.asarray(v) for k, v in inputs.items()}
    t = _np.ascontiguousarray
    arrays = {
        "u": a["attn_a_u"].reshape(NTOK, D),
        "w_in": t(a["attn_a_W_in"].T),
        "conv_w": a["attn_a_conv_w"], "conv_b": a["attn_a_conv_b"], "dt_bias": a["attn_a_dt_bias"],
        "a_log": a["attn_a_A_log"], "d_skip": a["attn_a_D"], "norm_w": a["attn_a_norm_w"],
        "w_mix_out": t(a["attn_a_W_out"].T),
        "w_qkv": t(a["attn_b_w_qkv"].reshape(AH, 3, AD, D).transpose(1, 3, 0, 2)).reshape(3, D, AI),
        "w_att_out": t(a["attn_b_w_out"].T), "ln_w": a["attn_b_ln_w"], "ln_b": a["attn_b_ln_b"],
        "w_route": t(a["ffn_Wr"].T), "b_route": a["ffn_br"],
        "w1": a["ffn_Wl1"], "b1": a["ffn_bl1"], "w2": a["ffn_Wl2"], "b2": a["ffn_bl2"],
        "bias_n": a["ffn_biases_N"], "consts": constants(),
    }
    nc = _bacc.Bacc("TRN2", target_bir_lowering=False, num_devices=1)
    arrays = {f"in_{k}": t(v) for k, v in arrays.items()}
    args = [nc.dram_tensor(k, v.shape, _mybir.dt.from_np(v.dtype), kind="ExternalInput").ap() for k, v in arrays.items()]
    args.append(nc.dram_tensor("out_0", (NTOK + P, D), _mybir.dt.float32, kind="ExternalOutput").ap())
    hybrid_block(nc, *args)
    r = _run(nc, [arrays], core_ids=[0])
    return r.results[0]["out_0"][:NTOK].reshape(B, L, D)
```

```python
import concourse.bass as bass
from concourse import mybir
from contextlib import ExitStack

B, L, D = 2, 2048, 256
P = 128
NC = L // P
NQ = B * NC
KD = D // P
H, HD = 8, 64
DI = H * HD
NS = 128
CONV = DI + 2 * NS
MC = CONV // P
TAPS = 4
E, HF = 8, 512
TOPK = 2
KF = HF // P
SLOTS_T = B * L * TOPK // P + E - 1
ST = SLOTS_T + 1
AH, AD = 16, 64
AI = AH * AD
KA = AI // P
EPS = 1e-5
NTOK = B * L
BIG = 3.0e38
MASKED = -1.0e30

C_ID, C_UP, C_ONE, C_US, C_IOTA, C_MASK = 0, 128, 256, 384, 512, 640
C_IT = 768
C_TOK = C_IT + ST
C_K128 = C_TOK + NQ
C_REV = C_K128 + NQ
C_PAD = C_REV + E
C_N = C_PAD + 1


def hybrid_block(nc: bass.Bass, u, w_in, conv_w, conv_b, dt_bias, a_log, d_skip, norm_w, w_mix_out,
                 w_qkv, w_att_out, ln_w, ln_b, w_route, b_route, w1, b1, w2, b2, bias_n, consts, out):
    f32, bf16, i32, f32r = mybir.dt.float32, mybir.dt.bfloat16, mybir.dt.int32, mybir.dt.float32r
    ALU = mybir.AluOpType
    ACT = mybir.ActivationFunctionType
    AX = mybir.AxisListType
    ds = bass.ds

    ctx = ExitStack()
    with ctx:
        place = {}

        def sb(name, cols, dt=f32):
            t = ctx.enter_context(nc.sbuf_tensor(name, [P, cols], dt))
            place[name] = nc.sbuf_base - 4 * cols
            return t

        def rounded(name, inside, col, cols):
            return nc.alloc_sbuf_tensor_at(name, [P, cols], f32r, offset=place[inside] + 4 * col)[:, :]

        def sem(name):
            return ctx.enter_context(nc.semaphore(name))

        X = sb("X", NQ * D)
        KEEP = sb("KEEP", NQ * D)
        W1 = sb("W1", E * KD * 2 * HF)
        W1v = W1[:, :].rearrange("p (e k n) -> p e k n", e=E, k=KD)
        CST = sb("CST", C_N)
        WR = sb("WR", KD * E)
        STATS = sb("STATS", NQ * 6)
        MEAN, RSTD, VARE, RST2 = (sb(n, NQ) for n in ("MEAN", "RSTD", "VARE", "RST2"))
        TMP = [sb(f"TMP{i}", NQ) for i in range(3)]
        ROUTE_B = sb("ROUTE_B", 2 * E)
        GATE = sb("GATE", ST)
        IDX = sb("IDX", ST, i32)
        EXPERT = sb("EXPERT", ST, i32)
        IDC = sb("IDC", 4, i32)
        PHASE = sb("PHASE", 18848)

        Xv = X[:, :].rearrange("p (q d) -> p q d", d=D)
        KEEPv = KEEP[:, :].rearrange("p (q d) -> p q d", d=D)
        STv = STATS[:, :].rearrange("p (q s) -> p q s", s=6)
        ident = CST[:, C_ID:C_ID + P]

        def carve(base):
            at = [0]

            def take(cols):
                at[0] += cols
                assert at[0] <= base.shape[1], at[0]
                return base[:, at[0] - cols:at[0]]
            take.at = at
            return take

        BK = [ctx.enter_context(nc.psum_tensor(f"BK{i}", [P, 512], f32)) for i in range(8)]

        def spread(ap, n):
            return ap.unsqueeze(2).broadcast_to([ap.shape[0], ap.shape[1], n])

        def repeat(ap, n):
            return ap.unsqueeze(1).broadcast_to([ap.shape[0], n, ap.shape[1]])

        def need(eng, s, value):
            if not isinstance(value, int) or value > 0:
                eng.wait_ge(s, value)

        class Steps:

            def __init__(self, eng, s):
                self.eng, self.s, self.n = eng, s, 0

            def __call__(self, instruction):
                instruction.then_inc(self.s, 1)
                self.n += 1
                return self.n

            def after(self, n=None):
                self.eng.wait_ge(self.s, self.n if n is None else n)

            def clear(self):
                if self.n:
                    self.after()
                    self.eng.sem_clear(self.s)
                    self.n = 0

        bar = sem("phase_done")
        bars = {}

        def barrier(eng):
            n = bars[id(eng)] = bars.get(id(eng), 0) + 1
            eng.drain().then_inc(bar, 1)
            eng.wait_ge(bar, 5 * n)

        dve_step, act_step, pool_step, pe_step = sem("dve_step"), sem("act_step"), sem("pool_step"), sem("pe_step")
        loaded_small, loaded_w1, loaded_b = sem("loaded_small"), sem("loaded_w1"), sem("loaded_b")
        loaded_w2 = [sem(f"loaded_w2_{f}") for f in range(2)]
        loaded_x, reloaded_x = ([sem(f"{n}{b}") for b in range(2)] for n in ("loaded_x", "reloaded_x"))
        stored_x, zeroed = [sem(f"stored_x{b}") for b in range(2)], sem("zeroed")

        xn_dram = nc.dram_tensor("xn_dram", [NTOK + P, D], f32, kind="Internal").ap()
        acc_dram = nc.dram_tensor("acc_dram", [NTOK + P, D], f32, kind="Internal").ap()

        take = carve(PHASE)
        NIN = DI + CONV + H
        split_rows = lambda ap, k: ap.rearrange("p (k n) -> p k n", k=k)
        WIN = take(KD * NIN).rearrange("p (k n) -> p k n", k=KD)
        WOUT = take(4 * D).rearrange("p (k n) -> p k n", k=4)
        WINLO = split_rows(rounded("MIX_IN_LO", "PHASE", 0, KD * NIN), KD)
        WOUTLO = split_rows(rounded("MIX_OUT_LO", "PHASE", KD * NIN, 4 * D), 4)
        XLO = split_rows(rounded("MIX_X_LO", "W1", 0, NQ * D), NQ)
        XHI = split_rows(rounded("MIX_X_HI", "KEEP", 0, NQ * D), NQ)
        WINHI = split_rows(rounded("MIX_IN_HI", "W1", NQ * D, KD * NIN), KD)
        WOUTHI = split_rows(rounded("MIX_OUT_HI", "W1", NQ * D + KD * NIN, 4 * D), 4)
        at_w1 = NQ * D + KD * NIN + 4 * D
        XTSHI, XTSLO = (rounded(n, where, col, 2 * D).rearrange("p (k b t) -> p k b t", k=KD, b=2) for n, where, col
                        in (("MIX_XTS_HI", "PHASE", take.at[0]), ("MIX_XTS_LO", "W1", at_w1)))
        take(2 * D)
        YTHI, YTLO = (rounded(n, where, col, 2 * DI).rearrange("p (b n) -> p b n", b=2) for n, where, col
                      in (("MIX_YT_HI", "PHASE", take.at[0]), ("MIX_YT_LO", "W1", at_w1 + 2 * D)))
        YT0 = take(2 * 4 * P)
        CW = take(MC * TAPS).rearrange("p (m s) -> p m s", m=MC)
        CB = take(MC)
        DTB, ALG, DSK = take(H), take(H), take(H)
        NW = take(4)
        PA, PNC, PEC, PDT, PWD, PET = (take(NQ * H) for _ in range(6))
        XB = take(MC * 2 * 131).rearrange("p (m b t) -> p m b t", m=MC, b=2)
        ACC = take(MC * 2 * P).rearrange("p (m b t) -> p m b t", m=MC, b=2)
        XC = take(MC * 2 * P).rearrange("p (m b t) -> p m b t", m=MC, b=2)
        XS, XDT, XDEC, DX, ZS, SST = (take(2 * DI).rearrange("p (b n) -> p b n", b=2) for _ in range(6))
        BT = take(2 * NS).rearrange("p (b n) -> p b n", b=2)
        Y = take(2 * DI).rearrange("p (b n) -> p b n", b=2)
        LAST_EXPERT = W1[:, (E - 1) * KD * 2 * HF:]
        LM = LAST_EXPERT.rearrange("p (b h i) -> p b h i", b=2, h=H)
        SS = take(NQ)
        ANOW = take(2 * H).rearrange("p (b h) -> p b h", b=2)
        MB = CST[:, C_MASK:C_MASK + P].bitcast(bf16)
        identb, maskb = MB[:, 0:P], MB[:, P:2 * P]
        SP_ = [ACC.rearrange("p m b t -> p (m b t)")[:, i * 256:(i + 1) * 256] for i in range(6)]
        XNB0 = LAST_EXPERT.rearrange("p (s n) -> p s n", s=4)
        XT0 = XDT

        take = carve(PHASE)
        W2 = take(E * KF * D)
        W2HI, W2LO = rounded("W2_HI", "X", 0, E * KF * D), rounded("W2_LO", "PHASE", 0, E * KF * D)
        W2HIv, W2LOv = (w.rearrange("p (e k n) -> p e k n", e=E, k=KF) for w in (W2HI, W2LO))
        B1 = take(E * 2 * HF).rearrange("p (e n) -> p e n", e=E)
        B2 = take(E * D).rearrange("p (e n) -> p e n", e=E)
        ftake = carve(KEEP)
        XG, YO = (ftake(2 * D).rearrange("p (b n) -> p b n", b=2) for _ in range(2))
        XTF = ftake(2 * D).rearrange("p (b k t) -> p b k t", b=2, k=KD)
        HA, HB = (ftake(2 * HF).rearrange("p (b n) -> p b n", b=2) for _ in range(2))
        HTH, HTL = (rounded(n, "KEEP", 6 * D + (4 + 2 * i) * HF, 2 * HF).rearrange("p (b n) -> p b n", b=2)
                    for i, n in enumerate(("HIDDEN_HI", "HIDDEN_LO")))

        def split_matmul(pe, out, hi, lo, w_hi, w_lo, start, stop):
            pe.matmul(out, hi, w_hi, start=start, stop=False)
            pe.matmul(out, hi, w_lo, start=False, stop=False)
            return pe.matmul(out, lo, w_hi, start=False, stop=stop)

        def rstd_steps(dve, st, n, q=slice(0, NQ)):
            me, m2e, mo, m2o = (STv[:, q, j] for j in (1, 2, 4, 5))
            t0, t1, t2 = (t[:, q] for t in TMP)
            a = st(dve.tensor_tensor(t0, me, mo, ALU.add))
            b = st(dve.tensor_tensor(t1, me, mo, ALU.subtract))
            c = st(dve.tensor_tensor(t2, m2e, m2o, ALU.add))
            st.after(a)
            st(dve.tensor_scalar(MEAN[:, q], t0, 0.5, None, ALU.mult))
            st.after()
            d = st(dve.tensor_tensor(t0, t1, t1, ALU.mult))
            st(dve.tensor_scalar(t2, t2, 1.0 / D, EPS, ALU.mult, ALU.add))
            st.after()
            st(dve.scalar_tensor_tensor(VARE[:, q], t0, 0.25, t2, ALU.mult, ALU.add))
            st.after()
            root(dve, st, n, VARE, RSTD, q)

        def root(dve, st, n, var, result, q=slice(0, NQ)):
            v, r, t = var[:, q], result[:, q], TMP[2][:, q]
            dve.tensor_copy(TMP[0][:, q], v).then_inc(root_ready, 1)
            dve.wait_ge(root_done, n)
            st(dve.reciprocal(r, TMP[1][:, q]))
            st.after()
            st(dve.tensor_tensor(t, r, r, ALU.mult))
            st.after()
            st(dve.tensor_tensor(t, t, v, ALU.mult))
            st.after()
            st(dve.tensor_scalar(t, t, -0.5, 1.5, ALU.mult, ALU.add))
            st.after()
            st(dve.tensor_tensor(r, r, t, ALU.mult))
            st.after()

        root_ready, root_done = sem("root_ready"), sem("root_done")

        def load_x(sp, src, done):
            for b in range(2):
                sp.dma_start(Xv.rearrange("p (c b) d -> p c b d", b=2)[:, :, b, :],
                             src[b * L:(b + 1) * L, :].rearrange("(c p) d -> p c d", p=P)).then_inc(done[b], 16)

        def stats(dve, loaded):
            for b in range(2):
                dve.wait_ge(loaded[b], 16)
                with dve.Fori(0, NC // 4) as i:
                    for j in range(4):
                        q = 8 * i + 2 * j + b
                        dve.bn_stats(STv[:, ds(q, 1), :], Xv[:, ds(q, 1), :])
            dve.drain()

        def act_root(act, n, q=slice(0, NQ)):
            act.wait_ge(root_ready, n)
            act.activation(TMP[1][:, q], TMP[0][:, q], ACT.Sqrt).then_inc(root_done, 1)

        class Norm:

            def __init__(self, tag, xnb, xt, w8, mean, rstd, keep, store):
                self.xn, self.tr, self.xt, self.pj = (
                    sem(f"{n}_{tag}") for n in ("normed", "transposed", "xt_ready", "projected"))
                if keep:
                    self.kept = sem(f"kept_{tag}")
                self.st = [sem(f"normed_stored{s}_{tag}") for s in range(4 if store else 0)]
                self.xnb, self.xT, self.w8, self.mean, self.rstd = xnb, xt, w8, mean, rstd
                self.keep, self.store = keep, store

        def chunks(eng, body, between=()):
            apart = max(1, len(between))
            for i in range(apart):
                for s in range(4):
                    body(i, s)
                if between:
                    between[i]()
            with eng.Fori(apart, NC // 4) as i:
                for s in range(4):
                    body(i, s)

        def norm_dve(dve, N, between=()):
            def body(i, s):
                c = 4 * i + s
                need(dve, N.tr, c - 3)
                if N.store:
                    need(dve, N.st[s], 16 * i)
                for b in range(2):
                    q = 2 * c + b
                    ins = dve.tensor_scalar(N.xnb[:, s, b * D:(b + 1) * D], Xv[:, ds(q, 1), :], N.mean[:, ds(q, 1)],
                                            N.rstd[:, ds(q, 1)], ALU.subtract, ALU.mult)
                ins.then_inc(N.xn, 1)
            chunks(dve, body, between)

        def norm_act(act, N, between=()):
            def body(i, s):
                c = 4 * i + s
                need(act, N.pj, c - 1)
                if N.keep:
                    need(act, N.kept, c - 1)
                act.wait_ge(N.tr, c + 1)
                if N.keep:
                    act.activation(XHI[:, ds(2 * c, 2), :], BK[s % 2][:, :].rearrange("p (b d) -> p b d", b=2), ACT.Copy)
                act.activation(N.xT[:, s % 2], BK[s % 2][:, :], ACT.Copy).then_inc(N.xt, 1)
            chunks(act, body, between)

        def norm_pe(pe, N, dest):
            def transpose(i, s):
                c = 4 * i + s
                need(pe, N.xt, c - 1)
                pe.wait_ge(N.xn, c + 1)
                for j in range(2 * KD):
                    t = pe.transpose(BK[s % 2][:, j * P:(j + 1) * P], N.xnb[:, s, j * P:(j + 1) * P], ident)
                t.then_inc(N.tr, 1)

            def project(i, s):
                c = 4 * i + s
                pe.wait_ge(N.xt, c + 1)
                for b in range(2):
                    for k in range(KD):
                        j = b * KD + k
                        m = pe.matmul(dest[:, ds(c * 16 + b * 8, 8)], N.xT[:, s % 2, j * P:(j + 1) * P],
                                      N.w8[:, k, :], start=k == 0, stop=k == KD - 1)
                m.then_inc(N.pj, 1)

            def body(i, s):
                transpose(i, s)
                if s:
                    project(i, s - 1)
                elif not isinstance(i, int) or i:
                    project(i - 1, 3)
            chunks(pe, body)
            project(NC // 4 - 1, 3)

        def norm_sp(sp, N, between=()):
            rows = xn_dram[0:NTOK].rearrange("(b l) d -> b l d", b=2)

            def body(i, s):
                c = 4 * i + s
                sp.wait_ge(N.xn, c + 1)
                sp.dma_start(rows[:, ds(c * P, P), :].rearrange("b p d -> p b d"),
                             N.xnb[:, s].rearrange("p (b d) -> p b d", b=2)).then_inc(N.st[s], 16)
            chunks(sp, body, between)
            for s in range(4):
                sp.wait_ge(N.st[s], 16 * (NC // 4))

        wdt = WIN[:, :, DI + CONV:DI + CONV + H]
        norm_a = Norm("a", XNB0, XT0, wdt, MEAN, RSTD, True, False)
        wr8 = WR[:, :].rearrange("p (k n) -> p k n", k=KD)

        M = {n: sem("mix_" + n) for n in (
            "act_in", "act_out", "cum", "a_now", "xts", "xbc", "taken", "tapped", "xc", "z", "zs", "rg", "bc",
            "decay", "masked", "y2", "st", "y1", "y2_read", "y1_read", "st_read", "y", "scaled", "ytr", "yth", "yt", "po", "po_out",
            "xtr", "xs", "xdt", "xdec", "dx", "square")}
        R = [{n: sem(f"{n}_{f}") for n in (
            "exp_in", "exp_out", "routed", "summed", "onehot_dve", "onehot_pool", "listed", "idx",
            "gath0", "gath1", "tr", "xt", "up0", "up1", "ha", "silu", "hb", "gated", "htr", "ht", "y", "yo",
            "scat0", "scat1", "w2_hi", "hth")} for f in range(2)]

        def router_scratch(base):
            t = carve(base)
            r = {}
            r["XNB"] = t(4 * 2 * D).rearrange("p (s n) -> p s n", s=4)
            r["XT"] = t(2 * 2 * D).rearrange("p (s n) -> p s n", s=2)
            r["OHR"] = r["XT"].rearrange("p s (i n) -> p (s i) n", n=P)
            assert t.at[0] <= NQ // 2 * D
            for n in ("SC", "W", "SBI", "EQ", "OH1", "OH2", "M12", "INC", "RK"):
                r[n] = t(NQ * E)
            for n in ("MX", "Z", "R1", "V1", "P1", "G1", "T1", "TI"):
                r[n] = t(NQ)
            r["TWO"] = t(NQ * 4)
            for j, n in enumerate(("R2", "P2", "V2", "G2")):
                r[n] = r["TWO"].rearrange("p (q j) -> p q j", j=4)[:, :, j]
            r["NOW"] = t(16)
            r["CNT"], r["END"] = t(E), t(E)
            r["CMP"] = t(E * NQ)
            r["EF"] = t(ST)
            r["RHS"] = t(8 * 2 * ST).rearrange("p (i j n) -> p i j n", i=8, j=2)
            r["ZERO"] = t(2 * ST)
            return r
        G = router_scratch(KEEP)
        norm_f = [Norm(f"f{f}", G["XNB"], G["XT"], wr8, MEAN, RSTD, False, True) for f in range(2)]

        def route_dve(dve, st, f):
            g, r = G, R[f]
            v3 = lambda ap: ap.rearrange("p (q e) -> p q e", e=E)
            sc, w, sbi, eq = g["SC"], g["W"], g["SBI"], g["EQ"]
            rev = repeat(CST[:, C_REV:C_REV + E], NQ)
            st(dve.tensor_tensor(v3(sc), v3(BK[2][:, 0:NQ * E]), repeat(ROUTE_B[:, 0:E], NQ), ALU.add))
            st.after()
            st(dve.tensor_reduce(g["MX"], v3(sc), AX.X, ALU.max))
            st(dve.tensor_tensor(v3(sbi), v3(sc), repeat(ROUTE_B[:, E:2 * E], NQ), ALU.add))
            st.after()
            dve.tensor_tensor(v3(w), v3(sc), spread(g["MX"], E), ALU.subtract).then_inc(r["exp_in"], 1)
            for k in range(TOPK):
                oh, rk = g[f"OH{k + 1}"], g[f"R{k + 1}"]
                st(dve.tensor_reduce(g["T1"], v3(sbi), AX.X, ALU.max))
                st.after()
                st(dve.tensor_tensor(v3(eq), v3(sbi), spread(g["T1"], E), ALU.is_equal))
                st.after()
                st(dve.tensor_tensor(v3(eq), v3(eq), rev, ALU.mult))
                st.after()
                st(dve.tensor_reduce(rk, v3(eq), AX.X, ALU.max))
                st.after()
                st(dve.tensor_tensor(v3(oh), spread(rk, E), rev, ALU.is_equal))
                st.after()
                if k == 0:
                    st(dve.scalar_tensor_tensor(sbi, oh, -BIG, sbi, ALU.mult, ALU.add))
                    st.after()
            dve.tensor_tensor(g["M12"], g["OH1"], g["OH2"], ALU.add).then_inc(r["routed"], 1)
            dve.wait_ge(r["exp_out"], 1)
            st(dve.tensor_reduce(g["Z"], v3(w), AX.X, ALU.add))
            st.after()
            st(dve.reciprocal(g["Z"], g["Z"]))
            st.after()
            st(dve.tensor_tensor(v3(w), v3(w), spread(g["Z"], E), ALU.mult))
            st.after()
            for k in range(TOPK):
                st(dve.tensor_tensor(eq, w, g[f"OH{k + 1}"], ALU.mult))
                st.after()
                st(dve.tensor_reduce(g[f"V{k + 1}"], v3(eq), AX.X, ALU.add))
                st.after()
            st(dve.tensor_tensor(g["T1"], g["V1"], g["V2"], ALU.add))
            st.after()
            st(dve.reciprocal(g["T1"], g["T1"]))
            st.after()
            for k in range(TOPK):
                st(dve.tensor_tensor(g[f"G{k + 1}"], g[f"V{k + 1}"], g["T1"], ALU.mult))
            dve.wait_ge(r["summed"], 1)
            tot = BK[3][:, 256:512]
            st(dve.tensor_copy(g["RK"], tot))
            st(dve.memset(eq, 1.0))
            st.after()
            for e in range(E):
                st(dve.tensor_tensor_scan(v3(g["INC"])[:, :, e], v3(eq)[:, :, e], v3(g["RK"])[:, :, e],
                                          0.0, ALU.mult, ALU.add))
            st.after()
            last = v3(g["INC"])[:, NQ - 1, :]
            cmp3 = g["CMP"].rearrange("p (e k) -> p e k", e=E)
            st(dve.tensor_tensor(cmp3, spread(last, NQ), repeat(CST[:, C_K128:C_K128 + NQ], E), ALU.is_gt))
            st.after()
            st(dve.tensor_reduce(g["CNT"], cmp3, AX.X, ALU.add))
            st.after()
            st(dve.tensor_tensor_scan(g["END"], eq[:, 0:E], g["CNT"], 0.0, ALU.mult, ALU.add))
            st.after()
            st(dve.tensor_tensor(g["CNT"], g["END"], g["CNT"], ALU.subtract))
            st.after()
            st(dve.tensor_scalar(g["CNT"], g["CNT"], float(P), None, ALU.mult))
            st(dve.tensor_tensor(g["INC"], g["INC"], g["RK"], ALU.subtract))
            st.after()
            st(dve.tensor_tensor(g["INC"], g["INC"], BK[3][:, 0:256], ALU.add))
            st.after()
            st(dve.tensor_tensor(v3(g["INC"]), v3(g["INC"]), repeat(g["CNT"], NQ), ALU.add))
            st.after()
            ti = g["TI"].bitcast(i32)
            for k in range(TOPK):
                p, row = g[f"P{k + 1}"], g[f"R{k + 1}"]
                st(dve.tensor_tensor(eq, g["INC"], g[f"OH{k + 1}"], ALU.mult))
                st.after()
                st(dve.tensor_reduce(g["T1"], v3(eq), AX.X, ALU.add))
                st.after()
                st(dve.tensor_copy(ti, g["T1"]))
                st.after()
                st(dve.tensor_single_scalar(ti, ti, 7, ALU.arith_shift_right))
                st.after()
                st(dve.tensor_copy(p, ti))
                st.after()
                st(dve.scalar_tensor_tensor(row, p, -float(P), g["T1"], ALU.mult, ALU.add))
                st.after()
                st(dve.tensor_tensor(g[f"V{k + 1}"], CST[:, C_TOK:C_TOK + NQ], row, ALU.subtract))
                st.after()
            st(dve.memset(g["EF"], 0.0))
            st(dve.memset(g["ZERO"], 0.0))
            st.after()
            for e in range(E - 1):
                st(dve.scalar_tensor_tensor(g["EF"], CST[:, C_IT:C_IT + ST], g["END"][:, e:e + 1], g["EF"],
                                            ALU.is_ge, ALU.add))
                st.after()
            dve.tensor_copy(EXPERT[:, :], g["EF"]).then_inc(r["routed"], 1)
            st.clear()

            onehots(dve, st, f, False)
            dve.wait_ge(r["summed"], 2)
            st(dve.tensor_scalar(g["EF"], BK[4][:, 0:ST], CST[:, C_PAD:C_PAD + 1], None, ALU.add))
            st(dve.tensor_copy(GATE[:, :], BK[4][:, ST:2 * ST]))
            st.after()
            dve.tensor_copy(IDX[:, :], g["EF"]).then_inc(r["idx"], 1)
            st.clear()

        POOLS = (3, 7)

        def onehots(eng, st, f, pool):
            g, r = G, R[f]

            def body(i):
                for at in (x for x in range(8) if (x in POOLS) == pool):
                    s, k = divmod(at, 2)
                    if not isinstance(i, int):
                        eng.wait_ge(r["listed"], 8 * (i - 1) + at + 1)
                    if pool:
                        now = g["NOW"][:, 4 * s:4 * s + 4]
                        row, tile, token, gate = (now[:, j:j + 1] for j in range(4))
                        st(eng.tensor_copy(now, g["TWO"][:, ds(16 * i + 4 * s, 4)]))
                        st.after()
                    else:
                        row, tile, token, gate = (g[f"{n}{k + 1}"][:, ds(4 * i + s, 1)] for n in ("R", "P", "V", "G"))
                    eng.tensor_scalar(g["OHR"][:, at], CST[:, C_IOTA:C_IOTA + P], row, None, ALU.is_equal)
                    for j, val in enumerate((token, gate)):
                        ins = eng.tensor_scalar(g["RHS"][:, at, j], CST[:, C_IT:C_IT + ST], tile, val,
                                                ALU.is_equal, ALU.mult)
                    ins.then_inc(r["onehot_pool" if pool else "onehot_dve"], 1)
                if pool:
                    st.clear()
            body(0)
            with eng.Fori(1, NQ // 4) as i:
                body(i)

        def route_pool(pool, st, f):
            for i in range(4):
                pool.wait_ge(R[f]["w2_hi"], i + 1)
                part = slice(i * 2048, (i + 1) * 2048)
                pool.tensor_tensor(W2LO[:, part], W2[:, part], W2HI[:, part].bitcast(f32), ALU.subtract)
            pool.wait_ge(R[f]["routed"], 2)
            onehots(pool, st, f, True)

        def route_act(act, f):
            act.wait_ge(loaded_w2[f], 16)
            for b in range(2):
                act.wait_ge(stored_x[b], 16 * (f + 1))
            act.wait_ge(norm_f[f].xn, NC)
            for i in range(4):
                part = slice(i * 2048, (i + 1) * 2048)
                act.activation(W2HI[:, part], W2[:, part], ACT.Copy).then_inc(R[f]["w2_hi"], 1)
            act.wait_ge(R[f]["exp_in"], 1)
            act.activation(G["W"], G["W"], ACT.Exp).then_inc(R[f]["exp_out"], 1)

        def route_pe(pe, f):
            r, g = R[f], G
            pe.wait_ge(r["routed"], 1)
            pe.matmul(BK[3][:, 0:256], CST[:, C_US:C_US + P], g["M12"], start=True, stop=True)
            pe.matmul(BK[3][:, 256:512], CST[:, C_ONE:C_ONE + P], g["M12"], start=True, stop=True
                      ).then_inc(r["summed"], 1)
            pe.wait_ge(r["routed"], 2)
            pe.matmul(BK[4][:, 0:2 * ST], ident, g["ZERO"], start=True, stop=False)
            with pe.Fori(0, NQ // 4) as i:
                done = {True: 0, False: 0}
                for at in range(8):
                    pool = at in POOLS
                    done[pool] += 1
                    each = len(POOLS) if pool else 8 - len(POOLS)
                    pe.wait_ge(r["onehot_pool" if pool else "onehot_dve"], each * i + done[pool])
                    pe.matmul(BK[4][:, 0:2 * ST], g["OHR"][:, at], g["RHS"][:, at].rearrange("p j n -> p (j n)"),
                              start=False, stop=False).then_inc(r["listed"], 1)
            pe.matmul(BK[4][:, 0:2 * ST], ident, g["ZERO"], start=False, stop=True).then_inc(r["summed"], 1)

        def experts(eng_name, eng, st, f, acc):
            r = R[f]
            gath, scat = (r["gath0"], r["gath1"]), (r["scat0"], r["scat1"])

            if eng_name in ("pe", "dve"):
                coming = eng.alloc_register(f"{eng_name}_coming_{f}")
                under_way = [eng.alloc_register(f"{eng_name}_expert{p}_{f}") for p in range(2)]

            def fetch_expert(t):
                eng.load(coming, EXPERT[0:1, ds(t, 1)])

            def take_expert(p):
                eng.reg_mov(under_way[p], coming)

            def expert(p):
                return eng.snap(under_way[p], min_val=0, max_val=E - 1)

            def gather(t, p):
                need(eng, r["tr"], t - 1)
                eng.wait_ge(r["idx"], 1)
                st(eng.tensor_copy(IDC[:, p:p + 1], IDX[:, ds(t, 1)]))
                st.after()
                eng.indirect_dma_start(out=XG[:, p, :], out_offset=None, in_=xn_dram,
                                       in_offset=bass.IndirectOffsetOnAxis(ap=IDC[:, p:p + 1], axis=0)
                                       ).then_inc(gath[p], 16)

            def scatter(t, h, p):
                eng.wait_ge(r["yo"], t + 1)
                if not (isinstance(t, int) and t == 0):
                    eng.wait_ge(scat[1 - p], 16 * (h + p))
                st(eng.tensor_copy(IDC[:, 2 + p:3 + p], IDX[:, ds(t, 1)]))
                st.after()
                eng.indirect_dma_start(out=acc, out_offset=bass.IndirectOffsetOnAxis(ap=IDC[:, 2 + p:3 + p], axis=0),
                                       in_=YO[:, p, :], in_offset=None, compute_op=ALU.add
                                       ).then_inc(scat[p], 16)

            def pe_transpose(t, h, p):
                need(eng, r["xt"], t)
                eng.wait_ge(gath[p], 16 * (h + 1))
                for k in range(KD):
                    i = eng.transpose(BK[4][:, k * P:(k + 1) * P], XG[:, p, k * P:(k + 1) * P], ident)
                i.then_inc(r["tr"], 1)

            def pe_up(t, p, n):
                if n == 0:
                    take_expert(p)
                e = expert(p)
                if n == 0:
                    eng.wait_ge(r["xt"], t + 1)
                need(eng, r["hb" if n else "ha"], t - 1)
                for k in range(KD):
                    i = eng.matmul(BK[2 * p + n][:, :], XTF[:, p, k, :],
                                   W1v[:, ds(e, 1), k, n * HF:(n + 1) * HF], start=k == 0, stop=k == KD - 1)
                i.then_inc(r[f"up{n}"], 1)
                if n:
                    fetch_expert(t + 1)

            def pe_hidden(t, p):
                need(eng, r["ht"], t)
                eng.wait_ge(r["gated"], t + 1)
                for k in range(KF):
                    i = eng.transpose(BK[5][:, k * P:(k + 1) * P], HB[:, p, k * P:(k + 1) * P], ident)
                i.then_inc(r["htr"], 1)

            def pe_down(t, p):
                e = expert(p)
                need(eng, r["yo"], t)
                eng.wait_ge(r["ht"], t + 1)
                for k in range(KF):
                    x = slice(k * P, (k + 1) * P)
                    i = split_matmul(eng, BK[6][:, 0:D], HTH[:, p, x], HTL[:, p, x], W2HIv[:, ds(e, 1), k, :],
                                     W2LOv[:, ds(e, 1), k, :], k == 0, k == KF - 1)
                i.then_inc(r["y"], 1)

            def act_xt(t, p):
                need(eng, r["up1"], t - 1)
                eng.wait_ge(r["tr"], t + 1)
                eng.activation(XTF[:, p], BK[4][:, 0:D], ACT.Copy).then_inc(r["xt"], 1)

            def act_silu(t, p):
                eng.wait_ge(r["ha"], t + 1)
                eng.activation(HA[:, p], HA[:, p], ACT.Silu).then_inc(r["silu"], 1)

            def act_ht(t, p):
                need(eng, r["y"], t - 1)
                eng.wait_ge(r["htr"], t + 1)
                eng.activation(HTH[:, p], BK[5][:, :], ACT.Copy).then_inc(r["hth"], 1)

            def dve_hidden(t, p, rest):
                take_expert(p)
                e = expert(p)
                eng.wait_ge(r["up0"], t + 1)
                need(eng, r["gated"], t - 1)
                eng.tensor_tensor(HA[:, p], BK[2 * p][:, :], B1[:, ds(e, 1), 0:HF], ALU.add).then_inc(r["ha"], 1)
                if rest is not None:
                    eng.wait_ge(r["hth"], rest + 1)
                    eng.tensor_tensor(HTL[:, 1 - p], BK[5][:, :], HTH[:, 1 - p].bitcast(f32), ALU.subtract
                                      ).then_inc(r["ht"], 1)
                eng.wait_ge(r["up1"], t + 1)
                need(eng, r["htr"], t - 1)
                eng.tensor_tensor(HB[:, p], BK[2 * p + 1][:, :], B1[:, ds(e, 1), HF:2 * HF], ALU.add
                                  ).then_inc(r["hb"], 1)
                eng.wait_ge(r["silu"], t + 1)
                eng.wait_ge(r["hb"], t + 1)
                eng.tensor_tensor(HB[:, p], HB[:, p], HA[:, p], ALU.mult).then_inc(r["gated"], 1)
                fetch_expert(t + 1)

            def dve_out(t, h, p):
                e = expert(p)
                need(eng, scat[p], 16 * h)
                eng.wait_ge(r["y"], t + 1)
                st(eng.tensor_tensor(YO[:, p], BK[6][:, 0:D], B2[:, ds(e, 1), :], ALU.add))
                st.after()
                eng.tensor_scalar(YO[:, p], YO[:, p], GATE[:, ds(t, 1)], None, ALU.mult).then_inc(r["yo"], 1)

            def body(h, parts=(0, 1)):
                for p in parts:
                    t = 2 * h + p
                    const = isinstance(h, int)

                    def there(x):
                        return not const or x < SLOTS_T
                    o = 1 - p
                    if eng_name == "pe":
                        if there(t + 1):
                            pe_up(t + 1, o, 0)
                        pe_hidden(t, p)
                        if there(t + 1):
                            pe_up(t + 1, o, 1)
                        if there(t + 2):
                            pe_transpose(t + 2, h + 1, p)
                        pe_down(t, p)
                    if eng_name == "pool":
                        if there(t + 3):
                            gather(t + 3, o)
                        scatter(t, h, p)
                        st.clear()
                    if eng_name == "act":
                        act_ht(t, p)
                        if there(t + 1):
                            act_silu(t + 1, o)
                        if there(t + 2):
                            act_xt(t + 2, p)
                    if eng_name == "dve":
                        if there(t + 1):
                            dve_hidden(t + 1, o, t)
                        else:
                            eng.wait_ge(r["hth"], t + 1)
                            eng.tensor_tensor(HTL[:, p], BK[5][:, :], HTH[:, p].bitcast(f32), ALU.subtract
                                              ).then_inc(r["ht"], 1)
                        dve_out(t, h, p)
                        st.clear()

            if eng_name == "pe":
                fetch_expert(0)
                pe_transpose(0, 0, 0)
                pe_up(0, 0, 0)
                pe_up(0, 0, 1)
                pe_transpose(1, 0, 1)
            if eng_name == "pool":
                for t in range(3):
                    gather(t, t % 2)
                st.clear()
            if eng_name == "act":
                act_xt(0, 0)
                act_silu(0, 0)
                act_xt(1, 1)
            if eng_name == "dve":
                fetch_expert(0)
                dve_hidden(0, 0, None)
            body(0)
            with eng.Fori(1, SLOTS_T // 2 - 1) as h:
                body(h)
            body(SLOTS_T // 2 - 1)
            body(SLOTS_T // 2, (0,))
            if eng_name == "pool":
                eng.wait_ge(scat[0], 16 * (SLOTS_T // 2 + 1))
                eng.wait_ge(scat[1], 16 * (SLOTS_T // 2))

        take, ktake = carve(PHASE), carve(KEEP)
        WHI, WLO = (rounded(n, "PHASE", i * 8192, 8192) for i, n in enumerate(("ATT_W_HI", "ATT_W_LO")))
        take(8192)
        WRAW = take(8192)
        LNWB = take(2 * KD).rearrange("p (s k) -> p s k", s=2)
        XH = take(2 * D).rearrange("p (b n) -> p b n", b=2)
        XR = take(2 * D).rearrange("p (b n) -> p b n", b=2)
        SCO = take(2 * 8)
        SMX = take(2 * 8)
        SEX = take(2 * 2 * 8).rearrange("p (j n) -> p j n", j=2)
        SPR = take(2 * 8)
        PRD = take(2 * HF).rearrange("p (b n) -> p b n", b=2)
        XTA = ktake(3 * D)
        XTAv = XTA.rearrange("p (b k t) -> p b k t", b=3, k=KD)
        XTH, XTL = (rounded(n, "KEEP", (3 + 6 * i) * D, 6 * D).rearrange("p (s n) -> p s n", s=2)
                    for i, n in enumerate(("ATT_X_HI", "ATT_X_LO")))
        ktake(12 * D)
        KDF, VDF, V1S = ktake(HF), ktake(HF), ktake(HF)
        OA = ktake(2 * HF).rearrange("p (b n) -> p b n", b=2)
        OTH, OTL = (rounded(n, "W1", (E - 1) * KD * 2 * HF + i * 2 * HF, 2 * HF).rearrange("p (b n) -> p b n", b=2)
                    for i, n in enumerate(("ATT_O_HI", "ATT_O_LO")))
        A = {n: sem("att_" + n) for n in (
            "w0", "w1", "w2", "w3", "w_hi", "w_lo", "xh", "tr", "xt", "xd", "xth", "split", "kd", "vd", "v1", "q0", "q1",
            "kds", "vds", "v1s", "prod", "sin", "sexp", "spr", "out0", "out1", "otr", "oth", "ot", "po", "x3")}

        def weight(w, j):
            return w[:, j * 2048:(j + 1) * 2048]

        block = ctx.enter_context(nc.Block())

        @block.sync
        def _(sp):
            load_x(sp, u, loaded_x)
            sp.dma_start(CST[:, :], consts).then_inc(loaded_small, 16)
            sp.dma_start(WIN, w_in.rearrange("(k p) n -> p k n", p=P)).then_inc(loaded_small, 16)
            sp.dma_start(WOUT, w_mix_out.rearrange("(k p) n -> p k n", p=P)).then_inc(loaded_small, 16)
            sp.dma_start(CW, conv_w.rearrange("(m p) s -> p m s", p=P)).then_inc(loaded_small, 16)
            sp.dma_start(CB, conv_b.rearrange("(m p) -> p m", p=P), allow_slow_non_contiguous=True).then_inc(loaded_small, 16)
            sp.dma_start(NW, norm_w.rearrange("(m p) -> p m", p=P), allow_slow_non_contiguous=True).then_inc(loaded_small, 16)
            for dst, src in ((DTB, dt_bias), (ALG, a_log), (DSK, d_skip), (ROUTE_B[:, 0:E], b_route),
                             (ROUTE_B[:, E:2 * E], bias_n)):
                sp.dma_start(dst, src.unsqueeze(0).broadcast_to([P, 8])).then_inc(loaded_small, 16)
            sp.dma_start(WR[:, :].rearrange("p (k n) -> p k n", k=KD),
                         w_route.rearrange("(k p) n -> p k n", p=P)).then_inc(loaded_small, 16)
            barrier(sp)
            barrier(sp)

            def load_last():
                sp.dma_start(W1v[:, E - 1], w1[E - 1].rearrange("(k p) n -> p k n", p=P)).then_inc(loaded_w1, 16)

            def load_w2(n):
                sp.dma_start(W2.rearrange("p (e k n) -> p e k n", e=E, k=KF), w2.rearrange("e (k p) n -> p e k n", p=P)).then_inc(loaded_w2[n], 16)
                sp.dma_start(B1, b1.unsqueeze(0).broadcast_to([P, E, 2 * HF])).then_inc(loaded_b, 16)
                sp.dma_start(B2, b2.unsqueeze(0).broadcast_to([P, E, D])).then_inc(loaded_b, 16)

            def store_x(dst, n):
                for b in range(2):
                    sp.dma_start(dst[b * L:(b + 1) * L, :].rearrange("(c p) d -> p c d", p=P),
                                 Xv.rearrange("p (c b) d -> p c b d", b=2)[:, :, b, :]).then_inc(stored_x[b], 16)
            load_w2(0)

            def store_sum():
                sp.wait_ge(root_ready, 4)
                store_x(acc_dram, 0)
            norm_sp(sp, norm_f[0], [lambda: None, store_sum])
            for e in range(E):
                sp.dma_start(W1v[:, e], w1[e].rearrange("(k p) n -> p k n", p=P)).then_inc(loaded_w1, 16)
            for b in range(2):
                sp.wait_ge(stored_x[b], 16)
            barrier(sp)
            sp.wait_ge(loaded_b, 32)
            barrier(sp)
            load_x(sp, acc_dram, reloaded_x)
            for s in range(3):
                sp.dma_start(weight(WRAW, s).rearrange("p (k n) -> p k n", k=KD),
                             w_qkv[s].rearrange("(k p) n -> p k n", p=P)).then_inc(A[f"w{s}"], 16)
            sp.dma_start(weight(WRAW, 3).rearrange("p (k n) -> p k n", k=KA),
                         w_att_out.rearrange("(k p) n -> p k n", p=P)).then_inc(A["w3"], 16)
            for s, src in enumerate((ln_w, ln_b)):
                sp.dma_start(LNWB[:, s], src.rearrange("(k p) -> p k", p=P), allow_slow_non_contiguous=True).then_inc(A["w2"], 16)
            barrier(sp)
            load_last()
            load_w2(1)
            store_x(out, 1)
            norm_sp(sp, norm_f[1])
            for b in range(2):
                sp.wait_ge(stored_x[b], 32)
            barrier(sp)
            sp.wait_ge(loaded_b, 64)
            barrier(sp)

        @block.vector
        def _(dve):
            st = Steps(dve, dve_step)
            stats(dve, loaded_x)
            rstd_steps(dve, st, 1)
            st.clear()
            dve.wait_ge(loaded_small, 16 * 12)

            def split_weights():
                for k in range(4):
                    st(dve.tensor_scalar(WOUT[:, k, :], WOUT[:, k, :], NW[:, k:k + 1], None, ALU.mult))
                st.after()
                st(dve.tensor_copy(WOUTHI, WOUT))
                dve.wait_ge(norm_a.xt, 1)
                dve.tensor_tensor(WINLO[:, :, 0:DI + CONV], WIN[:, :, 0:DI + CONV],
                                  WINHI[:, :, 0:DI + CONV].bitcast(f32), ALU.subtract)
                st.after()
                dve.tensor_tensor(WOUTLO, WOUT, WOUTHI.bitcast(f32), ALU.subtract)

            norm_dve(dve, norm_a, [split_weights])
            st.clear()
            st(dve.tensor_copy(YT0[:, 0:P], CST[:, C_MASK:C_MASK + P]))
            st.after()
            st(dve.tensor_copy(identb, CST[:, C_ID:C_ID + P]))
            st(dve.tensor_copy(maskb, YT0[:, 0:P]))
            st(dve.memset(XB[:, :, :, 0:3], 0.0))
            st(dve.memset(SST, 0.0))
            x, ax, s, w, pl, rl = SP_
            v3 = lambda ap: ap.rearrange("p (q h) -> p q h", h=H)
            dve.wait_ge(norm_a.pj, NC)
            st(dve.tensor_tensor(v3(x), v3(BK[2][:, 0:NQ * H]), repeat(DTB, NQ), ALU.add))
            st.after()
            st(dve.scalar_tensor_tensor(ax, x, -1.0, x, ALU.mult, ALU.max))
            dve.tensor_scalar(rl, x, 0.0, None, ALU.max).then_inc(M["act_in"], 1)
            dve.wait_ge(M["act_out"], 1)
            st(dve.tensor_scalar(w, ax, 2.0, None, ALU.add))
            st.after()
            st(dve.reciprocal(w, w))
            st.after()
            st(dve.tensor_tensor(s, ax, w, ALU.mult))
            st.after()
            st(dve.tensor_tensor(w, s, s, ALU.mult))
            st.after()
            st(dve.tensor_scalar(pl, w, 1.0 / 17, None, ALU.mult))
            for d in (15, 13, 11, 9, 7, 5, 3):
                st.after()
                st(dve.scalar_tensor_tensor(pl, pl, 1.0 / d, w, ALU.add, ALU.mult))
            st.after()
            st(dve.scalar_tensor_tensor(pl, pl, 1.0, s, ALU.add, ALU.mult))
            st.after()
            st(dve.scalar_tensor_tensor(PDT, pl, 2.0, rl, ALU.mult, ALU.add))
            st.after()
            st(dve.tensor_scalar(ALG, ALG, -1.0, None, ALU.mult))
            st.after()
            dve.tensor_tensor(v3(PA), v3(PDT), repeat(ALG, NQ), ALU.mult).then_inc(M["act_in"], 1)
            dve.wait_ge(M["cum"], 1)
            st(dve.tensor_scalar(PNC, BK[3][:, 0:256], -1.0, None, ALU.mult))
            st(dve.tensor_copy(PEC, BK[3][:, 0:256]))
            st(dve.tensor_copy(PET, BK[3][:, 256:512]))
            st.after()
            dve.tensor_tensor(PWD, PET, PNC, ALU.add).then_inc(M["act_in"], 1)
            dve.wait_ge(M["act_out"], 2)
            st(dve.tensor_tensor(PWD, PWD, PDT, ALU.mult))
            st.clear()
            barrier(dve)

            def taps(c, lo, hi, prev):
                ns = prev
                for i in range(lo, hi):
                    s, m = divmod(i, MC)
                    if s:
                        st.after(ns[i - MC])
                    ins = dve.scalar_tensor_tensor(ACC[:, m], XB[:, m, :, s:s + P], CW[:, m, s:s + 1], ACC[:, m],
                                                   ALU.mult, ALU.add)
                    if i == 3 * MC - 1:
                        ins.then_inc(M["tapped"], 1)
                    else:
                        ns[i] = st(ins)
                return ns

            def mask(c, b):
                dve.wait_ge(M["decay"], 2 * c + b + 1)
                if b:
                    dve.wait_ge(M["xs"], 2 * c + 2)
                else:
                    dve.wait_ge(M["bc"], c + 1)
                bc = BK[6][:, P:2 * P] if b else BK[1][:, 0:P]
                dve.tensor_tensor(LM[:, b], LM[:, b], bc.unsqueeze(1).broadcast_to([P, H, P]),
                                  ALU.mult).then_inc(M["masked"], 1)

            def from_state(c, b):
                q = 2 * c + b
                need(dve, M["ytr"], q - 1)
                need(dve, M["square"], q - 1)
                dve.wait_ge(M["y2"], q + 1)
                dve.tensor_tensor(Y[:, b].rearrange("p (h n) -> p h n", h=H),
                                  BK[0][:, :].rearrange("p (h n) -> p h n", h=H),
                                  spread(PEC[:, ds(q * 8, 8)], HD), ALU.mult).then_inc(M["y2_read"], 1)

            def within(c, b):
                q = 2 * c + b
                dve.wait_ge(M["y1"], q + 1)
                dve.wait_ge(M["y2_read"], q + 1)
                dve.tensor_tensor(Y[:, b], Y[:, b], BK[1][:, :], ALU.add).then_inc(M["y1_read"], 1)

            def increment(c, b):
                q = 2 * c + b
                dve.wait_ge(M["st"], q + 1)
                dve.wait_ge(M["scaled"], q + 1)
                dve.tensor_tensor(SST[:, b], SST[:, b], BK[2][:, :], ALU.add).then_inc(M["st_read"], 1)

            def outputs(c, b):
                q = 2 * c + b
                dve.wait_ge(M["dx"], q + 1)
                dve.wait_ge(M["y1_read"], q + 1)
                st(dve.tensor_tensor(Y[:, b], Y[:, b], DX[:, b], ALU.add))
                dve.wait_ge(M["zs"], q + 1)
                st.after()
                dve.tensor_tensor(Y[:, b], Y[:, b], ZS[:, b], ALU.mult).then_inc(M["y"], 1)

            def rest(c, b):
                q = 2 * c + b
                dve.wait_ge(M["yth"], q + 1)
                dve.tensor_tensor(YTLO[:, b], BK[5][:, :], YTHI[:, b].bitcast(f32), ALU.subtract).then_inc(M["yt"], 1)

            def xdt(c, b):
                q = 2 * c + b
                dve.wait_ge(M["xs"], q + 1)
                need(dve, M["y1"], q - 1)
                dve.tensor_tensor(XDT[:, b].rearrange("p (h n) -> p h n", h=H),
                                  XS[:, b].rearrange("p (h n) -> p h n", h=H),
                                  spread(PDT[:, ds(q * 8, 8)], HD), ALU.mult).then_inc(M["xdt"], 1)

            def mixer(c, n):
                ns = {}

                def some_taps(lo, hi):
                    if n is not None:
                        taps(n, lo, hi, ns)
                if n is not None:
                    dve.wait_ge(M["taken"], 3 * n + 3)
                some_taps(0, 4)
                if c is not None:
                    mask(c, 0)
                    xdt(c, 0)
                    from_state(c, 0)
                    xdt(c, 1)
                    increment(c, 0)
                some_taps(4, 5)
                if c is not None:
                    within(c, 0)
                some_taps(5, 7)
                if c is not None:
                    mask(c, 1)
                    outputs(c, 0)
                    from_state(c, 1)
                    increment(c, 1)
                    within(c, 1)
                    rest(c, 0)
                    outputs(c, 1)
                some_taps(7, 18)
                if c is not None:
                    rest(c, 1)
                st.clear()
            mixer(None, 0)
            mixer(0, 1)
            with dve.Fori(1, NC - 1) as c:
                mixer(c, c + 1)
            mixer(NC - 1, None)
            barrier(dve)

            st(dve.tensor_scalar(VARE[:, :], SS, 1.0 / DI, EPS, ALU.mult, ALU.add))
            st.after()
            root(dve, st, 2, VARE, RST2)
            st.clear()
            def residual(lo, hi):
                with dve.Fori(lo, hi) as i:
                    added = [st(dve.scalar_tensor_tensor(Xv[:, ds(4 * i + j, 1), :], KEEPv[:, ds(4 * i + j, 1), :],
                                                         RST2[:, ds(4 * i + j, 1)], Xv[:, ds(4 * i + j, 1), :],
                                                         ALU.mult, ALU.add)) for j in range(4)]
                    for j in range(4):
                        st.after(added[j])
                        st(dve.bn_stats(STv[:, ds(4 * i + j, 1), :], Xv[:, ds(4 * i + j, 1), :]))
                    st.clear()

            first, second = slice(0, NQ // 2), slice(NQ // 2, NQ)
            residual(0, 4)
            rstd_steps(dve, st, 3, first)
            st.clear()

            def second_half():
                residual(6, 8)
                rstd_steps(dve, st, 4, second)
                st.clear()

            norm_dve(dve, norm_f[0], [lambda: residual(4, 6), second_half])
            dve.wait_ge(norm_f[0].pj, NC)
            route_dve(dve, st, 0)
            barrier(dve)
            dve.wait_ge(loaded_b, 32)
            experts("dve", dve, st, 0, acc_dram)
            barrier(dve)

            stats(dve, reloaded_x)
            rstd_steps(dve, st, 5)
            st(dve.tensor_scalar(TMP[2][:, :], VARE[:, :], -EPS, None, ALU.add))
            st.after()
            st(dve.tensor_tensor(TMP[2][:, :], TMP[2][:, :], RSTD[:, :], ALU.mult))
            st.after()
            st(dve.tensor_tensor(TMP[2][:, :], TMP[2][:, :], RSTD[:, :], ALU.mult))
            st.after()
            st(dve.tensor_scalar(VARE[:, :], TMP[2][:, :], EPS, None, ALU.add))
            st.after()
            root(dve, st, 6, VARE, RST2)
            st(dve.tensor_tensor(RST2[:, :], RST2[:, :], RSTD[:, :], ALU.mult))
            st.clear()

            def normed(c):
                for b in range(2):
                    q = 2 * c + b
                    need(dve, A["tr"], c)
                    dve.tensor_scalar(XH[:, b], Xv[:, ds(q, 1), :], MEAN[:, ds(q, 1)],
                                      RST2[:, ds(q, 1)], ALU.subtract, ALU.mult).then_inc(A["xh"], 1)

            def difference(c):
                dve.wait_ge(A["xt"], c + 1)
                need(dve, A["split"], c)
                dve.tensor_tensor(XTAv[:, 2], XTAv[:, 0], XTAv[:, 1], ALU.subtract).then_inc(A["xd"], 1)

            def rest(c, h):
                s = 2 * c + h
                for b in range(2):
                    dve.wait_ge(A["oth"], 2 * s + b + 1)
                    dve.tensor_tensor(OTL[:, b], BK[7 - 7 * b][:, :], OTH[:, b].bitcast(f32), ALU.subtract
                                      ).then_inc(A["ot"], 1)

            def attend(c, h, between):
                s = 2 * c + h
                dve.wait_ge(A["kds"], s + 1)
                for b, sq in enumerate((A["q0"], A["q1"])):
                    dve.wait_ge(sq, s + 1)
                    dve.tensor_tensor(PRD[:, b], BK[1 + b][:, :], KDF, ALU.mult).then_inc(A["prod"], 1)
                for b in range(2):
                    dve.wait_ge(A["prod"], 2 * s + b + 1)
                    st(dve.tensor_reduce(SCO[:, b * 8:(b + 1) * 8], PRD[:, b].rearrange("p (h n) -> p h n", h=8),
                                         AX.X, ALU.add))
                st.after()
                scale = 1.0 / 16.0
                st(dve.tensor_scalar(SMX, SCO, scale, 0.0, ALU.mult, ALU.max))
                st.after()
                st(dve.scalar_tensor_tensor(SEX[:, 0], SCO, scale, SMX, ALU.mult, ALU.subtract))
                dve.tensor_scalar(SEX[:, 1], SMX, -1.0, None, ALU.mult).then_inc(A["sin"], 1)
                between()
                dve.wait_ge(A["sexp"], s + 1)
                st(dve.tensor_tensor(SMX, SEX[:, 0], SEX[:, 1], ALU.add))
                st.after()
                st(dve.reciprocal(SMX, SMX))
                st.after()
                need(dve, A["out1"], s)
                dve.tensor_tensor(SPR, SEX[:, 0], SMX, ALU.mult).then_inc(A["spr"], 1)
                dve.wait_ge(A["vds"], s + 1)
                need(dve, A["otr"], 2 * s - 1)
                dve.wait_ge(A["spr"], s + 1)
                st(dve.tensor_tensor(OA[:, 0].rearrange("p (h n) -> p h n", h=8),
                                     VDF.rearrange("p (h n) -> p h n", h=8), spread(SPR[:, 0:8], AD), ALU.mult))
                dve.wait_ge(A["v1s"], s + 1)
                st.after()
                dve.tensor_tensor(OA[:, 0], OA[:, 0], V1S, ALU.add).then_inc(A["out0"], 1)

            def residual_a(c):
                for b in range(2):
                    q = 2 * c + b
                    st(dve.tensor_scalar(XR[:, b], Xv[:, ds(q, 1), :], MEAN[:, ds(q, 1)], RSTD[:, ds(q, 1)],
                                         ALU.subtract, ALU.mult))
                for b in range(2):
                    q = 2 * c + b
                    st.after(st.n - 1)
                    st(dve.tensor_tensor(XR[:, b], XR[:, b], Xv[:, ds(q, 1), :], ALU.add))
                st.after()

            def residual_b(c):
                added = []
                dve.wait_ge(A["po"], 4 * c + 4)
                for b in range(2):
                    q = 2 * c + b
                    added.append(st(dve.tensor_tensor(Xv[:, ds(q, 1), :], XR[:, b], BK[6][:, b * D:(b + 1) * D],
                                                      ALU.add)))
                for b in range(2):
                    q = 2 * c + b
                    st.after(added[b])
                    dve.bn_stats(STv[:, ds(q, 1), :], Xv[:, ds(q, 1), :]).then_inc(A["x3"], 1)

            def nothing():
                pass

            def att(c, first=False, last=False):
                if not first:
                    rest(c - 1, 0)
                if not last:
                    normed(c + 1)
                attend(c, 0, nothing if first else lambda: residual_a(c - 1))
                if not last:
                    difference(c + 1)
                if not first:
                    rest(c - 1, 1)
                attend(c, 1, nothing if first else lambda: residual_b(c - 1))
                st.clear()
            normed(0)
            difference(0)
            att(0, first=True)
            with dve.Fori(1, NC - 1) as c:
                att(c)
            att(NC - 1, last=True)
            rest(NC - 1, 0)
            rest(NC - 1, 1)
            residual_a(NC - 1)
            residual_b(NC - 1)
            dve.wait_ge(A["x3"], NQ)
            rstd_steps(dve, st, 7)
            st.clear()
            barrier(dve)
            norm_dve(dve, norm_f[1])
            dve.wait_ge(norm_f[1].pj, NC)
            route_dve(dve, st, 1)
            barrier(dve)
            dve.wait_ge(loaded_b, 64)
            experts("dve", dve, st, 1, out)
            barrier(dve)

        @block.scalar
        def _(act):
            act_root(act, 1)
            act.wait_ge(loaded_small, 16 * 12)
            act.activation(WINHI[:, :, 0:DI + CONV], WIN[:, :, 0:DI + CONV], ACT.Copy)
            norm_act(act, norm_a)
            act.wait_ge(M["act_in"], 1)
            act.activation(SP_[1], SP_[1], ACT.Exp, scale=-1.0)
            act.activation(ALG, ALG, ACT.Exp).then_inc(M["act_out"], 1)
            act.wait_ge(M["act_in"], 3)
            act.activation(PEC, PEC, ACT.Exp)
            act.activation(PET, PET, ACT.Exp)
            act.activation(PWD, PWD, ACT.Exp).then_inc(M["act_out"], 1)
            barrier(act)
            st = Steps(act, act_step)

            def pre(n, between=lambda: None):
                if not (isinstance(n, int) and n == 0):
                    act.wait_ge(M["tapped"], n)
                    st(act.activation(XB[:, :, :, 0:3], XB[:, :, :, P:P + 3], ACT.Copy))
                need(act, M["xc"], n)
                for j in range(3):
                    act.wait_ge(M["xbc"], 3 * n + j + 1)
                    for m in (2 * j, 2 * j + 1):
                        act.activation(ACC[:, m], BK[j][:, (m % 2) * 256:(m % 2) * 256 + 256].rearrange(
                            "p (b t) -> p b t", b=2), ACT.Identity, bias=CB[:, m:m + 1], scale=CW[:, m, 3:4])
                    if j == 0 and not (isinstance(n, int) and n == 0):
                        st.after()
                    act.activation(XB[:, 2 * j:2 * j + 2, :, 3:3 + P],
                                   BK[j][:, :].rearrange("p (m b t) -> p m b t", m=2, b=2), ACT.Copy
                                   ).then_inc(M["taken"], 1)
                    if j == 0:
                        between()

            def decays(c, b):
                q = 2 * c + b
                act.wait_ge(M["rg"], q + 1)
                need(act, M["y1"], q - 1)
                for h in range(H):
                    i = act.activation(LM[:, b, h], BK[3 + h // 4][:, (h % 4) * P:(h % 4 + 1) * P], ACT.Exp,
                                       bias=PNC[:, ds(q * 8 + h, 1)])
                i.then_inc(M["decay"], 1)

            def yt(c, b):
                q = 2 * c + b
                act.wait_ge(M["ytr"], q + 1)
                need(act, M["po"], q - 1)
                act.activation(YTHI[:, b], BK[5][:, :], ACT.Copy).then_inc(M["yth"], 1)

            def square(c, b):
                q = 2 * c + b
                act.wait_ge(M["y"], q + 1)
                act.activation(ZS[:, b], Y[:, b], ACT.Square, accum_out=SS[:, ds(q, 1)]).then_inc(M["square"], 1)

            def po_out(c, b):
                q = 2 * c + b
                act.wait_ge(M["po"], q + 1)
                act.activation(KEEPv[:, ds(q, 1), :], BK[6][:, 256:512], ACT.Copy).then_inc(M["po_out"], 1)

            def zs(c, b):
                q = 2 * c + b
                act.wait_ge(M["z"], q + 1)
                need(act, M["y"], q - 1)
                need(act, M["square"], q - 1)
                act.activation(ZS[:, b], BK[7][:, :], ACT.Silu).then_inc(M["zs"], 1)

            def xs(c, b):
                q = 2 * c + b
                act.wait_ge(M["xtr"], q + 1)
                need(act, M["st"], q - 1)
                need(act, M["xdt"], q - 1)
                need(act, M["dx"], q - 1)
                act.activation(BT[:, b], BK[6][:, 0:P], ACT.Copy)
                act.activation(XS[:, b], BK[5][:, :], ACT.Copy).then_inc(M["xs"], 1)

            def xc(n):
                act.wait_ge(M["tapped"], n + 1)
                need(act, M["y2"], 2 * n)
                act.activation(XC, ACC, ACT.Silu).then_inc(M["xc"], 1)

            def mixer(c, n):
                last_out = not (c is None or isinstance(c, int) and c == 0)
                if n is not None:
                    pre(n, (lambda: po_out(c - 1, 1)) if last_out else (lambda: None))
                if c is not None:
                    if n is None:
                        po_out(c - 1, 1)
                    xs(c, 0)
                    zs(c, 0)
                    xs(c, 1)
                    decays(c, 1)
                    if not (isinstance(c, int) and c == 0):
                        square(c - 1, 1)
                    zs(c, 1)
                    yt(c, 0)
                    square(c, 0)
                if n is not None:
                    decays(n, 0)
                if c is not None:
                    po_out(c, 0)
                    yt(c, 1)
                if n is not None:
                    xc(n)
                st.clear()
            mixer(None, 0)
            mixer(0, 1)
            with act.Fori(1, NC - 1) as c:
                mixer(c, c + 1)
            mixer(NC - 1, None)
            square(NC - 1, 1)
            po_out(NC - 1, 1)
            barrier(act)
            act_root(act, 2)
            act_root(act, 3, slice(0, NQ // 2))
            norm_act(act, norm_f[0], [lambda: None, lambda: act_root(act, 4, slice(NQ // 2, NQ))])
            route_act(act, 0)
            barrier(act)
            experts("act", act, st, 0, acc_dram)
            barrier(act)
            def round_weights(j):
                act.wait_ge(A[f"w{j}"], 48 if j == 2 else 16)
                act.activation(weight(WHI, j), weight(WRAW, j), ACT.Copy).then_inc(A["w_hi"], 1)

            round_weights(0)
            round_weights(1)
            act_root(act, 5)
            act_root(act, 6)
            act.wait_ge(A["w2"], 48)

            def heads(c):
                act.wait_ge(A["tr"], c + 1)
                need(act, A["split"], c)
                for k in range(KD):
                    i = act.activation(XTAv[:, 0:2, k, :],
                                       BK[0][:, :].rearrange("p (b k t) -> p b k t", b=2, k=KD)[:, :, k, :],
                                       ACT.Identity, bias=LNWB[:, 1, k:k + 1], scale=LNWB[:, 0, k:k + 1])
                i.then_inc(A["xt"], 1)

            def round_heads(c, s):
                act.wait_ge(A["xd"], c + 1)
                need(act, A["v1"], 2 * c - 2)
                act.activation(XTH[:, s], XTA, ACT.Copy).then_inc(A["xth"], 1)

            def kd_copy(c, h):
                s = 2 * c + h
                act.wait_ge(A["kd"], s + 1)
                need(act, A["prod"], 2 * s)
                act.activation(KDF, BK[3][:, :], ACT.Copy).then_inc(A["kds"], 1)

            def v_copy(c, h, bank, dst, done, copied):
                s = 2 * c + h
                act.wait_ge(A[done], s + 1)
                need(act, A["out0"], s)
                need(act, A["out1"], s)
                act.activation(dst, BK[bank][:, :], ACT.Copy).then_inc(A[copied], 1)

            def vd_copy(c, h):
                v_copy(c, h, 4, VDF, "vd", "vds")

            def v1_copy(c, h):
                v_copy(c, h, 5, V1S, "v1", "v1s")

            def exps(c, h):
                s = 2 * c + h
                act.wait_ge(A["sin"], s + 1)
                act.activation(SEX, SEX, ACT.Exp).then_inc(A["sexp"], 1)

            def transposed(c, h):
                s = 2 * c + h
                for b in range(2):
                    act.wait_ge(A["otr"], 2 * s + b + 1)
                    need(act, A["po"], 2 * s + b - 1)
                    act.activation(OTH[:, b], BK[7 - 7 * b][:, :], ACT.Copy).then_inc(A["oth"], 1)

            def att(c, s, first=False, last=False):
                if not first:
                    transposed(c - 1, 0)
                kd_copy(c, 0)
                exps(c, 0)
                vd_copy(c, 0)
                if not last:
                    heads(c + 1)
                v1_copy(c, 0)
                if not last:
                    round_heads(c + 1, 1 - s)
                if not first:
                    transposed(c - 1, 1)
                kd_copy(c, 1)
                exps(c, 1)
                vd_copy(c, 1)
                v1_copy(c, 1)
            heads(0)
            round_heads(0, 0)
            round_weights(2)
            round_weights(3)
            att(0, 0, first=True)
            att(1, 1)
            with act.Fori(1, NC // 2 - 1) as i:
                att(2 * i, 0)
                att(2 * i + 1, 1)
            att(NC - 2, 0)
            att(NC - 1, 1, last=True)
            transposed(NC - 1, 0)
            transposed(NC - 1, 1)
            act_root(act, 7)
            barrier(act)
            norm_act(act, norm_f[1])
            route_act(act, 1)
            barrier(act)
            experts("act", act, st, 1, out)
            barrier(act)

        @block.gpsimd
        def _(pool):
            st = Steps(pool, pool_step)
            st(pool.memset(DX, 0.0))
            st.after()
            for dst in (xn_dram, acc_dram, out):
                pool.dma_start(dst[NTOK:NTOK + P, :], DX[:, 0, 0:D]).then_inc(zeroed, 16)
            pool.wait_ge(zeroed, 48)
            st.clear()

            def keep(i, s):
                c = 4 * i + s
                pool.wait_ge(norm_a.xt, c + 1)
                x = XT0[:, s % 2].rearrange("p (b d) -> p b d", b=2)
                pool.tensor_tensor(XLO[:, ds(2 * c, 2), :], x, XHI[:, ds(2 * c, 2), :].bitcast(f32), ALU.subtract
                                   ).then_inc(norm_a.kept, 1)
            chunks(pool, keep)
            barrier(pool)

            def prepare(n):
                need(pool, M["rg"], 2 * n)
                pool.tensor_copy(ANOW.rearrange("p b h -> p (b h)"), PA[:, ds(16 * n, 16)]).then_inc(M["a_now"], 1)
                need(pool, M["z"], 2 * n)
                for dst, src in ((XTSHI, XHI), (XTSLO, XLO)):
                    i = pool.tensor_copy(dst, src[:, ds(2 * n, 2), :].bitcast(f32).rearrange("p b (k t) -> p k b t", k=KD))
                i.then_inc(M["xts"], 1)

            def state(c, b):
                q = 2 * c + b
                pool.wait_ge(M["y2"], q + 1)
                s3 = SST[:, b].rearrange("p (h n) -> p h n", h=H)
                pool.tensor_tensor(s3, s3, spread(PET[:, ds(q * 8, 8)], HD), ALU.mult).then_inc(M["scaled"], 1)

            def inputs(c, b):
                q = 2 * c + b
                x3 = XS[:, b].rearrange("p (h n) -> p h n", h=H)
                pool.wait_ge(M["xs"], q + 1)
                need(pool, M["st"], q - 1)
                pool.tensor_tensor(XDEC[:, b].rearrange("p (h n) -> p h n", h=H), x3,
                                   spread(PWD[:, ds(q * 8, 8)], HD), ALU.mult).then_inc(M["xdec"], 1)
                need(pool, M["y"], q - 1)
                pool.tensor_tensor(DX[:, b].rearrange("p (h n) -> p h n", h=H), x3, spread(DSK, HD), ALU.mult
                                   ).then_inc(M["dx"], 1)

            def mixer(c, n):
                if c is not None:
                    for b in range(2):
                        inputs(c, b)
                        state(c, b)
                if n is not None:
                    prepare(n)
            mixer(None, 0)
            mixer(0, 1)
            with pool.Fori(1, NC - 1) as c:
                mixer(c, c + 1)
            mixer(NC - 1, None)
            barrier(pool)
            route_pool(pool, st, 0)
            barrier(pool)
            experts("pool", pool, st, 0, acc_dram)
            barrier(pool)

            def split_weights(j):
                pool.wait_ge(A["w_hi"], j + 1)
                pool.tensor_tensor(weight(WLO, j), weight(WRAW, j), weight(WHI, j).bitcast(f32), ALU.subtract
                                   ).then_inc(A["w_lo"], 1)

            def split(c, s):
                pool.wait_ge(A["xth"], c + 1)
                pool.tensor_tensor(XTL[:, s], XTA, XTH[:, s].bitcast(f32), ALU.subtract).then_inc(A["split"], 1)

            def second_output(c, h):
                s = 2 * c + h
                pool.wait_ge(A["spr"], s + 1)
                pool.wait_ge(A["vds"], s + 1)
                need(pool, A["otr"], 2 * s)
                st(pool.tensor_tensor(OA[:, 1].rearrange("p (h n) -> p h n", h=8),
                                      VDF.rearrange("p (h n) -> p h n", h=8), spread(SPR[:, 8:16], AD), ALU.mult))
                pool.wait_ge(A["v1s"], s + 1)
                st.after()
                pool.tensor_tensor(OA[:, 1], OA[:, 1], V1S, ALU.add).then_inc(A["out1"], 1)

            def att(c, s, last=False):
                second_output(c, 0)
                if not last:
                    split(c + 1, 1 - s)
                second_output(c, 1)
                st.clear()
            split_weights(0)
            split_weights(1)
            split(0, 0)
            split_weights(2)
            split_weights(3)
            att(0, 0)
            att(1, 1)
            with pool.Fori(1, NC // 2 - 1) as i:
                att(2 * i, 0)
                att(2 * i + 1, 1)
            att(NC - 2, 0)
            att(NC - 1, 1, last=True)
            barrier(pool)
            route_pool(pool, st, 1)
            barrier(pool)
            experts("pool", pool, st, 1, out)
            barrier(pool)

        @block.tensor
        def _(pe):
            pe.wait_ge(loaded_small, 16 * 12)
            norm_pe(pe, norm_a, BK[2])
            pe.wait_ge(M["act_in"], 2)
            pe.matmul(BK[3][:, 0:256], CST[:, C_UP:C_UP + P], PA, start=True, stop=True)
            pe.matmul(BK[3][:, 256:512], CST[:, C_ONE:C_ONE + P], PA, start=True, stop=True).then_inc(M["cum"], 1)
            barrier(pe)

            def xbc(n):
                need(pe, M["taken"], 3 * n)
                for m in range(MC):
                    for k in range(KD):
                        w, x = slice(DI + m * P, DI + (m + 1) * P), slice(k * P, (k + 1) * P)
                        i = split_matmul(pe, BK[m // 2][:, (m % 2) * 256:(m % 2) * 256 + 256], WINHI[:, k, w],
                                         WINLO[:, k, w], XHI[:, ds(2 * n, 2), x], XLO[:, ds(2 * n, 2), x],
                                         k == 0, k == KD - 1)
                    if m % 2:
                        i.then_inc(M["xbc"], 1)

            def z(c, b):
                q = 2 * c + b
                pe.wait_ge(M["xts"], c + 1)
                need(pe, M["zs"], q)
                for k in range(KD):
                    i = split_matmul(pe, BK[7][:, :], XTSHI[:, k, b, :], XTSLO[:, k, b, :], WINHI[:, k, 0:DI],
                                     WINLO[:, k, 0:DI], k == 0, k == KD - 1)
                i.then_inc(M["z"], 1)

            def x_back(c, b):
                pe.wait_ge(M["xc"], c + 1)
                if b == 0:
                    need(pe, M["yt"], 2 * c)
                    need(pe, M["po_out"], 2 * c)
                else:
                    pe.wait_ge(M["xs"], 2 * c + 1)
                for m in range(4):
                    pe.transpose(BK[5][:, m * P:(m + 1) * P], XC[:, m, b, :], ident)
                i = pe.transpose(BK[6][:, 0:P], XC[:, 4, b, :], ident)
                if b:
                    i = pe.matmul(BK[6][:, P:2 * P], XC[:, 4, b, :], XC[:, 5, b, :], start=True, stop=True)
                i.then_inc(M["xtr"], 1)

            def bc(c):
                pe.matmul(BK[1][:, 0:P], XC[:, 4, 0, :], XC[:, 5, 0, :], start=True, stop=True).then_inc(M["bc"], 1)

            def decay(c, b):
                q = 2 * c + b
                pe.wait_ge(M["a_now"], c + 1)
                need(pe, M["decay"], q)
                for g in range(2):
                    pe.matmul(BK[3 + g][:, :].rearrange("p (h i) -> p h i", h=4), identb,
                              maskb.unsqueeze(1).broadcast_to([P, 4, P]), start=True, stop=False)
                    for h in range(4):
                        i = pe.matmul(BK[3 + g][:, h * P:(h + 1) * P], ANOW[:, b, 4 * g + h:4 * g + h + 1].broadcast_to([P, P]),
                                      CST[:, C_UP:C_UP + P], start=False, stop=h == 3)
                i.then_inc(M["rg"], 1)

            def from_state(c, b):
                q = 2 * c + b
                need(pe, M["st_read"], q - 1)
                need(pe, M["y2_read"], q)
                pe.matmul(BK[0][:, :], XC[:, 5, b, :], SST[:, b], start=True, stop=True).then_inc(M["y2"], 1)

            def increment(c, b):
                q = 2 * c + b
                need(pe, M["st_read"], q)
                pe.wait_ge(M["xdec"], q + 1)
                pe.matmul(BK[2][:, :], BT[:, b], XDEC[:, b], start=True, stop=True).then_inc(M["st"], 1)

            def within(c, b):
                q = 2 * c + b
                need(pe, M["y1_read"], q)
                pe.wait_ge(M["masked"], q + 1)
                pe.wait_ge(M["xdt"], q + 1)
                for h in range(H):
                    i = pe.matmul(BK[1][:, h * HD:(h + 1) * HD], LM[:, b, h, :], XDT[:, b, h * HD:(h + 1) * HD],
                                  start=True, stop=True)
                i.then_inc(M["y1"], 1)

            def y_back(c, b):
                q = 2 * c + b
                if b == 0:
                    pe.wait_ge(M["xs"], 2 * c + 2)
                else:
                    pe.wait_ge(M["yt"], 2 * c + 1)
                pe.wait_ge(M["y"], q + 1)
                for k in range(4):
                    i = pe.transpose(BK[5][:, k * P:(k + 1) * P], Y[:, b, k * P:(k + 1) * P], ident)
                i.then_inc(M["ytr"], 1)

            def mix_out(c, b):
                q = 2 * c + b
                pe.wait_ge(M["yt"], q + 1)
                need(pe, M["po_out"], q)
                for k in range(4):
                    x = slice(k * P, (k + 1) * P)
                    i = split_matmul(pe, BK[6][:, 256:512], YTHI[:, b, x], YTLO[:, b, x], WOUTHI[:, k, :],
                                     WOUTLO[:, k, :], k == 0, k == 3)
                i.then_inc(M["po"], 1)

            def mixer(c, n):
                if n is not None:
                    xbc(n)
                if c is not None:
                    if not (isinstance(c, int) and c == 0):
                        mix_out(c - 1, 1)
                    decay(c, 1)
                    z(c, 0)
                    x_back(c, 0)
                    if n is not None:
                        pe.wait_ge(M["taken"], 3 * n + 3)
                    bc(c)
                    from_state(c, 0)
                    x_back(c, 1)
                    increment(c, 0)
                    within(c, 0)
                    z(c, 1)
                    from_state(c, 1)
                    increment(c, 1)
                    within(c, 1)
                    y_back(c, 0)
                if n is not None:
                    decay(n, 0)
                if c is not None:
                    mix_out(c, 0)
                    y_back(c, 1)
            mixer(None, 0)
            mixer(0, 1)
            with pe.Fori(1, NC - 1) as c:
                mixer(c, c + 1)
            mixer(NC - 1, None)
            mix_out(NC - 1, 1)
            barrier(pe)
            norm_pe(pe, norm_f[0], BK[2])
            route_pe(pe, 0)
            barrier(pe)
            pe.wait_ge(loaded_w1, 16 * E)
            pe.wait_ge(loaded_b, 32)
            st = Steps(pe, pe_step)
            experts("pe", pe, st, 0, acc_dram)
            barrier(pe)

            def heads(c):
                pe.wait_ge(A["xh"], 2 * c + 2)
                need(pe, A["xt"], c)
                need(pe, A["ot"], 4 * c - 6)
                for b in range(2):
                    for k in range(KD):
                        i = pe.transpose(BK[0][:, (2 * b + k) * P:(2 * b + k + 1) * P], XH[:, b, k * P:(k + 1) * P], ident)
                i.then_inc(A["tr"], 1)

            def project(c, par, h, parts):
                s = 2 * c + h
                pe.wait_ge(A["split"], c + 1)
                for bank, lhs, w, done, free, n in ((1, 0, 0, "q0", "prod", 2 * s), (2, 1, 0, "q1", "prod", 2 * s),
                                                    (3, 2, 1, "kd", "kds", s), (4, 2, 2, "vd", "vds", s),
                                                    (5, 1, 2, "v1", "v1s", s))[parts]:
                    if isinstance(c, int) and c == 0:
                        pe.wait_ge(A["w_lo"], w + 1)
                    need(pe, A[free], n)
                    for k in range(KD):
                        x = slice((lhs * KD + k) * P, (lhs * KD + k + 1) * P)
                        n0 = w * 2048 + k * AI + h * HF
                        i = split_matmul(pe, BK[bank][:, :], XTH[:, par, x], XTL[:, par, x],
                                         WHI[:, n0:n0 + HF], WLO[:, n0:n0 + HF], k == 0, k == KD - 1)
                    i.then_inc(A[done], 1)

            def transposed(c, h):
                s = 2 * c + h
                for b in range(2):
                    need(pe, A["ot"], 2 * s + b - 1)
                    if b == 1:
                        pe.wait_ge(A["xt"], c + 2 + h if not isinstance(c, int) else min(c + 2 + h, NC))
                    pe.wait_ge(A[f"out{b}"], s + 1)
                    for k in range(4):
                        i = pe.transpose(BK[7 - 7 * b][:, k * P:(k + 1) * P], OA[:, b, k * P:(k + 1) * P], ident)
                    i.then_inc(A["otr"], 1)

            def att_out(c, h):
                s = 2 * c + h
                if h == 0:
                    need(pe, A["x3"], 2 * c)
                    pe.matmul(BK[6][:, :], identb, maskb[:, P - 1:P].broadcast_to([P, 2 * D]), start=True, stop=False)
                if isinstance(c, int) and c == 0:
                    pe.wait_ge(A["w_lo"], 4)
                for b in range(2):
                    pe.wait_ge(A["ot"], 2 * s + b + 1)
                    for k in range(4):
                        x = slice(k * P, (k + 1) * P)
                        n0 = 3 * 2048 + (4 * h + k) * D
                        i = split_matmul(pe, BK[6][:, b * D:(b + 1) * D], OTH[:, b, x], OTL[:, b, x],
                                         WHI[:, n0:n0 + D], WLO[:, n0:n0 + D], False, h == 1 and b == 1 and k == 3)
                    i.then_inc(A["po"], 1)

            def att(c, par, first=False, last=False):
                project(c, par, 0, slice(0, 3))
                if not first:
                    att_out(c - 1, 0)
                project(c, par, 0, slice(3, 4))
                if not last:
                    heads(c + 1)
                project(c, par, 0, slice(4, 5))
                if not first:
                    transposed(c - 1, 1)
                project(c, par, 1, slice(0, 3))
                if not first:
                    att_out(c - 1, 1)
                project(c, par, 1, slice(3, 5))
                transposed(c, 0)
            heads(0)
            att(0, 0, first=True)
            att(1, 1)
            with pe.Fori(1, NC // 2 - 1) as i:
                att(2 * i, 0)
                att(2 * i + 1, 1)
            att(NC - 2, 0)
            att(NC - 1, 1, last=True)
            att_out(NC - 1, 0)
            transposed(NC - 1, 1)
            att_out(NC - 1, 1)
            barrier(pe)
            norm_pe(pe, norm_f[1], BK[2])
            route_pe(pe, 1)
            barrier(pe)
            pe.wait_ge(loaded_w1, 16 * (E + 1))
            pe.wait_ge(loaded_b, 64)
            experts("pe", pe, st, 1, out)
            barrier(pe)


def constants():
    import numpy as np
    c = np.zeros((P, C_N), np.float32)
    i, j = np.arange(P)[:, None], np.arange(P)[None, :]
    c[:, C_ID:C_ID + P] = i == j
    c[:, C_UP:C_UP + P] = i <= j
    c[:, C_ONE:C_ONE + P] = 1
    c[:, C_US:C_US + P] = i < j
    c[:, C_IOTA:C_IOTA + P] = j
    c[:, C_MASK:C_MASK + P] = np.where(j < i, MASKED, 0)
    c[:, C_IT:C_IT + ST] = np.arange(ST)
    q = np.arange(NQ)[None, :]
    c[:, C_TOK:C_TOK + NQ] = (q % 2) * L + (q // 2) * P + i - NTOK
    c[:, C_K128:C_K128 + NQ] = P * q
    c[:, C_REV:C_REV + E] = E - np.arange(E)
    c[:, C_PAD] = NTOK + np.arange(P)
    return c


def kernel(**inputs):
    import numpy as _np
    import concourse.bacc as _bacc
    from concourse import mybir as _mybir
    from concourse.bass_utils import run_bass_kernel_spmd as _run

    a = {k.split("_", 1)[1]: _np.asarray(v) for k, v in inputs.items()}
    t = _np.ascontiguousarray
    arrays = {
        "u": a["attn_a_u"].reshape(NTOK, D),
        "w_in": t(a["attn_a_W_in"].T),
        "conv_w": a["attn_a_conv_w"], "conv_b": a["attn_a_conv_b"], "dt_bias": a["attn_a_dt_bias"],
        "a_log": a["attn_a_A_log"], "d_skip": a["attn_a_D"], "norm_w": a["attn_a_norm_w"],
        "w_mix_out": t(a["attn_a_W_out"].T),
        "w_qkv": t(a["attn_b_w_qkv"].reshape(AH, 3, AD, D).transpose(1, 3, 0, 2)).reshape(3, D, AI),
        "w_att_out": t(a["attn_b_w_out"].T), "ln_w": a["attn_b_ln_w"], "ln_b": a["attn_b_ln_b"],
        "w_route": t(a["ffn_Wr"].T), "b_route": a["ffn_br"],
        "w1": a["ffn_Wl1"], "b1": a["ffn_bl1"], "w2": a["ffn_Wl2"], "b2": a["ffn_bl2"],
        "bias_n": a["ffn_biases_N"], "consts": constants(),
    }
    nc = _bacc.Bacc("TRN2", target_bir_lowering=False, num_devices=1)
    arrays = {f"in_{k}": t(v) for k, v in arrays.items()}
    args = [nc.dram_tensor(k, v.shape, _mybir.dt.from_np(v.dtype), kind="ExternalInput").ap() for k, v in arrays.items()]
    args.append(nc.dram_tensor("out_0", (NTOK + P, D), _mybir.dt.float32, kind="ExternalOutput").ap())
    hybrid_block(nc, *args)
    r = _run(nc, [arrays], core_ids=[0])
    return r.results[0]["out_0"][:NTOK].reshape(B, L, D)
```
